# Optimizing a Trainium2 kernel written in Bass

```python
import numpy as np
import jax
import jax.numpy as jnp

def _softmax(x, axis=-1):
    return jax.nn.softmax(x, axis=axis)

def _gelu(x):
    return jax.nn.gelu(x, approximate=True)

def _silu(x):
    return jax.nn.silu(x)

def _sigmoid(x):
    return jax.nn.sigmoid(x)

def _layernorm(x, axis=-1, eps=1e-05):
    m = jnp.mean(x, axis=axis, keepdims=True)
    v = jnp.var(x, axis=axis, keepdims=True)
    return (x - m) / jnp.sqrt(v + eps)

def _scatter_add(tgt, idx, src, axis=0):
    return tgt.at[idx].add(src)

def _segment_sum(src, seg, n):
    return jax.ops.segment_sum(src, seg, n)
kernel_name = 'mk_prb_d1_jaxref_r4_d4fc98'

def setup_inputs(seed: int=0):
    np.random.seed(seed)
    _w = jnp.asarray

    def _L0_attn_setup():
        import jax, jax.numpy as jnp
        import numpy as np
        D_MODEL = 256
        D_STATE = 16
        EXPAND = 2
        D_INNER = EXPAND * D_MODEL
        DT_RANK = 64
        D_CONV = 4

        def _silu(v):
            return v * jax.nn.sigmoid(v)
        key = jax.random.key(seed)
        ks = jax.random.split(key, 8)
        s = 0.02
        x = jax.random.normal(ks[0], (2, 512, D_MODEL), dtype=jnp.float32)
        W_in = jax.random.normal(ks[1], (D_MODEL, 2 * D_INNER), dtype=jnp.float32) * s
        W_conv = jax.random.normal(ks[2], (D_CONV, D_INNER), dtype=jnp.float32) * s
        b_conv = jnp.zeros((D_INNER,), dtype=jnp.float32)
        W_xproj = jax.random.normal(ks[3], (D_INNER, DT_RANK + 2 * D_STATE), dtype=jnp.float32) * s
        W_dt = jax.random.normal(ks[4], (DT_RANK, D_INNER), dtype=jnp.float32) * s
        b_dt = jnp.zeros((D_INNER,), dtype=jnp.float32)
        A_log = jnp.broadcast_to(jnp.log(jnp.arange(1, D_STATE + 1, dtype=jnp.float32)), (D_INNER, D_STATE))
        D = jnp.ones((D_INNER,), dtype=jnp.float32)
        W_out = jax.random.normal(ks[5], (D_INNER, D_MODEL), dtype=jnp.float32) * s
        return {'x': x, 'W_in': W_in, 'W_conv': W_conv, 'b_conv': b_conv, 'W_xproj': W_xproj, 'W_dt': W_dt, 'b_dt': b_dt, 'A_log': A_log, 'D': D, 'W_out': W_out}
    _L0_attn_in = _L0_attn_setup()

    def _L0_ffn_setup():
        import jax, jax.numpy as jnp
        import numpy as np
        H = 256
        NH = 16
        HD = H // NH
        HH = HD // 2
        L = H // 4
        I = int(H * 1.0)
        ER = 7
        TOPK = 2
        BASE = 10000.0
        EPS = 1e-05

        def rmsnorm(x, w):
            norm = jnp.sqrt(jnp.mean(x * x, axis=-1, keepdims=True)) + EPS
            return x / norm * w

        def rope_tables(seq_len):
            inv_freq = 1.0 / BASE ** (jnp.arange(0, HH, 2, dtype=jnp.float32) / HH)
            t = jnp.arange(seq_len, dtype=jnp.float32)
            freqs = jnp.einsum('i,j->ij', t, inv_freq)
            emb = jnp.concatenate([freqs, freqs], axis=-1)
            cos = jnp.cos(emb)[None, :, None, :]
            sin = jnp.sin(emb)[None, :, None, :]
            return (cos, sin)

        def rotate_half(x):
            x1, x2 = jnp.split(x, 2, axis=-1)
            return jnp.concatenate([-x2, x1], axis=-1)

        def silu(x):
            return x * jax.nn.sigmoid(x)

        def mla(xn, W_kvd, W_qd, W_ku, W_qu, W_vu, W_ropeq, W_ropek, W_o):
            B, S, _ = xn.shape
            kv_lat = xn @ W_kvd
            q_lat = xn @ W_qd
            k = (kv_lat @ W_ku).reshape(B, S, NH, HH)
            q = (q_lat @ W_qu).reshape(B, S, NH, HH)
            v = (kv_lat @ W_vu).reshape(B, S, NH, HD)
            q_rope = (q_lat @ W_ropeq).reshape(B, S, NH, HH)
            k_rope = (xn @ W_ropek).reshape(B, S, NH, HH)
            cos, sin = rope_tables(S)
            k_rope = k_rope * cos + rotate_half(k_rope) * sin
            q_rope = q_rope * cos + rotate_half(q_rope) * sin
            kk = jnp.concatenate([k, k_rope], axis=-1)
            qq = jnp.concatenate([q, q_rope], axis=-1)
            scale = 1.0 / jnp.sqrt(jnp.float32(HD))
            scores = jnp.einsum('bqhd,bkhd->bhqk', qq, kk) * scale
            causal = jnp.tril(jnp.ones((S, S), dtype=bool))
            scores = jnp.where(causal[None, None], scores, jnp.finfo(scores.dtype).min)
            probs = jax.nn.softmax(scores, axis=-1)
            y = jnp.einsum('bhqk,bkhd->bqhd', probs, v).reshape(B, S, H)
            return y @ W_o

        def moe(xn, Wg_s, Wu_s, Wd_s, Wg_r, Wu_r, Wd_r, W_router, routing_bias):
            B, S, _ = xn.shape
            xt = xn.reshape(B * S, H)
            shared = silu(xt @ Wg_s) * (xt @ Wu_s) @ Wd_s
            logits = xt @ W_router + routing_bias
            probs = jax.nn.sigmoid(logits)
            scores, idx = jax.lax.top_k(probs, TOPK)
            scores = scores / jnp.sum(scores, axis=-1, keepdims=True)
            wts = jnp.sum(jax.nn.one_hot(idx, ER, dtype=xt.dtype) * scores[..., None], axis=1)
            g = jnp.einsum('th,ehi->tei', xt, Wg_r)
            u = jnp.einsum('th,ehi->tei', xt, Wu_r)
            hmid = silu(g) * u
            combined = jnp.einsum('tei,eih,te->th', hmid, Wd_r, wts)
            return (shared + combined).reshape(B, S, H)
        key = jax.random.key(seed)
        ks = jax.random.split(key, 20)
        s = 0.02
        r = lambda k, shp: jax.random.normal(k, shp, dtype=jnp.float32) * s
        return {'x': jax.random.normal(ks[0], (4, 256, H), dtype=jnp.float32), 'w_ln1': jnp.ones((H,), jnp.float32), 'w_ln2': jnp.ones((H,), jnp.float32), 'W_kvd': r(ks[1], (H, L)), 'W_qd': r(ks[2], (H, L)), 'W_ku': r(ks[3], (L, NH * HH)), 'W_qu': r(ks[4], (L, NH * HH)), 'W_vu': r(ks[5], (L, H)), 'W_ropeq': r(ks[6], (L, H // 2)), 'W_ropek': r(ks[7], (H, H // 2)), 'W_o': r(ks[8], (H, H)), 'Wg_s': r(ks[9], (H, I)), 'Wu_s': r(ks[10], (H, I)), 'Wd_s': r(ks[11], (I, H)), 'Wg_r': r(ks[12], (ER, H, I)), 'Wu_r': r(ks[13], (ER, H, I)), 'Wd_r': r(ks[14], (ER, I, H)), 'W_router': r(ks[15], (H, ER)), 'routing_bias': jnp.zeros((ER,), jnp.float32)}
    _L0_ffn_in = _L0_ffn_setup()
    _d = {'L0_attn_x': _L0_attn_in['x'], 'L0_attn_W_in': _L0_attn_in['W_in'], 'L0_attn_W_conv': _L0_attn_in['W_conv'], 'L0_attn_b_conv': _L0_attn_in['b_conv'], 'L0_attn_W_xproj': _L0_attn_in['W_xproj'], 'L0_attn_W_dt': _L0_attn_in['W_dt'], 'L0_attn_b_dt': _L0_attn_in['b_dt'], 'L0_attn_A_log': _L0_attn_in['A_log'], 'L0_attn_D': _L0_attn_in['D'], 'L0_attn_W_out': _L0_attn_in['W_out'], 'L0_ffn_w_ln1': _L0_ffn_in['w_ln1'], 'L0_ffn_w_ln2': _L0_ffn_in['w_ln2'], 'L0_ffn_W_kvd': _L0_ffn_in['W_kvd'], 'L0_ffn_W_qd': _L0_ffn_in['W_qd'], 'L0_ffn_W_ku': _L0_ffn_in['W_ku'], 'L0_ffn_W_qu': _L0_ffn_in['W_qu'], 'L0_ffn_W_vu': _L0_ffn_in['W_vu'], 'L0_ffn_W_ropeq': _L0_ffn_in['W_ropeq'], 'L0_ffn_W_ropek': _L0_ffn_in['W_ropek'], 'L0_ffn_W_o': _L0_ffn_in['W_o'], 'L0_ffn_Wg_s': _L0_ffn_in['Wg_s'], 'L0_ffn_Wu_s': _L0_ffn_in['Wu_s'], 'L0_ffn_Wd_s': _L0_ffn_in['Wd_s'], 'L0_ffn_Wg_r': _L0_ffn_in['Wg_r'], 'L0_ffn_Wu_r': _L0_ffn_in['Wu_r'], 'L0_ffn_Wd_r': _L0_ffn_in['Wd_r'], 'L0_ffn_W_router': _L0_ffn_in['W_router'], 'L0_ffn_routing_bias': _L0_ffn_in['routing_bias']}
    _x0 = _d['L0_attn_x']
    _d['L0_attn_x'] = jax.random.normal(jax.random.fold_in(jax.random.key(seed), 1), (16, 512, 256), dtype=_x0.dtype)
    del _x0
    return _d

def reference(L0_attn_x, L0_attn_W_in, L0_attn_W_conv, L0_attn_b_conv, L0_attn_W_xproj, L0_attn_W_dt, L0_attn_b_dt, L0_attn_A_log, L0_attn_D, L0_attn_W_out, L0_ffn_w_ln1, L0_ffn_w_ln2, L0_ffn_W_kvd, L0_ffn_W_qd, L0_ffn_W_ku, L0_ffn_W_qu, L0_ffn_W_vu, L0_ffn_W_ropeq, L0_ffn_W_ropek, L0_ffn_W_o, L0_ffn_Wg_s, L0_ffn_Wu_s, L0_ffn_Wd_s, L0_ffn_Wg_r, L0_ffn_Wu_r, L0_ffn_Wd_r, L0_ffn_W_router, L0_ffn_routing_bias):

    def _L0_attn_ref(x, W_in, W_conv, b_conv, W_xproj, W_dt, b_dt, A_log, D, W_out):
        import jax, jax.numpy as jnp
        import numpy as np
        D_MODEL = 256
        D_STATE = 16
        EXPAND = 2
        D_INNER = EXPAND * D_MODEL
        DT_RANK = 64
        D_CONV = 4

        def _silu(v):
            return v * jax.nn.sigmoid(v)
        B_, L, _ = x.shape
        xz = x @ W_in
        x_in, z = jnp.split(xz, 2, axis=-1)
        pad = D_CONV - 1
        x_pad = jnp.pad(x_in, ((0, 0), (pad, 0), (0, 0)))
        x_conv = b_conv
        x_conv = sum((x_pad[:, k:k + L, :] * W_conv[k] for k in range(D_CONV))) + b_conv
        x_in = _silu(x_conv)
        dbc = x_in @ W_xproj
        dt = jax.nn.softplus(dbc[..., :DT_RANK] @ W_dt + b_dt)
        Bm = dbc[..., DT_RANK:DT_RANK + D_STATE]
        Cm = dbc[..., DT_RANK + D_STATE:]
        A = -jnp.exp(A_log)

        def step(state, inp):
            x_t, dt_t, B_t, C_t = inp
            dA = jnp.exp(jnp.clip(dt_t[:, :, None] * A[None], -10.0, 10.0))
            dB = dt_t[:, :, None] * B_t[:, None, :]
            state = jnp.clip(state * dA + x_t[:, :, None] * dB, -10.0, 10.0)
            y_t = jnp.einsum('bdn,bn->bd', state, C_t) + D * x_t
            return (state, y_t)
        tm = lambda a: jnp.swapaxes(a, 0, 1)
        state0 = jnp.zeros((B_, D_INNER, D_STATE), dtype=x.dtype)
        _, ys = jax.lax.scan(step, state0, (tm(x_in), tm(dt), tm(Bm), tm(Cm)))
        y = jnp.swapaxes(ys, 0, 1)
        y = y * _silu(z)
        return y @ W_out

    def _L0_ffn_ref(x, w_ln1, w_ln2, W_kvd, W_qd, W_ku, W_qu, W_vu, W_ropeq, W_ropek, W_o, Wg_s, Wu_s, Wd_s, Wg_r, Wu_r, Wd_r, W_router, routing_bias):
        import jax, jax.numpy as jnp
        import numpy as np
        H = 256
        NH = 16
        HD = H // NH
        HH = HD // 2
        L = H // 4
        I = int(H * 1.0)
        ER = 7
        TOPK = 2
        BASE = 10000.0
        EPS = 1e-05

        def rmsnorm(x, w):
            norm = jnp.sqrt(jnp.mean(x * x, axis=-1, keepdims=True)) + EPS
            return x / norm * w

        def rope_tables(seq_len):
            inv_freq = 1.0 / BASE ** (jnp.arange(0, HH, 2, dtype=jnp.float32) / HH)
            t = jnp.arange(seq_len, dtype=jnp.float32)
            freqs = jnp.einsum('i,j->ij', t, inv_freq)
            emb = jnp.concatenate([freqs, freqs], axis=-1)
            cos = jnp.cos(emb)[None, :, None, :]
            sin = jnp.sin(emb)[None, :, None, :]
            return (cos, sin)

        def rotate_half(x):
            x1, x2 = jnp.split(x, 2, axis=-1)
            return jnp.concatenate([-x2, x1], axis=-1)

        def silu(x):
            return x * jax.nn.sigmoid(x)

        def mla(xn, W_kvd, W_qd, W_ku, W_qu, W_vu, W_ropeq, W_ropek, W_o):
            B, S, _ = xn.shape
            kv_lat = xn @ W_kvd
            q_lat = xn @ W_qd
            k = (kv_lat @ W_ku).reshape(B, S, NH, HH)
            q = (q_lat @ W_qu).reshape(B, S, NH, HH)
            v = (kv_lat @ W_vu).reshape(B, S, NH, HD)
            q_rope = (q_lat @ W_ropeq).reshape(B, S, NH, HH)
            k_rope = (xn @ W_ropek).reshape(B, S, NH, HH)
            cos, sin = rope_tables(S)
            k_rope = k_rope * cos + rotate_half(k_rope) * sin
            q_rope = q_rope * cos + rotate_half(q_rope) * sin
            kk = jnp.concatenate([k, k_rope], axis=-1)
            qq = jnp.concatenate([q, q_rope], axis=-1)
            scale = 1.0 / jnp.sqrt(jnp.float32(HD))
            scores = jnp.einsum('bqhd,bkhd->bhqk', qq, kk) * scale
            causal = jnp.tril(jnp.ones((S, S), dtype=bool))
            scores = jnp.where(causal[None, None], scores, jnp.finfo(scores.dtype).min)
            probs = jax.nn.softmax(scores, axis=-1)
            y = jnp.einsum('bhqk,bkhd->bqhd', probs, v).reshape(B, S, H)
            return y @ W_o

        def moe(xn, Wg_s, Wu_s, Wd_s, Wg_r, Wu_r, Wd_r, W_router, routing_bias):
            B, S, _ = xn.shape
            xt = xn.reshape(B * S, H)
            shared = silu(xt @ Wg_s) * (xt @ Wu_s) @ Wd_s
            logits = xt @ W_router + routing_bias
            probs = jax.nn.sigmoid(logits)
            scores, idx = jax.lax.top_k(probs, TOPK)
            scores = scores / jnp.sum(scores, axis=-1, keepdims=True)
            wts = jnp.sum(jax.nn.one_hot(idx, ER, dtype=xt.dtype) * scores[..., None], axis=1)
            g = jnp.einsum('th,ehi->tei', xt, Wg_r)
            u = jnp.einsum('th,ehi->tei', xt, Wu_r)
            hmid = silu(g) * u
            combined = jnp.einsum('tei,eih,te->th', hmid, Wd_r, wts)
            return (shared + combined).reshape(B, S, H)
        x = x + mla(rmsnorm(x, w_ln1), W_kvd, W_qd, W_ku, W_qu, W_vu, W_ropeq, W_ropek, W_o)
        x = x + moe(rmsnorm(x, w_ln2), Wg_s, Wu_s, Wd_s, Wg_r, Wu_r, Wd_r, W_router, routing_bias)
        return x
    x = L0_attn_x
    xn = _layernorm(x, axis=-1)
    x = x + _L0_attn_ref(xn, L0_attn_W_in, L0_attn_W_conv, L0_attn_b_conv, L0_attn_W_xproj, L0_attn_W_dt, L0_attn_b_dt, L0_attn_A_log, L0_attn_D, L0_attn_W_out) + _L0_ffn_ref(xn, L0_ffn_w_ln1, L0_ffn_w_ln2, L0_ffn_W_kvd, L0_ffn_W_qd, L0_ffn_W_ku, L0_ffn_W_qu, L0_ffn_W_vu, L0_ffn_W_ropeq, L0_ffn_W_ropek, L0_ffn_W_o, L0_ffn_Wg_s, L0_ffn_Wu_s, L0_ffn_Wd_s, L0_ffn_Wg_r, L0_ffn_Wu_r, L0_ffn_Wd_r, L0_ffn_W_router, L0_ffn_routing_bias)
    return x

_drawn_inputs = setup_inputs


def setup_inputs(seed=0):
    import zlib

    import numpy as np

    out = dict(_drawn_inputs(seed))
    spreads = {'L0_attn_b_conv': (0.0, 0.8),
     'L0_attn_b_dt': (0.0, 0.8),
     'L0_attn_D': (1.0, 0.6),
     'L0_ffn_w_ln1': (1.0, 0.6),
     'L0_ffn_w_ln2': (1.0, 0.6),
     'L0_ffn_routing_bias': (0.0, 0.8)}
    factors = {'L0_attn_W_in': 8.0,
     'L0_attn_W_conv': 8.0,
     'L0_attn_W_xproj': 8.0,
     'L0_attn_W_dt': 8.0,
     'L0_attn_A_log': 8.0,
     'L0_attn_W_out': 8.0,
     'L0_ffn_W_kvd': 8.0,
     'L0_ffn_W_qd': 8.0,
     'L0_ffn_W_ku': 8.0,
     'L0_ffn_W_qu': 8.0,
     'L0_ffn_W_vu': 8.0,
     'L0_ffn_W_ropeq': 8.0,
     'L0_ffn_W_ropek': 8.0,
     'L0_ffn_W_o': 8.0,
     'L0_ffn_Wg_s': 6.098,
     'L0_ffn_Wu_s': 6.05,
     'L0_ffn_Wd_s': 6.039,
     'L0_ffn_Wg_r': 8.0,
     'L0_ffn_Wu_r': 8.0,
     'L0_ffn_Wd_r': 8.0,
     'L0_ffn_W_router': 8.0}
    for name, (base, spread) in spreads.items():
        noise = np.random.default_rng([zlib.crc32(name.encode()), seed]).standard_normal(out[name].shape)
        drawn = base * np.exp(spread * noise) if base else spread * noise
        out[name] = jnp.asarray(drawn.astype(out[name].dtype))
    for name, factor in factors.items():
        out[name] = (out[name] * factor).astype(out[name].dtype)
    return out
```

```python
import concourse.bass as bass
from concourse import mybir
from contextlib import ExitStack
import math
import numpy as np

BATCH, SEQ, DM = 16, 512, 256
DI, NST, RANK, TAPS = 512, 16, 64, 4
P = 128


def build_ffn(nc, ctx, x_tm, out_tm, w_ln1, w_ln2, W_kvd, W_qd, W_ka, W_kra, W_krb, W_qa, W_qb, W_vu, W_o,
              Wg, Wu, Wd, W_router, routing_bias, rope_tab):
    f32, bf16 = mybir.dt.float32, mybir.dt.bfloat16
    ALU, ACT, AX = mybir.AluOpType, mybir.ActivationFunctionType, mybir.AxisListType

    NH, HD, LAT = 16, 16, 64
    NX = 8
    ER = NX - 1
    KM = DM // P
    TT = SEQ // P
    PARTS = 3
    K_PART = (0, 0, 1, 0, 2, 1)
    Q_PART = (0, 1, 0, 2, 0, 1)
    KS = HD * len(K_PART)
    MASKED = -1e30
    VA = HD + 1
    HH = NH // 2

    def sb(name, shape, dt=f32):
        return ctx.enter_context(nc.sbuf_tensor(name, shape, dt))

    def pb(name, shape, dt=f32):
        return ctx.enter_context(nc.psum_tensor(name, shape, dt))

    def sem(name):
        return ctx.enter_context(nc.semaphore(name))

    ln1 = sb("f_ln1", [P, KM])
    ln2 = sb("f_ln2", [P, KM])
    w_lat = sb("f_w_lat", [P, KM, 2 * LAT])
    w_ka = sb("f_w_ka", [LAT, 2, P])
    w_kra = sb("f_w_kra", [P, KM, 2, P])
    w_krb = sb("f_w_krb", [P, KM, 2, P])
    w_q = sb("f_w_q", [P, 2, 2, P])
    w_vu = sb("f_w_vu", [LAT, DM])
    w_o = sb("f_w_o", [P, KM, DM])
    wg = sb("f_wg", [P, NX, KM, DM])
    wu = sb("f_wu", [P, NX, KM, DM])
    wd = sb("f_wd", [P, NX, KM, DM])
    w_r = sb("f_w_r", [P, KM, ER])
    b_r = sb("f_b_r", [1, ER])
    rope = sb("f_rope", [P, 4, SEQ])
    ident = sb("f_ident", [P, P])
    identb = sb("f_identb", [P, P], bf16)
    mask_q = sb("f_mask_q", [P, P], bf16)
    mask_k = sb("f_mask_k", [P, P], bf16)
    ones = sb("f_ones", [1, P])
    before = sb("f_before", [P, ER, ER])
    consts = sb("f_consts", [P, 3, TT])

    xm = sb("f_xm", [P, TT, DM])
    st6 = sb("f_st6", [P, TT, 6])
    mv = sb("f_mv", [P, TT, 2])
    sc1 = sb("f_sc1", [P, 8, TT])
    xn = sb("f_xn", [P, TT, DM])
    h1 = sb("f_h1", [P, TT, DM])
    h1T = sb("f_h1T", [P, KM, SEQ])
    lat = sb("f_lat", [P, SEQ])
    kq = sb("f_kq", [P, 4, SEQ])
    parts = sb("f_parts", [P, PARTS, 4, SEQ], bf16)
    kst = sb("f_kst", [KS + PARTS, NH, SEQ], bf16)
    qst = sb("f_qst", [KS + PARTS, NH, SEQ], bf16)
    va = sb("f_va", [P, TT, NH, VA])
    nm = sb("f_nm", [P, TT, NH])
    nm_rest = sb("f_nm_rest", [P, TT, NH])
    nm_part = sb("f_nm_part", [P, TT, PARTS, NH], bf16)
    nmT = sb("f_nmT", [PARTS * NH, SEQ], bf16)
    NPT = 3
    pt = sb("f_pt", [P, NPT, 1280])
    kq_rest = pt[:, :, :].rearrange("p a n -> p (a n)")[:, 0:4 * SEQ].rearrange("p (g n) -> p g n", g=4)
    ra = pt[:, :, :].rearrange("p a n -> p (a n)")[:, 4 * SEQ:5 * SEQ]
    rb = pt[:, :, :].rearrange("p a n -> p (a n)")[:, 5 * SEQ:6 * SEQ]
    rec = sb("f_rec", [P, TT, HH])
    y = h1
    yT = h1T
    x2 = xn
    xs = sb("f_xs", [P, TT, DM])
    h2 = h1
    h2T = sb("f_h2T", [P, KM, SEQ])
    st2 = sb("f_st2", [P, TT, 6])
    mv2 = sb("f_mv2", [P, TT, 2])
    sc2 = sb("f_sc2", [P, 6, TT])
    pe_ = sb("f_pe", [P, TT, ER])
    prob = sb("f_prob", [P, TT, ER])
    cmp1 = sb("f_cmp1", [P, TT, ER, ER])
    cmp2 = sb("f_cmp2", [P, TT, ER, ER])
    rank = sb("f_rank", [P, TT, ER])
    wsel = sb("f_wsel", [P, TT, ER])
    wsum = sb("f_wsum", [P, TT])
    wrec = sb("f_wrec", [P, TT])
    wt = sb("f_wt", [P, TT, NX])
    wtT = sb("f_wtT", [TT * NX, P])
    wbc = sb("f_wbc", [P, ER, SEQ])
    th = sb("f_th", [P, 2, SEQ])
    sg = sb("f_sg", [P, 2, SEQ])
    hm = sb("f_hm", [P, 4, SEQ])
    ot = sb("f_ot", [P, TT, DM])
    parts_dram = nc.dram_tensor("f_parts_dram", [PARTS, 4, 8, HD, SEQ], bf16).ap()
    w_dram = nc.dram_tensor("f_w_dram", [ER, TT, P], f32).ap()

    A = [pb(f"f_A{i}", [P, SEQ]) for i in range(2)]
    O = [pb(f"f_O{i}", [P, 2, HH, VA]) for i in range(2)]
    ACC = [pb(f"f_ACC{i}", [P, 2, DM]) for i in range(2)]
    G = pb("f_G", [P, SEQ])
    U = pb("f_U", [P, SEQ])

    F_T, F_LAT, F_KQ, F_V, F_S1 = 0, 2, 3, 11, 13
    F_NM = F_S1 + 5 * (NH // 2)
    F_S2 = F_NM + 1
    F_YT = F_S2 + 3 * NH
    F_WO, F_HT, F_RT, F_WT = F_YT + 2, F_YT + 4, F_YT + 6, F_YT + 7
    NF = F_WT + 1
    assert NF % 2 == 0

    w_loaded = sem("f_w_loaded")
    moe_w_loaded = sem("f_moe_w_loaded")
    const_ready = sem("f_const_ready")
    a_full = [sem(f"f_a_full{i}") for i in range(2)]
    a_free = [sem(f"f_a_free{i}") for i in range(2)]
    x_loaded = sem("f_x_loaded")
    stat1 = sem("f_stat1")
    stats_done = sem("f_stats_done")
    sc_step = sem("f_sc_step")
    rms_rec = sem("f_rms_rec")
    xn_done = sem("f_xn_done")
    h1_done = sem("f_h1_done")
    kq_ready = sem("f_kq_ready")
    hi_ready = sem("f_hi_ready")
    rest_ready = sem("f_rest_ready")
    mid_ready = sem("f_mid_ready")
    lo_ready = sem("f_lo_ready")
    parts_stored = sem("f_parts_stored")
    stacked = sem("f_stacked")
    nm_step = sem("f_nm_step")
    nm_stacked = sem("f_nm_stacked")
    pv_done = sem("f_pv_done")
    rec_done = sem("f_rec_done")
    y_done = sem("f_y_done")
    xs_ready = sem("f_xs_ready")
    stat2 = sem("f_stat2")
    stats2_done = sem("f_stats2_done")
    sc2_step = sem("f_sc2_step")
    rms2_rec = sem("f_rms2_rec")
    h2_done = sem("f_h2_done")
    rt_step = sem("f_rt_step")
    wt_ready = sem("f_wt_ready")
    w_stored = sem("f_w_stored")
    wbc_loaded = sem("f_wbc_loaded")
    g_full = sem("f_g_full")
    u_full = sem("f_u_full")
    th_ready = sem("f_th_ready")
    sg_ready = sem("f_sg_ready")
    hm_raw = sem("f_hm_raw")
    hm_ready = sem("f_hm_ready")
    down_done = sem("f_down_done")
    ot_done = sem("f_ot_done")
    ot_stored = sem("f_ot_stored")
    taken = sem("f_taken")
    RT = 10

    def filled(k, b):
        return a_full[k % 2], b * (NF // 2) + k // 2 + 1

    def freed(k, b):
        return a_free[k % 2], b * (NF // 2) + k // 2

    def used(k, b):
        return a_free[k % 2], b * (NF // 2) + k // 2 + 1

    NS = 2 * NX
    ATT = {0: ["stats", "T"], 1: ["lat"], 2: ["kq0"], 3: ["kq1", "split"], 4: ["v"],
           6: ["s1_0", "s1_1"], 7: ["s1_2", "s1_3"], 8: ["s1_4", "s1_5"], 9: ["s1_6", "s1_7"], 10: ["nm"],
           11: ["s2_0", "s2_1", "s2_2"], 12: ["s2_3", "s2_4", "s2_5"], 13: ["s2_6", "s2_7", "s2_8"],
           14: ["s2_9", "s2_10", "s2_11"], 15: ["s2_12", "s2_13", "s2_14"]}
    ORDER = []
    for s in range(NS):
        ORDER.append(("gu", s))
        if s >= 1:
            ORDER.append(("down", s - 1))
        ORDER += [("att", a) for a in ATT.get(s, [])]
    ORDER += [("down", NS - 1), ("final", 0), ("att", "s2_15"), ("att", "tail")]

    def run(eng, att, moe):
        def both(b):
            for kind, what in ORDER:
                if kind == "att":
                    att(what, b + 1)
                else:
                    moe(kind, what, b)
        for kind, what in ORDER:
            if kind == "att":
                att(what, 0)
        both(0)
        with eng.Fori(1, BATCH - 1) as b:
            both(b)
        for kind, what in ORDER:
            if kind != "att":
                moe(kind, what, BATCH - 1)

    block = ctx.enter_context(nc.Block())

    @block.sync
    def _(sp):
        kp = "(k p) n -> p k n"
        loads = [
            (w_lat[:, :, 0:LAT], W_kvd.rearrange(kp, p=P)), (w_lat[:, :, LAT:2 * LAT], W_qd.rearrange(kp, p=P)),
            (w_ka[:, :, :], W_ka.rearrange("p (g n) -> p g n", g=2)),
            (w_kra[:, :, :, :], W_kra.rearrange("(k p) (g n) -> p k g n", p=P, g=2)),
            (w_krb[:, :, :, :], W_krb.rearrange("(k p) (g n) -> p k g n", p=P, g=2)),
            (w_q[LAT:P, 0, :, :], W_qa.rearrange("p (g n) -> p g n", g=2)),
            (w_q[LAT:P, 1, :, :], W_qb.rearrange("p (g n) -> p g n", g=2)),
            (w_vu[:, :], W_vu), (w_o[:, :, :], W_o.rearrange(kp, p=P)),
            (w_r[:, :, :], W_router.rearrange(kp, p=P)),
            (b_r[:, :], routing_bias.rearrange("(a n) -> a n", a=1)),
            (rope[:, :, :], rope_tab.rearrange("i p t -> p i t")),
        ]
        for dst, src in loads:
            sp.dma_start(dst, src).then_inc(w_loaded, 16)
        with nc.allow_non_contiguous_dma(reason="per-feature columns, once"):
            sp.dma_start(ln1[:, :], w_ln1.rearrange("(k p) -> p k", p=P)).then_inc(w_loaded, 16)
            sp.dma_start(ln2[:, :], w_ln2.rearrange("(k p) -> p k", p=P)).then_inc(w_loaded, 16)

        rows = x_tm.rearrange("(t b) d -> b t d", b=BATCH)
        rows_out = out_tm.rearrange("(t b) d -> b t d", b=BATCH)

        def at(view, b):
            b = b if isinstance(b, int) else sp.snap(b)
            return view[bass.ds(b, 1), :, :].rearrange("a (j p) d -> p (a j) d", p=P)

        def held(s, v):
            sp.wait_ge(s, v)
            sp.sem_inc(taken)

        def load_x(b):
            src = at(rows, b)
            held(xs_ready, b)
            held(h1_done, b)
            sp.dma_start(xm[:, :, :], src).then_inc(x_loaded, 16)

        def att(what, b):
            if what == "split":
                held(stacked, 16 * 24 * b)
                held(lo_ready, b + 1)
                held(mid_ready, b + 1)
                held(hi_ready, b + 1)
                sp.dma_start(parts_dram.rearrange("c g h d t -> (h d) c g t"), parts[:, :, :, :]).then_inc(parts_stored, 16)
                held(parts_stored, 16 * (b + 1))
                held(pv_done, NH * b)
                for r in range(len(K_PART)):
                    for dst, part, g0 in ((kst, K_PART[r], 0), (qst, Q_PART[r], 2)):
                        for g in range(2):
                            sp.dma_start(dst[r * HD:(r + 1) * HD, g * 8:(g + 1) * 8, :],
                                         parts_dram[part, g0 + g, :, :, :].rearrange("h d t -> d h t")).then_inc(stacked, 16)
            if what == "nm":
                held(*used(F_NM, b))
                for c in range(PARTS):
                    sp.dma_start(qst[KS + c:KS + c + 1, :, :], nmT[c * NH:(c + 1) * NH, :]).then_inc(nm_stacked, 16)
            if what == "tail":
                held(wbc_loaded, 16 * b)
                held(*used(F_WT, b))
                for j in range(TT):
                    sp.dma_start(w_dram[:, j, :], wtT[j * NX:j * NX + ER, :]).then_inc(w_stored, 16)
                held(w_stored, 64 * (b + 1))
                held(hm_ready, 14 * b)
                sp.dma_start(wbc[:, :, :], w_dram.rearrange("e j t -> (e j t)").rearrange("(a n) -> a n", a=1).to_broadcast([P, ER * SEQ]).rearrange("p (e t) -> p e t", e=ER)).then_inc(wbc_loaded, 16)

        def moe(kind, s, b):
            if kind == "final":
                dst = at(rows_out, b)
                held(ot_done, 2 * (b + 1))
                sp.dma_start(dst, ot[:, :, :]).then_inc(ot_stored, 16)

        load_x(0)
        for e in range(NX):
            for dst, src in ((wg, Wg), (wu, Wu), (wd, Wd)):
                sp.dma_start(dst[:, e, :, :], src[e, :, :].rearrange("(k p) n -> p k n", p=P)).then_inc(moe_w_loaded, 16)
        for kind, what in ORDER:
            if kind == "att":
                att(what, 0)

        def both(b):
            load_x(b + 1)
            for kind, what in ORDER:
                if kind == "att":
                    att(what, b + 1)
                else:
                    moe(kind, what, b)
        both(0)
        with sp.Fori(1, BATCH - 1) as b:
            both(b)
        moe("final", 0, BATCH - 1)
        sp.wait_ge(ot_stored, 16 * BATCH)

    W_SMALL = 16 * 14

    @block.gpsimd
    def _(pool):
        def fixed(ins, n=[0]):
            ins.then_inc(const_ready, 1)
            n[0] += 1
            pool.wait_ge(const_ready, n[0])
        fixed(pool.memset(ident[:, :], 0.0))
        fixed(pool.affine_select(out=ident[:, :], in_=ident[:, :], compare_op=ALU.not_equal, fill=1.0,
                                 base=0, pattern=[[-1, P]], channel_multiplier=1))
        fixed(pool.memset(identb[:, :], 0.0))
        fixed(pool.affine_select(out=identb[:, :], in_=identb[:, :], compare_op=ALU.not_equal, fill=1.0,
                                 base=0, pattern=[[-1, P]], channel_multiplier=1))
        fixed(pool.memset(mask_q[:, :], 0.0))
        fixed(pool.affine_select(out=mask_q[:, :], in_=mask_q[:, :], compare_op=ALU.is_ge, fill=MASKED,
                                 base=0, pattern=[[-1, P]], channel_multiplier=1))
        fixed(pool.memset(mask_k[:, :], 0.0))
        fixed(pool.affine_select(out=mask_k[:, :], in_=mask_k[:, :], compare_op=ALU.is_ge, fill=MASKED,
                                 base=0, pattern=[[1, P]], channel_multiplier=-1))
        fixed(pool.memset(before[:, :, :], 0.0))
        fixed(pool.affine_select(out=before[:, :, :], in_=before[:, :, :], compare_op=ALU.is_ge, fill=1.0,
                                 base=0, pattern=[[-1, ER], [1, ER]], channel_multiplier=0))
        fixed(pool.memset(ones[:, :], 1.0))
        fixed(pool.memset(consts[:, 0, :], -0.5))
        fixed(pool.memset(consts[:, 1, :], 0.5))
        fixed(pool.memset(consts[:, 2, :], 1e-5))
        fixed(pool.memset(va[:, :, :, HD:VA], 1.0))
        fixed(pool.memset(kst[KS:KS + PARTS, :, :], 1.0))
        fixed(pool.memset(wt[:, :, :], 0.0))

        def chain(s, K, b, n, ins):
            ins.then_inc(s, 1)
            pool.wait_ge(s, K * b + n)

        def att(what, b):
            if what == "stats":
                pool.wait_ge(stats_done, TT * (b + 1))
                pool.wait_ge(h1_done, b)
                tt = pool.tensor_tensor
                chain(sc_step, 7, b, 1, tt(sc1[:, 0, :], mv[:, :, 1], consts[:, 2, :], ALU.add))
                chain(sc_step, 7, b, 2, tt(sc1[:, 1, :], sc1[:, 0, :], consts[:, 0, :], ALU.pow))
                chain(sc_step, 7, b, 3, tt(sc1[:, 2, :], mv[:, :, 1], sc1[:, 1, :], ALU.mult))
                chain(sc_step, 7, b, 4, tt(sc1[:, 3, :], sc1[:, 2, :], sc1[:, 1, :], ALU.mult))
                chain(sc_step, 7, b, 5, tt(sc1[:, 4, :], sc1[:, 3, :], consts[:, 1, :], ALU.pow))
                chain(sc_step, 7, b, 6, tt(sc1[:, 5, :], sc1[:, 4, :], consts[:, 2, :], ALU.add))
                pool.wait_ge(rms_rec, b + 1)
                tt(sc1[:, 7, :], sc1[:, 1, :], sc1[:, 6, :], ALU.mult).then_inc(sc_step, 1)
            if what == "tail":
                pool.wait_ge(*used(F_WO, b))
                pool.wait_ge(*used(F_WO + 1, b))
                pool.wait_ge(ot_done, 2 * b)
                pool.tensor_tensor(xs[:, :, :], x2[:, :, :], xm[:, :, :], ALU.add).then_inc(xs_ready, 1)
                pool.wait_ge(stats2_done, TT * (b + 1))
                pool.wait_ge(h2_done, b)
                tt = pool.tensor_tensor
                chain(sc2_step, 4, b, 1, tt(sc2[:, 0, :], mv2[:, :, 0], mv2[:, :, 0], ALU.mult))
                chain(sc2_step, 4, b, 2, tt(sc2[:, 1, :], sc2[:, 0, :], mv2[:, :, 1], ALU.add))
                chain(sc2_step, 4, b, 3, tt(sc2[:, 2, :], sc2[:, 1, :], consts[:, 1, :], ALU.pow))
                tt(sc2[:, 3, :], sc2[:, 2, :], consts[:, 2, :], ALU.add).then_inc(sc2_step, 1)

        def moe(kind, s, b):
            if kind == "gu" and s >= 2:
                pool.wait_ge(wbc_loaded, 16 * (b + 1))
                pool.wait_ge(hm_raw, NS * b + s + 1)
                pool.tensor_tensor(hm[:, s % 4, :], hm[:, s % 4, :], wbc[:, s // 2 - 1, :], ALU.mult).then_inc(hm_ready, 1)
        run(nc.gpsimd, att, moe)

    @block.scalar
    def _(act):
        act.wait_ge(w_loaded, W_SMALL)

        def att(what, b):
            def fill(k):
                act.wait_ge(*filled(k, b))
                return A[k % 2]
            if what == "T":
                for k in range(KM):
                    act.activation(h1T[:, k, :], fill(F_T + k)[:, :], ACT.Copy, scale=ln1[:, k:k + 1]).then_inc(a_free[(F_T + k) % 2], 1)
            if what == "lat":
                act.activation(lat[:, :], fill(F_LAT)[:, :], ACT.Copy).then_inc(a_free[F_LAT % 2], 1)
            if what == "split":
                act.wait_ge(kq_ready, 4 * (b + 1))
                act.wait_ge(parts_stored, 16 * b)
                act.activation(parts[:, 0, :, :], kq[:, :, :], ACT.Copy).then_inc(hi_ready, 1)
                act.wait_ge(rest_ready, b + 1)
                act.activation(parts[:, 1, :, :], kq_rest[:, :, :], ACT.Copy).then_inc(mid_ready, 1)
            if what == "v":
                for i in range(2):
                    k = F_V + i
                    act.activation(va[:, 2 * i:2 * i + 2, :, 0:HD],
                                   fill(k)[:, :].rearrange("p (j h d) -> p j h d", j=2, h=NH), ACT.Copy).then_inc(a_free[k % 2], 1)
            if what == "nm":
                act.wait_ge(nm_stacked, 48 * b)
                act.activation(nmT[:, :], fill(F_NM)[0:PARTS * NH, 0:SEQ // 2].bitcast(bf16), ACT.Copy).then_inc(a_free[F_NM % 2], 1)
            if what.startswith("s2_"):
                h = int(what[3:])
                for i, (c0, n) in enumerate(((0, 512), (512, 384), (896, 384))):
                    k = F_S2 + 3 * h + i
                    act.activation(pt[:, h % NPT, c0:c0 + n], fill(k)[:, 0:n], ACT.Exp).then_inc(a_free[k % 2], 1)
            if what == "tail":
                for k in range(KM):
                    act.activation(yT[:, k, :], fill(F_YT + k)[:, :], ACT.Copy).then_inc(a_free[(F_YT + k) % 2], 1)
                for k in range(KM):
                    act.activation(h2T[:, k, :], fill(F_HT + k)[:, :], ACT.Copy, scale=ln2[:, k:k + 1]).then_inc(a_free[(F_HT + k) % 2], 1)
                act.wait_ge(wt_ready, b)
                act.activation(pe_[:, :, :], fill(F_RT)[:, 0:TT * ER].rearrange("p (j e) -> p j e", j=TT), ACT.Exp, scale=-1.0).then_inc(a_free[F_RT % 2], 1)
                act.wait_ge(w_stored, 64 * b)
                act.activation(wtT[:, :], fill(F_WT)[0:TT * NX, 0:P], ACT.Copy).then_inc(a_free[F_WT % 2], 1)

        def moe(kind, s, b):
            if kind == "gu":
                act.wait_ge(g_full, NS * b + s + 1)
                if s >= 2:
                    act.wait_ge(sg_ready, NS * b + s - 1)
                else:
                    act.wait_ge(sg_ready, NS * b)
                act.activation(th[:, s % 2, :], G[:, :], ACT.Tanh, scale=0.5).then_inc(th_ready, 1)
        run(nc.scalar, att, moe)

    @block.vector
    def _(dve):
        dve.wait_ge(w_loaded, W_SMALL)
        dve.wait_ge(const_ready, 17)

        def att(what, b):
            def fill(k):
                dve.wait_ge(*filled(k, b))
                return A[k % 2]
            if what == "stats":
                dve.wait_ge(x_loaded, 16 * (b + 1))
                for j in range(TT):
                    dve.bn_stats(st6[:, j, :], xm[:, j, :]).then_inc(stat1, 1)
                dve.wait_ge(sc_step, 7 * b)
                dve.sem_inc(taken)
                for j in range(TT):
                    dve.wait_ge(stat1, TT * b + j + 1)
                    dve.sem_inc(taken)
                    dve.bn_aggr(mv[:, j, :], st6[:, j, :]).then_inc(stats_done, 1)
                dve.wait_ge(sc_step, 7 * b + 6)
                dve.reciprocal(sc1[:, 6, :], sc1[:, 5, :]).then_inc(rms_rec, 1)
                dve.wait_ge(sc_step, 7 * b + 2)
                for j in range(TT):
                    last = dve.tensor_scalar(xn[:, j, :], xm[:, j, :], mv[:, j, 0:1], sc1[:, 1, j:j + 1], ALU.subtract, ALU.mult)
                last.then_inc(xn_done, 1)
                dve.wait_ge(sc_step, 7 * b + 7)
                for j in range(TT):
                    last = dve.tensor_scalar(h1[:, j, :], xm[:, j, :], mv[:, j, 0:1], sc1[:, 7, j:j + 1], ALU.subtract, ALU.mult)
                last.then_inc(h1_done, 1)
            if what in ("kq0", "kq1"):
                g = int(what[2])
                for i in range(2):
                    n = 2 * g + i
                    k = F_KQ + 4 * g + 2 * i
                    dve.wait_ge(kq_ready, 4 * b + n)
                    dve.tensor_tensor(ra[:, :], fill(k)[:, :], rope[:, 2 * i, :], ALU.mult).then_inc(a_free[k % 2], 1)
                    k += 1
                    dve.tensor_tensor(rb[:, :], fill(k)[:, :], rope[:, 2 * i + 1, :], ALU.mult).then_inc(a_free[k % 2], 1)
                    if n == 0:
                        dve.wait_ge(hi_ready, b)
                        dve.wait_ge(rest_ready, b)
                    dve.wait_ge(*used(k - 1, b))
                    dve.wait_ge(*used(k, b))
                    dve.tensor_tensor(kq[:, 2 * i + g, :], ra[:, :], rb[:, :], ALU.add).then_inc(kq_ready, 1)
            if what == "split":
                dve.wait_ge(hi_ready, b + 1)
                dve.wait_ge(lo_ready, b)
                dve.tensor_tensor(kq_rest[:, :, :], kq[:, :, :], parts[:, 0, :, :], ALU.subtract).then_inc(rest_ready, 1)
                dve.wait_ge(mid_ready, b + 1)
                dve.wait_ge(parts_stored, 16 * b)
                dve.tensor_tensor(parts[:, 2, :, :], kq_rest[:, :, :], parts[:, 1, :, :], ALU.subtract).then_inc(lo_ready, 1)
            if what.startswith("s1_"):
                i = int(what[3:])
                h = 2 * i
                if i == 0:
                    dve.wait_ge(nm_step, 5 * b)
                for d in range(2):
                    k = F_S1 + 5 * i + 2 * d
                    dve.tensor_reduce(nm[:, 3, h + d:h + d + 1], fill(k)[:, :], AX.X, ALU.max, negate=True).then_inc(a_free[k % 2], 1)
                    k += 1
                    dve.tensor_reduce(nm[:, 2, h + d:h + d + 1], fill(k)[:, 0:384], AX.X, ALU.max, negate=True)
                    dve.tensor_reduce(nm[:, 0, h + d:h + d + 1], A[k % 2][:, 384:512], AX.X, ALU.max, negate=True).then_inc(a_free[k % 2], 1)
                k = F_S1 + 5 * i + 4
                dve.tensor_reduce(nm[:, 1, h:h + 2], fill(k)[:, :].rearrange("p (h n) -> p h n", h=2), AX.X, ALU.max, negate=True).then_inc(a_free[k % 2], 1)
            if what == "nm":
                for i in range(2):
                    k = F_NM - 1 - i
                    dve.wait_ge(*used(k, b))
                dve.tensor_copy(nm_part[:, :, 0, :], nm[:, :, :]).then_inc(nm_step, 1)
                dve.wait_ge(nm_step, 5 * b + 1)
                dve.tensor_tensor(nm_rest[:, :, :], nm[:, :, :], nm_part[:, :, 0, :], ALU.subtract).then_inc(nm_step, 1)
                dve.wait_ge(nm_step, 5 * b + 2)
                dve.tensor_copy(nm_part[:, :, 1, :], nm_rest[:, :, :]).then_inc(nm_step, 1)
                dve.wait_ge(nm_step, 5 * b + 3)
                dve.tensor_tensor(nm_rest[:, :, :], nm_rest[:, :, :], nm_part[:, :, 1, :], ALU.subtract).then_inc(nm_step, 1)
                dve.wait_ge(nm_step, 5 * b + 4)
                dve.tensor_copy(nm_part[:, :, 2, :], nm_rest[:, :, :]).then_inc(nm_step, 1)
            if what in ("s2_9", "tail"):
                half = 0 if what == "s2_9" else 1
                dve.wait_ge(pv_done, NH * b + HH * (half + 1))
                dve.wait_ge(y_done, 4 * b + 2 * half)
                for i in range(2):
                    dve.reciprocal(rec[:, 2 * i:2 * i + 2, :], O[i][:, :, :, HD]).then_inc(rec_done, 1)
                for i in range(2):
                    dve.wait_ge(rec_done, 4 * b + 2 * half + i + 1)
                    for q in range(2):
                        j = 2 * i + q
                        last = dve.tensor_tensor(
                            y[:, j, half * P:(half + 1) * P].rearrange("p (h d) -> p h d", d=HD), O[i][:, q, :, 0:HD],
                            rec[:, j, :, None].to_broadcast([P, HH, HD]), ALU.mult)
                    last.then_inc(y_done, 1)
            if what == "tail":
                dve.wait_ge(xs_ready, b)
                dve.wait_ge(h2_done, b)
                for i in range(2):
                    k = F_WO + i
                    dve.tensor_tensor(x2[:, 2 * i:2 * i + 2, :], fill(k)[:, :].rearrange("p (j d) -> p j d", j=2),
                                      xn[:, 2 * i:2 * i + 2, :], ALU.add).then_inc(a_free[k % 2], 1)
                dve.wait_ge(sc2_step, 4 * b)
                for j in range(TT):
                    dve.wait_ge(*used(F_WO + j // 2, b))
                    dve.bn_stats(st2[:, j, :], x2[:, j, :]).then_inc(stat2, 1)
                for j in range(TT):
                    dve.wait_ge(stat2, TT * b + j + 1)
                    dve.sem_inc(taken)
                    dve.bn_aggr(mv2[:, j, :], st2[:, j, :]).then_inc(stats2_done, 1)
                dve.wait_ge(sc2_step, 4 * (b + 1))
                dve.reciprocal(sc2[:, 4, :], sc2[:, 3, :]).then_inc(rms2_rec, 1)
                dve.wait_ge(rms2_rec, b + 1)
                for j in range(TT):
                    last = dve.tensor_scalar(h2[:, j, :], x2[:, j, :], sc2[:, 4, j:j + 1], None, ALU.mult)
                last.then_inc(h2_done, 1)
                steps = [0]

                def step(ins):
                    ins.then_inc(rt_step, 1)
                    steps[0] += 1
                    dve.wait_ge(rt_step, RT * b + steps[0])
                dve.wait_ge(*used(F_RT, b))
                step(dve.tensor_scalar(pe_[:, :, :], pe_[:, :, :], 1.0, None, ALU.add))
                step(dve.reciprocal(prob[:, :, :], pe_[:, :, :]))
                over = prob[:, :, None, :].to_broadcast([P, TT, ER, ER])
                own = prob[:, :, :, None].to_broadcast([P, TT, ER, ER])
                step(dve.tensor_tensor(cmp1[:, :, :, :], over, own, ALU.is_gt))
                step(dve.tensor_tensor(cmp2[:, :, :, :], over, own, ALU.is_equal))
                step(dve.tensor_tensor(cmp2[:, :, :, :], cmp2[:, :, :, :], before[:, None, :, :].to_broadcast([P, TT, ER, ER]), ALU.mult))
                step(dve.tensor_tensor(cmp1[:, :, :, :], cmp1[:, :, :, :], cmp2[:, :, :, :], ALU.add))
                step(dve.tensor_reduce(rank[:, :, :], cmp1[:, :, :, :], AX.X, ALU.add))
                step(dve.scalar_tensor_tensor(wsel[:, :, :], rank[:, :, :], 2.0, prob[:, :, :], ALU.is_lt, ALU.mult))
                step(dve.tensor_reduce(wsum[:, :], wsel[:, :, :], AX.X, ALU.add))
                step(dve.reciprocal(wrec[:, :], wsum[:, :]))
                dve.tensor_tensor(wt[:, :, 0:ER], wsel[:, :, :], wrec[:, :, None].to_broadcast([P, TT, ER]), ALU.mult).then_inc(wt_ready, 1)

        def moe(kind, s, b):
            if kind == "gu":
                dve.wait_ge(th_ready, NS * b + s + 1)
                if s >= 2:
                    dve.wait_ge(hm_raw, NS * b + s - 1)
                dve.scalar_tensor_tensor(sg[:, s % 2, :], th[:, s % 2, :], 1.0, G[:, :], ALU.add, ALU.mult).then_inc(sg_ready, 1)
                dve.wait_ge(sg_ready, NS * b + s + 1)
                dve.wait_ge(u_full, NS * b + s + 1)
                dve.wait_ge(down_done, NS * b + max(s - 3, 0))
                dve.tensor_tensor(hm[:, s % 4, :], sg[:, s % 2, :], U[:, :], ALU.mult).then_inc(hm_raw, 1)
            if kind == "final":
                dve.wait_ge(down_done, NS * (b + 1))
                dve.wait_ge(xs_ready, b + 1)
                dve.wait_ge(ot_stored, 16 * b)
                for i in range(2):
                    dve.scalar_tensor_tensor(ot[:, 2 * i:2 * i + 2, :], ACC[i][:, :, :], 0.5, xs[:, 2 * i:2 * i + 2, :],
                                             ALU.mult, ALU.add).then_inc(ot_done, 1)
        run(nc.vector, att, moe)

    @block.tensor
    def _(pe):
        pe.wait_ge(w_loaded, W_SMALL)
        pe.wait_ge(const_ready, 17)

        def att(what, b):
            def fill(k):
                pe.wait_ge(*freed(k, b))
                return A[k % 2]

            def full(k, ins):
                ins.then_inc(a_full[k % 2], 1)

            def transposed(first, src):
                for k in range(KM):
                    bank = fill(first + k)
                    for j in range(TT):
                        last = pe.transpose(bank[:, j * P:(j + 1) * P], src[:, j, k * P:(k + 1) * P], ident[:, :])
                    full(first + k, last)

            if what == "T":
                pe.wait_ge(h1_done, b + 1)
                transposed(F_T, h1)
            if what == "lat":
                bank = fill(F_LAT)
                pe.wait_ge(*used(F_T, b))
                pe.wait_ge(*used(F_T + 1, b))
                for k in range(KM):
                    last = pe.matmul(bank[:, :], w_lat[:, k, :], h1T[:, k, :], start=(k == 0), stop=(k == KM - 1))
                full(F_LAT, last)
            if what in ("kq0", "kq1"):
                g = int(what[2])
                k0 = F_KQ + 4 * g
                pe.wait_ge(*used(F_LAT, b))
                bank = fill(k0)
                pe.matmul(bank[:, :], w_ka[:, g, :], lat[0:LAT, :], start=True, stop=False)
                for k in range(KM):
                    last = pe.matmul(bank[:, :], w_kra[:, k, g, :], h1T[:, k, :], start=False, stop=(k == KM - 1))
                full(k0, last)
                bank = fill(k0 + 1)
                for k in range(KM):
                    last = pe.matmul(bank[:, :], w_krb[:, k, g, :], h1T[:, k, :], start=(k == 0), stop=(k == KM - 1))
                full(k0 + 1, last)
                for i in range(2):
                    bank = fill(k0 + 2 + i)
                    full(k0 + 2 + i, pe.matmul(bank[:, :], w_q[LAT:P, i, g, :], lat[LAT:P, :], start=True, stop=True))
            if what == "v":
                for i in range(2):
                    bank = fill(F_V + i)
                    for q in range(2):
                        j = 2 * i + q
                        last = pe.matmul(bank[:, q * DM:(q + 1) * DM], lat[0:LAT, j * P:(j + 1) * P], w_vu[:, :], start=True, stop=True)
                    full(F_V + i, last)

            def scores(bank, c0, h, qb):
                n = P * (qb + 1)
                pe.matmul(bank[:, c0:c0 + n], qst[0:KS, h, qb * P:(qb + 1) * P], kst[0:KS, h, 0:n], start=True, stop=False)
                return pe.matmul(bank[:, c0 + qb * P:c0 + n], identb[:, :], mask_q[:, :], start=False, stop=True)

            def scores_t(bank, c0, h, kb):
                n = SEQ - P * kb
                pe.matmul(bank[:, c0:c0 + n], kst[:, h, kb * P:(kb + 1) * P], qst[:, h, kb * P:SEQ], start=True, stop=False)
                return pe.matmul(bank[:, c0:c0 + P], identb[:, :], mask_k[:, :], start=False, stop=True)

            if what.startswith("s1_"):
                i = int(what[3:])
                h = 2 * i
                if i == 0:
                    pe.wait_ge(stacked, 16 * 24 * (b + 1))
                for d in range(2):
                    k = F_S1 + 5 * i + 2 * d
                    full(k, scores(fill(k), 0, h + d, 3))
                    k += 1
                    bank = fill(k)
                    scores(bank, 0, h + d, 2)
                    full(k, scores(bank, 384, h + d, 0))
                k = F_S1 + 5 * i + 4
                bank = fill(k)
                scores(bank, 0, h, 1)
                full(k, scores(bank, 256, h + 1, 1))
            if what == "nm":
                bank = fill(F_NM)
                pe.wait_ge(nm_step, 5 * (b + 1))
                pe.sem_inc(taken)
                for j in range(TT):
                    last = pe.transpose(bank[0:PARTS * NH, j * 64:(j + 1) * 64].bitcast(bf16),
                                        nm_part[:, j, :, :].rearrange("p c h -> p (c h)"), identb[:, :])
                full(F_NM, last)

            def values(h):
                k = F_S2 + 3 * h + 2
                for x in (k, k - 1):
                    pe.wait_ge(*used(x, b))
                if h == 0:
                    pe.wait_ge(y_done, 4 * b)
                if h == HH:
                    pe.wait_ge(y_done, 4 * b + 2)
                at = [0, 512, 896, 1152]
                for qb in range(TT):
                    for kb in range(qb + 1):
                        c = at[kb] + (qb - kb) * P
                        last = pe.matmul(O[qb // 2][:, qb % 2, h % HH, :], pt[:, h % NPT, c:c + P], va[:, kb, h, :],
                                         start=(kb == 0), stop=(kb == qb))
                last.then_inc(pv_done, 1)

            if what.startswith("s2_"):
                h = int(what[3:])
                if h == 0:
                    pe.wait_ge(nm_stacked, 48 * (b + 1))
                    for i in range(2):
                        x = F_V + i
                        pe.wait_ge(*used(x, b))
                k = F_S2 + 3 * h
                full(k, scores_t(fill(k), 0, h, 0))
                full(k + 1, scores_t(fill(k + 1), 0, h, 1))
                bank = fill(k + 2)
                scores_t(bank, 0, h, 2)
                full(k + 2, scores_t(bank, 256, h, 3))
                if h >= 1:
                    values(h - 1)
            if what == "tail":
                values(NH - 1)
                pe.wait_ge(y_done, 4 * (b + 1))
                transposed(F_YT, y)
                for i in range(2):
                    k = F_WO + i
                    bank = fill(k)
                    for x in (F_YT, F_YT + 1):
                        pe.wait_ge(*used(x, b))
                    for q in range(2):
                        j = 2 * i + q
                        for kk in range(KM):
                            last = pe.matmul(bank[:, q * DM:(q + 1) * DM], yT[:, kk, j * P:(j + 1) * P], w_o[:, kk, :],
                                             start=(kk == 0), stop=(kk == KM - 1))
                    full(k, last)
                pe.wait_ge(h2_done, b + 1)
                transposed(F_HT, h2)
                bank = fill(F_RT)
                for x in (F_HT, F_HT + 1):
                    pe.wait_ge(*used(x, b))
                for j in range(TT):
                    cols = bank[:, j * ER:(j + 1) * ER]
                    for k in range(KM):
                        pe.matmul(cols, h2T[:, k, j * P:(j + 1) * P], w_r[:, k, :], start=(k == 0), stop=False)
                    last = pe.matmul(cols, ones[:, :], b_r[:, :], start=False, stop=True)
                full(F_RT, last)
                bank = fill(F_WT)
                pe.wait_ge(wt_ready, b + 1)
                full(F_WT, pe.transpose(bank[0:TT * NX, 0:P], wt[:, :, :].rearrange("p j e -> p (j e)"), ident[:, :]))

        def moe(kind, s, b):
            if kind == "gu" and s == 0:
                pe.wait_ge(moe_w_loaded, 16 * 3 * NX)
            if kind == "gu":
                e, i = s // 2, s % 2
                for w, bank, done, free in ((wg, G, g_full, sg_ready), (wu, U, u_full, hm_raw)):
                    pe.wait_ge(free, NS * b + s)
                    for k in range(KM):
                        last = pe.matmul(bank[:, :], w[:, e, k, i * P:(i + 1) * P], h2T[:, k, :], start=(k == 0), stop=(k == KM - 1))
                    last.then_inc(done, 1)
            if kind == "down":
                e, i = s // 2, s % 2
                if s == 0:
                    pe.wait_ge(ot_done, 2 * b)
                if s < 2:
                    pe.wait_ge(hm_raw, NS * b + s + 1)
                else:
                    pe.wait_ge(hm_ready, 14 * b + s - 1)
                for j in range(TT):
                    last = pe.matmul(ACC[j // 2][:, j % 2, :], hm[:, s % 4, j * P:(j + 1) * P], wd[:, e, i, :],
                                     start=(s == 0 and j % 2 == 0), stop=(s == NS - 1 and j % 2 == 1), skip_group_check=True)
                last.then_inc(down_done, 1)
        run(nc.tensor, att, moe)


def build_mamba(nc, ctx, x_tm, res_tm, out_tm, W_in, W_conv, b_conv, W_xproj, W_dt, b_dt, A_log, D, W_out):
    f32 = mybir.dt.float32
    ALU = mybir.AluOpType
    ACT = mybir.ActivationFunctionType

    CT = 16
    CN = CT * BATCH
    NCH = SEQ // CT
    ST = 8
    SN = ST * BATCH
    NSUB = CT // ST
    NU = 2 * NSUB
    KM = DM // P
    MI = DI // P
    TT = CN // P
    HALO = (TAPS - 1) * BATCH
    UW = 2 * NST * BATCH
    CLIP = 10.0
    DA_MIN = math.exp(-CLIP)

    def sb(name, shape, dt=f32):
        return ctx.enter_context(nc.sbuf_tensor(name, shape, dt))

    def pb(name, shape, dt=f32):
        return ctx.enter_context(nc.psum_tensor(name, shape, dt))

    def sem(name):
        return ctx.enter_context(nc.semaphore(name))

    w_in = sb("m_w_in", [P, KM, 2 * DI])
    w_xp = sb("m_w_xp", [P, MI, RANK + 2 * NST])
    w_dt = sb("m_w_dt", [RANK + 1, DI])
    w_out = sb("m_w_out", [P, MI, DM])
    w_cv = sb("m_w_cv", [P, TAPS, MI])
    b_cv = sb("m_b_cv", [1, DI])
    a_neg = sb("m_a_neg", [P, MI, NST])
    d_col = sb("m_d_col", [P, MI])
    ident = sb("m_ident", [P, P])
    cv_diag = sb("m_cv_diag", [P, TAPS * MI, P])
    d_diag = sb("m_d_diag", [P, MI, P])
    ones = sb("m_ones", [1, CN])
    mhalf = sb("m_mhalf", [P, TT])
    eps = sb("m_eps", [P, TT])

    xm = sb("m_xm", [P, TT, DM])
    st6 = sb("m_st6", [P, TT, 6])
    mv = sb("m_mv", [P, TT, 2])
    veps = sb("m_veps", [P, TT])
    rstd = sb("m_rstd", [P, TT])
    xn = sb("m_xn", [P, TT, DM])
    xnT = sb("m_xnT", [P, KM, CN])
    xpad = sb("m_xpad", [P, MI, HALO + CN])
    th_z = sb("m_th_z", [P, MI, CN])
    th_x = sb("m_th_x", [P, MI, CN])
    dt_in = sb("m_dt_in", [RANK + 1, CN])
    bc_row = sb("m_bc_row", [RANK + 2 * NST, CN])
    sp_e = sb("m_sp_e", [P, MI, CN])
    sp_u = sb("m_sp_u", [P, MI, CN])
    sp_v = sb("m_sp_v", [P, MI, CN])
    sp_r = sb("m_sp_r", [P, MI, CN])
    x2 = sb("m_x2", [P, 2, MI, CN])
    zs = sb("m_zs", [P, 2, MI, CN])
    dtt = sb("m_dt", [P, 2, MI, CN])
    dtx = sb("m_dtx", [P, 2, MI, CN])
    dA = sb("m_dA", [P, 2, 2, NST, SN])
    ub = sb("m_ub", [P, 2, 2, NST, SN])
    Bb = sb("m_Bb", [P, NSUB, NST, SN])
    Cb = sb("m_Cb", [P, NSUB, NST, SN])
    yz = sb("m_yz", [P, MI, CN])
    res = sb("m_res", [P, TT, DM])
    ot = sb("m_ot", [P, TT, DM])
    bc_dram = nc.dram_tensor("m_bc_dram", [NSUB, 2, NST, SN], f32).ap()

    S = [pb(f"m_S{h}", [P, UW]) for h in range(2)]
    PR = pb("m_PR", [P, UW])
    Y = pb("m_Y", [P, 512])
    F = [pb(f"m_F{i}", [P, 2, CN]) for i in range(4)]

    w_loaded = sem("m_w_loaded")
    ident_ready = sem("m_ident_ready")
    setup_done = sem("m_setup_done")
    setup_neg = sem("m_setup_neg")
    sp_taken = sem("m_sp_taken")
    taken = sem("m_taken")
    x_loaded = sem("m_x_loaded")
    stat = sem("m_stat")
    stats_done = sem("m_stats_done")
    veps_done = sem("m_veps_done")
    rstd_done = sem("m_rstd_done")
    xn_done = sem("m_xn_done")
    xT_done = sem("m_xT_done")
    xnT_ready = sem("m_xnT_ready")
    xz_done = sem("m_xz_done")
    xpad_ready = sem("m_xpad_ready")
    halo_done = sem("m_halo_done")
    thz_ready = sem("m_thz_ready")
    zs_ready = sem("m_zs_ready")
    conv_done = sem("m_conv_done")
    thx_ready = sem("m_thx_ready")
    x2_ready = sem("m_x2_ready")
    dbc_done = sem("m_dbc_done")
    dtin_ready = sem("m_dtin_ready")
    bcrow_ready = sem("m_bcrow_ready")
    dtp_done = sem("m_dtp_done")
    sp_abs = sem("m_sp_abs")
    sp_relu = sem("m_sp_relu")
    sp_exp = sem("m_sp_exp")
    sp_one = sem("m_sp_one")
    sp_low = sem("m_sp_low")
    sp_ln = sem("m_sp_ln")
    sp_sub = sem("m_sp_sub")
    dt_ready = sem("m_dt_ready")
    dtx_ready = sem("m_dtx_ready")
    bc_stored = sem("m_bc_stored")
    b_loaded = [sem(f"m_b_loaded{s}") for s in range(NSUB)]
    c_loaded = [sem(f"m_c_loaded{s}") for s in range(NSUB)]
    dA_ready = [sem(f"m_dA_ready{u}") for u in range(NU)]
    u_ready = [sem(f"m_u_ready{u}") for u in range(NU)]
    p_step = sem("m_p_step")
    s_step = sem("m_s_step")
    sc_unit = [sem(f"m_sc_unit{u}") for u in range(NU)]
    nsum_done = [sem(f"m_nsum_done{u}") for u in range(NU)]
    yz_done = sem("m_yz_done")
    outp_done = sem("m_outp_done")
    res_loaded = sem("m_res_loaded")
    ot_done = sem("m_ot_done")
    ot_stored = sem("m_ot_stored")

    def same_half_before(u, c):
        return (u - 2, c + 1) if u >= 2 else (u + 2, c)

    def chunk_order(body, tail):
        def run(eng):
            body(0, 0, True, False)
            with eng.Fori(0, NCH // 2 - 1) as g:
                body(g * 2 + 1, 1, False, False)
                body(g * 2 + 2, 0, False, False)
            body(NCH - 1, 1, False, True)
            tail(NCH - 1, 1)
        return run

    block = ctx.enter_context(nc.Block())

    @block.sync
    def _(sp):
        loads = [
            (w_in[:, :, :], W_in.rearrange("(k p) n -> p k n", p=P)),
            (w_xp[:, :, :], W_xproj.rearrange("(k p) n -> p k n", p=P)),
            (w_dt[0:RANK, :], W_dt),
            (w_dt[RANK:RANK + 1, :], b_dt.rearrange("(a n) -> a n", a=1)),
            (w_out[:, :, :], W_out.rearrange("(k p) n -> p k n", p=P)),
            (a_neg[:, :, :], A_log.rearrange("(m p) n -> p m n", p=P)),
            (b_cv[:, :], b_conv.rearrange("(a n) -> a n", a=1)),
        ]
        for dst, src in loads:
            sp.dma_start(dst, src).then_inc(w_loaded, 16)
        with nc.allow_non_contiguous_dma(reason="per-channel columns, once"):
            for k in range(TAPS):
                sp.dma_start(w_cv[:, k, :], W_conv[k, :].rearrange("(m p) -> p m", p=P)).then_inc(w_loaded, 16)
            sp.dma_start(d_col[:, :], D.rearrange("(m p) -> p m", p=P)).then_inc(w_loaded, 16)

        def held(s, v):
            sp.wait_ge(s, v)
            sp.sem_inc(sp_taken)

        def row_of(c):
            return c * CN if isinstance(c, int) else sp.snap(c * CN)

        def load_x(c):
            rows = row_of(c)
            held(xn_done, TT * c)
            sp.dma_start(xm[:, :, :], x_tm[bass.ds(rows, CN), :].rearrange("(j p) d -> p j d", p=P)).then_inc(x_loaded, 16)

        def spread_bc(c):
            for s in range(NSUB):
                held(b_loaded[s], 16 * c)
                held(c_loaded[s], 16 * c)
            held(bcrow_ready, c + 1)
            for s in range(NSUB):
                for i in range(2):
                    sp.dma_start(bc_dram[s, i, :, :], bc_row[RANK + i * NST:RANK + (i + 1) * NST, s * SN:(s + 1) * SN]).then_inc(bc_stored, 16)
            held(bc_stored, 64 * (c + 1))
            for s in range(NSUB):
                held(u_ready[2 * s + 1], 2 * c)
                sp.dma_start(Bb[:, s, :, :], bc_dram[s:s + 1, 0, :, :].to_broadcast([P, NST, SN])).then_inc(b_loaded[s], 16)
                held(sc_unit[2 * s + 1], c)
                sp.dma_start(Cb[:, s, :, :], bc_dram[s:s + 1, 1, :, :].to_broadcast([P, NST, SN])).then_inc(c_loaded[s], 16)

        def load_res(c):
            rows = row_of(c)
            held(ot_done, c)
            sp.dma_start(res[:, :, :], res_tm[bass.ds(rows, CN), :].rearrange("(j p) d -> p j d", p=P)).then_inc(res_loaded, 16)

        def store(c):
            rows = row_of(c)
            held(ot_done, c + 1)
            sp.dma_start(out_tm[bass.ds(rows, CN), :].rearrange("(j p) d -> p j d", p=P), ot[:, :, :]).then_inc(ot_stored, 16)

        load_x(0)
        spread_bc(0)
        load_x(1)

        def chunk(c, rows_ahead=True):
            store(c - 1)
            load_res(c)
            spread_bc(c + 1)
            if rows_ahead:
                load_x(c + 2)

        load_res(0)
        spread_bc(1)
        load_x(2)
        with sp.Fori(1, NCH - 2) as c:
            chunk(c)
        chunk(NCH - 2, rows_ahead=False)
        store(NCH - 2)
        load_res(NCH - 1)
        store(NCH - 1)
        sp.wait_ge(ot_stored, 16 * NCH)

    @block.gpsimd
    def _(pool):
        pool.memset(ident[:, :], 0.0).then_inc(ident_ready, 1)
        pool.wait_ge(ident_ready, 1)
        pool.affine_select(out=ident[:, :], in_=ident[:, :], compare_op=ALU.not_equal, fill=1.0,
                           base=0, pattern=[[-1, P]], channel_multiplier=1).then_inc(ident_ready, 1)
        pool.wait_ge(ident_ready, 2)
        pool.memset(mhalf[:, :], -0.5).then_inc(ident_ready, 1)
        pool.wait_ge(ident_ready, 3)
        pool.memset(dt_in[RANK:RANK + 1, :], 1.0).then_inc(ident_ready, 1)
        pool.wait_ge(ident_ready, 4)
        pool.memset(ones[:, :], 1.0).then_inc(ident_ready, 1)
        pool.wait_ge(ident_ready, 5)
        pool.memset(xpad[:, :, 0:HALO], 0.0).then_inc(ident_ready, 1)
        pool.wait_ge(ident_ready, 6)
        pool.memset(eps[:, :], 1e-5).then_inc(ident_ready, 1)
        pool.wait_ge(ident_ready, 7)

        def rstd_of(c):
            pool.wait_ge(stats_done, TT * (c + 1))
            pool.tensor_tensor(veps[:, :], mv[:, :, 1], eps[:, :], ALU.add).then_inc(veps_done, 1)
            pool.wait_ge(veps_done, c + 1)
            pool.wait_ge(xn_done, TT * c)
            pool.tensor_tensor(rstd[:, :], veps[:, :], mhalf[:, :], ALU.pow).then_inc(rstd_done, 1)

        def dt_sum(c, par):
            pool.wait_ge(sp_ln, c + 1)
            pool.wait_ge(sp_relu, 2 * (c + 1))
            pool.tensor_tensor(sp_u[:, :, :], sp_u[:, :, :], sp_r[:, :, :], ALU.add).then_inc(sp_sub, 1)
            pool.wait_ge(sp_sub, c + 1)
            pool.wait_ge(sp_low, c + 1)
            if not isinstance(c, int) or c >= 2:
                pool.wait_ge(dtx_ready, c - 1)
                pool.wait_ge(dA_ready[NU - 1], c - 1)
            pool.tensor_tensor(dtt[:, par, :, :], sp_u[:, :, :], sp_v[:, :, :], ALU.subtract).then_inc(dt_ready, 1)

        def inputs_of(c, par, u):
            s, h = u // 2, u % 2
            pool.wait_ge(dtx_ready, c + 1)
            pool.wait_ge(b_loaded[s], 16 * (c + 1))
            pu, pc = same_half_before(u, c)
            for i in range(2):
                m = 2 * h + i
                pool.wait_ge(nsum_done[pu], 2 * (pc - 1) + i + 1 if isinstance(pc, int) and pc >= 1 or not isinstance(pc, int) else 0)
                pool.tensor_tensor(ub[:, h, i, :, :], Bb[:, s, :, :],
                                   dtx[:, par, m, None, s * SN:(s + 1) * SN].to_broadcast([P, NST, SN]),
                                   ALU.mult).then_inc(u_ready[u], 1)

        def front(c, par):
            rstd_of(c)
            dt_sum(c, par)

        front(0, 0)
        inputs_of(0, 0, 0)
        inputs_of(0, 0, 1)

        def body(c, par, first, last):
            if not last:
                rstd_of(c + 1)
            inputs_of(c, par, 2)
            inputs_of(c, par, 3)
            if not last:
                dt_sum(c + 1, 1 - par)
                inputs_of(c + 1, 1 - par, 0)
                inputs_of(c + 1, 1 - par, 1)
        chunk_order(body, lambda c, par: None)(nc.gpsimd)

    @block.scalar
    def _(act):
        act.wait_ge(w_loaded, 16 * 12)
        act.activation(a_neg[:, :, :], a_neg[:, :, :], ACT.Exp).then_inc(setup_neg, 1)

        def evac_T(c):
            act.wait_ge(xT_done, c + 1)
            act.wait_ge(xz_done, 4 * c)
            act.activation(xnT[:, :, :], F[0][:, :, :], ACT.Copy).then_inc(xnT_ready, 1)

        def evac_x(c):
            act.wait_ge(conv_done, 2 * c)
            act.wait_ge(xpad_ready, 2 * c)
            act.wait_ge(ident_ready, 6)
            if not isinstance(c, int) or c > 0:
                act.activation(xpad[:, :, 0:HALO], xpad[:, :, CN:CN + HALO], ACT.Copy).then_inc(halo_done, 1)
                act.wait_ge(halo_done, c)
            for i in range(2):
                act.wait_ge(xz_done, 4 * c + i + 1)
                act.activation(xpad[:, 2 * i:2 * i + 2, HALO:HALO + CN], F[1 + i][:, :, :], ACT.Copy).then_inc(xpad_ready, 1)

        def tanh_z(c):
            for i in range(2):
                act.wait_ge(xz_done, 4 * c + 3 + i)
                act.wait_ge(zs_ready, 2 * c)
                act.activation(th_z[:, 2 * i:2 * i + 2, :], F[(3 + i) % 4][:, :, :], ACT.Tanh, scale=0.5).then_inc(thz_ready, 1)

        def tanh_x(c):
            for i in range(2):
                act.wait_ge(conv_done, 2 * c + i + 1)
                act.wait_ge(x2_ready, 2 * c)
                act.activation(th_x[:, 2 * i:2 * i + 2, :], F[1 + i][:, :, :], ACT.Tanh, scale=0.5).then_inc(thx_ready, 1)

        def evac_dbc(c):
            act.wait_ge(dbc_done, c + 1)
            act.wait_ge(dtp_done, 2 * c)
            act.activation(dt_in[0:RANK, :], F[3][0:RANK, 0, :], ACT.Copy).then_inc(dtin_ready, 1)
            act.wait_ge(bc_stored, 64 * c)
            act.activation(bc_row[RANK:RANK + 2 * NST, :], F[3][RANK:RANK + 2 * NST, 0, :], ACT.Copy).then_inc(bcrow_ready, 1)

        def softplus(c):
            act.wait_ge(dt_ready, c)
            for i in range(2):
                act.wait_ge(dtp_done, 2 * c + i + 1)
                act.activation(sp_e[:, 2 * i:2 * i + 2, :], F[i][:, :, :], ACT.Abs).then_inc(sp_abs, 1)
                act.activation(sp_r[:, 2 * i:2 * i + 2, :], F[i][:, :, :], ACT.Relu).then_inc(sp_relu, 1)
            act.wait_ge(sp_abs, 2 * (c + 1))
            act.activation(sp_e[:, :, :], sp_e[:, :, :], ACT.Exp, scale=-1.0).then_inc(sp_exp, 1)

        def ln(c):
            act.wait_ge(sp_exp, c + 1)
            act.activation(sp_u[:, :, :], sp_e[:, :, :], ACT.Ln, bias=1.0).then_inc(sp_ln, 1)

        def decays(c, par, u):
            s, h = u // 2, u % 2
            act.wait_ge(dt_ready, c + 1)
            pu, pc = same_half_before(u, c)
            if pu < u:
                act.wait_ge(s_step, NU * ST * c + ST * (pu + 1) + 2)
            elif not isinstance(c, int) or c > 0:
                act.wait_ge(s_step, NU * ST * (c - 1) + ST * (pu + 1) + 2)
            for i in range(2):
                m = 2 * h + i
                for n in range(NST):
                    last = act.activation(dA[:, h, i, n, :], dtt[:, par, m, s * SN:(s + 1) * SN], ACT.Exp,
                                          scale=a_neg[:, m, n:n + 1])
            last.then_inc(dA_ready[u], 1)

        act.wait_ge(setup_neg, 2)
        evac_T(0)
        evac_x(0)
        tanh_z(0)
        tanh_x(0)
        evac_dbc(0)
        softplus(0)
        ln(0)
        decays(0, 0, 0)
        decays(0, 0, 1)

        def body(c, par, first, last):
            if not last:
                evac_T(c + 1)
                evac_x(c + 1)
                tanh_z(c + 1)
            decays(c, par, 2)
            if not last:
                tanh_x(c + 1)
                evac_dbc(c + 1)
                softplus(c + 1)
            decays(c, par, 3)
            if not last:
                ln(c + 1)
                decays(c + 1, 1 - par, 0)
                decays(c + 1, 1 - par, 1)
        chunk_order(body, lambda c, par: None)(nc.scalar)

    @block.vector
    def _(dve):
        dve.memset(S[0][:, :], 0.0).then_inc(s_step, 1)
        dve.memset(S[1][:, :], 0.0).then_inc(s_step, 1)
        dve.wait_ge(w_loaded, 16 * 12)
        dve.wait_ge(ident_ready, 6)
        dve.wait_ge(setup_neg, 1)
        dve.tensor_scalar(a_neg[:, :, :], a_neg[:, :, :], -1.0, None, ALU.mult).then_inc(setup_neg, 1)
        dve.tensor_scalar(w_xp[:, :, :], w_xp[:, :, :], 0.5, None, ALU.mult).then_inc(setup_done, 1)
        for k in range(TAPS):
            for m in range(MI):
                dve.tensor_scalar(cv_diag[:, k * MI + m, :], ident[:, :], w_cv[:, k, m:m + 1], None, ALU.mult).then_inc(setup_done, 1)
        for m in range(MI):
            dve.tensor_scalar(d_diag[:, m, :], ident[:, :], d_col[:, m:m + 1], 0.5, ALU.mult, ALU.mult).then_inc(setup_done, 1)

        def stats(c):
            dve.wait_ge(x_loaded, 16 * (c + 1))
            for j in range(TT):
                dve.bn_stats(st6[:, j, :], xm[:, j, :]).then_inc(stat, 1)
            for j in range(TT):
                dve.wait_ge(stat, TT * c + j + 1)
                dve.wait_ge(xn_done, TT * c)
                dve.wait_ge(veps_done, c)
                dve.sem_inc(taken)
                dve.bn_aggr(mv[:, j, :], st6[:, j, :]).then_inc(stats_done, 1)

        def normalise(c):
            dve.wait_ge(rstd_done, c + 1)
            dve.wait_ge(xT_done, c)
            for j in range(TT):
                dve.tensor_scalar(xn[:, j, :], xm[:, j, :], mv[:, j, 0:1], rstd[:, j:j + 1],
                                  ALU.subtract, ALU.mult).then_inc(xn_done, 1)

        def gate_z(c, par):
            if not isinstance(c, int) or c >= 2:
                dve.wait_ge(yz_done, NU * (c - 1))
            for i in range(2):
                dve.wait_ge(thz_ready, 2 * c + i + 1)
                dve.scalar_tensor_tensor(zs[:, par, 2 * i:2 * i + 2, :], th_z[:, 2 * i:2 * i + 2, :], 1.0,
                                         F[(3 + i) % 4][:, :, :], ALU.add, ALU.mult).then_inc(zs_ready, 1)

        def silu_x(c, par):
            if not isinstance(c, int) or c >= 2:
                dve.wait_ge(nsum_done[NU - 1], 2 * (c - 1))
            for i in range(2):
                dve.wait_ge(thx_ready, 2 * c + i + 1)
                dve.scalar_tensor_tensor(x2[:, par, 2 * i:2 * i + 2, :], th_x[:, 2 * i:2 * i + 2, :], 1.0,
                                         F[1 + i][:, :, :], ALU.add, ALU.mult).then_inc(x2_ready, 1)

        def log_rest(c):
            dve.wait_ge(sp_exp, c + 1)
            dve.wait_ge(dt_ready, c)
            dve.tensor_scalar(sp_v[:, :, :], sp_e[:, :, :], 1.0, 1.0, ALU.add, ALU.subtract).then_inc(sp_one, 1)
            dve.wait_ge(sp_one, c + 1)
            dve.tensor_tensor(sp_v[:, :, :], sp_v[:, :, :], sp_e[:, :, :], ALU.subtract).then_inc(sp_low, 1)

        def dt_times_x(c, par):
            dve.wait_ge(dt_ready, c + 1)
            dve.wait_ge(x2_ready, 2 * (c + 1))
            if not isinstance(c, int) or c >= 2:
                dve.wait_ge(u_ready[NU - 1], 2 * (c - 1))
            dve.scalar_tensor_tensor(dtx[:, par, :, :], x2[:, par, :, :], 0.5, dtt[:, par, :, :],
                                     ALU.mult, ALU.mult).then_inc(dtx_ready, 1)

        def scan(c, u, between):
            s, h = u // 2, u % 2
            base = NU * ST * c + ST * u
            dve.wait_ge(dA_ready[u], c + 1)
            dve.wait_ge(u_ready[u], 2 * (c + 1))
            dve.wait_ge(c_loaded[s], 16 * (c + 1))
            banks = (S[h], PR)

            def times_c(t):
                cols = slice(t * BATCH, (t + 1) * BATCH)
                return dve.tensor_tensor(ub[:, h, :, :, cols],
                                         banks[(t + 1) % 2][:, :].rearrange("p (i n b) -> p i n b", i=2, n=NST),
                                         Cb[:, s, None, :, cols].to_broadcast([P, 2, NST, BATCH]), ALU.mult)
            for t in range(ST):
                cols = slice(t * BATCH, (t + 1) * BATCH)
                old = banks[t % 2][:, :].rearrange("p (a b) -> p a b", b=BATCH)
                new = banks[(t + 1) % 2][:, :].rearrange("p (a b) -> p a b", b=BATCH)
                dve.wait_ge(s_step, base + t + 2)
                step = dve.scalar_tensor_tensor(new, dA[:, h, :, :, cols].rearrange("p i n b -> p (i n) b"), DA_MIN,
                                                old, ALU.max, ALU.mult)
                step.then_inc(p_step, 1)
                if t > 0:
                    times_c(t - 1)
                if t in between:
                    between[t]()
                dve.wait_ge(p_step, base + t + 1)
                dve.sem_inc(taken)
                dve._custom_dve(bass.dve_ops.TENSOR_ADD_SAT, out=new, in0=new,
                                in1=ub[:, h, :, :, cols].rearrange("p i n b -> p (i n) b"),
                                s0=CLIP, s1=-CLIP).then_inc(s_step, 1)
            dve.wait_ge(s_step, base + ST + 2)
            times_c(ST - 1).then_inc(sc_unit[u], 1)

        def gate_y(c, par, u):
            s, h = u // 2, u % 2
            dve.wait_ge(nsum_done[u], 2 * (c + 1))
            dve.wait_ge(outp_done, c)
            dve.tensor_tensor(yz[:, 2 * h:2 * h + 2, s * SN:(s + 1) * SN],
                              Y[:, 0:2 * SN].rearrange("p (i q) -> p i q", i=2),
                              zs[:, par, 2 * h:2 * h + 2, s * SN:(s + 1) * SN], ALU.mult).then_inc(yz_done, 1)

        def add_res(c):
            dve.wait_ge(outp_done, c + 1)
            dve.wait_ge(res_loaded, 16 * (c + 1))
            dve.wait_ge(ot_stored, 16 * c)
            dve.scalar_tensor_tensor(ot[:, :, :], Y[:, :].rearrange("p (j d) -> p j d", j=TT), 0.5, res[:, :, :],
                                     ALU.mult, ALU.add).then_inc(ot_done, 1)

        stats(0)
        normalise(0)
        gate_z(0, 0)
        silu_x(0, 0)
        log_rest(0)
        dt_times_x(0, 0)

        def body(c, par, first, last):
            slots = [dict() for _ in range(NU)]
            if not first:
                slots[0][3] = lambda: gate_y(c - 1, 1 - par, NU - 1)
                slots[0][6] = lambda: add_res(c - 1)
            for u in range(1, NU):
                slots[u][4] = lambda u=u: gate_y(c, par, u - 1)
            if not last:
                slots[0][1] = lambda: stats(c + 1)
                slots[0][4] = lambda: normalise(c + 1)
                slots[1][2] = lambda: gate_z(c + 1, 1 - par)
                slots[1][6] = lambda: silu_x(c + 1, 1 - par)
                slots[2][6] = lambda: log_rest(c + 1)
                slots[3][3] = lambda: dt_times_x(c + 1, 1 - par)
            for u in range(NU):
                scan(c, u, slots[u])

        def tail(c, par):
            gate_y(c, par, NU - 1)
            add_res(c)
        chunk_order(body, tail)(nc.vector)

    @block.tensor
    def _(pe):
        pe.wait_ge(w_loaded, 16 * 12)
        pe.wait_ge(setup_done, 1 + TAPS * MI + MI)
        pe.wait_ge(ident_ready, 6)

        def transposes(c):
            pe.wait_ge(xn_done, TT * (c + 1))
            pe.wait_ge(sp_abs, 2 * c)
            pe.wait_ge(sp_relu, 2 * c)
            for k in range(KM):
                for j in range(TT):
                    last = pe.transpose(F[0][:, k, j * P:(j + 1) * P], xn[:, j, k * P:(k + 1) * P], ident[:, :])
            last.then_inc(xT_done, 1)

        def project(c):
            pe.wait_ge(xnT_ready, c + 1)
            for i in range(4):
                if i == 0:
                    pe.wait_ge(sp_abs, 2 * c)
                    pe.wait_ge(sp_relu, 2 * c)
                if i == 1:
                    pe.wait_ge(x2_ready, 2 * c)
                if i == 2:
                    pe.wait_ge(bcrow_ready, c)
                    pe.wait_ge(dtin_ready, c)
                for m in range(2):
                    blk = 2 * i + m
                    for k in range(KM):
                        last = pe.matmul(F[(1 + i) % 4][:, m, :], w_in[:, k, blk * P:(blk + 1) * P], xnT[:, k, :],
                                         start=(k == 0), stop=(k == KM - 1))
                last.then_inc(xz_done, 1)

        def conv(c):
            for i in range(2):
                pe.wait_ge(xpad_ready, 2 * (c + 1))
                for j in range(2):
                    m = 2 * i + j
                    pe.matmul(F[1 + i][:, j, :], b_cv[:, m * P:(m + 1) * P], ones[:, :], start=True, stop=False)
                    for k in range(TAPS):
                        last = pe.matmul(F[1 + i][:, j, :], cv_diag[:, k * MI + m, :],
                                         xpad[:, m, k * BATCH:k * BATCH + CN], start=False, stop=(k == TAPS - 1))
                last.then_inc(conv_done, 1)

        def dbc(c):
            pe.wait_ge(zs_ready, 2 * c + 1)
            for m in range(MI):
                pe.wait_ge(x2_ready, 2 * c + m // 2 + 1)
                last = pe.matmul(F[3][0:RANK + 2 * NST, 0, :], w_xp[:, m, :], x2[:, ipar[0], m, :],
                                 start=(m == 0), stop=(m == MI - 1))
            last.then_inc(dbc_done, 1)

        ipar = [0]

        def dt_proj(c):
            pe.wait_ge(dtin_ready, c + 1)
            pe.wait_ge(zs_ready, 2 * (c + 1))
            for m in range(MI):
                last = pe.matmul(F[m // 2][:, m % 2, :], w_dt[:, m * P:(m + 1) * P], dt_in[:, :], start=True, stop=True)
                if m % 2:
                    last.then_inc(dtp_done, 1)

        def nsum(c, par, u):
            s, h = u // 2, u % 2
            if u > 0:
                pe.wait_ge(yz_done, NU * c + u)
            else:
                pe.wait_ge(ot_done, c)
            pe.wait_ge(sc_unit[u], c + 1)
            for i in range(2):
                m = 2 * h + i
                pe.matmul(Y[:, i * SN:(i + 1) * SN], d_diag[:, m, :], x2[:, par, m, s * SN:(s + 1) * SN], start=True, stop=False)
                for n in range(NST):
                    last = pe.matmul(Y[:, i * SN:(i + 1) * SN], ident[:, :], ub[:, h, i, n, :], start=False, stop=(n == NST - 1))
                last.then_inc(nsum_done[u], 1)

        def project_out(c):
            pe.wait_ge(yz_done, NU * (c + 1))
            for j in range(TT):
                for m in range(MI):
                    last = pe.matmul(Y[:, j * DM:(j + 1) * DM], yz[:, m, j * P:(j + 1) * P], w_out[:, m, :],
                                     start=(m == 0), stop=(m == MI - 1))
            last.then_inc(outp_done, 1)

        transposes(0)
        project(0)
        conv(0)
        dbc(0)
        dt_proj(0)

        def body(c, par, first, last):
            if not first:
                nsum(c - 1, 1 - par, NU - 1)
                project_out(c - 1)
            ipar[0] = 1 - par
            if not last:
                transposes(c + 1)
                project(c + 1)
            nsum(c, par, 0)
            if not last:
                conv(c + 1)
                dbc(c + 1)
            nsum(c, par, 1)
            if not last:
                dt_proj(c + 1)
            nsum(c, par, 2)

        def tail(c, par):
            nsum(c, par, NU - 1)
            project_out(c)
        chunk_order(body, tail)(nc.tensor)


_MAMBA_INS = ['L0_attn_W_in', 'L0_attn_W_conv', 'L0_attn_b_conv', 'L0_attn_W_xproj', 'L0_attn_W_dt', 'L0_attn_b_dt',
        'L0_attn_A_log', 'L0_attn_D', 'L0_attn_W_out']


_FFN_INS = ['w_ln1', 'w_ln2', 'W_kvd', 'W_qd', 'W_ka', 'W_kra', 'W_krb', 'W_qa', 'W_qb', 'W_vu', 'W_o', 'Wg', 'Wu', 'Wd',
        'W_router', 'routing_bias', 'rope_tab']


def rope_tables():
    HH = 8
    inv = (np.float32(1.0) / np.float32(10000.0) ** (np.arange(0, HH, 2, dtype=np.float32) / np.float32(HH))).astype(np.float32)
    f = np.arange(SEQ, dtype=np.float32)[:, None] * inv[None, :]
    f = np.concatenate([f, f], axis=1).astype(np.float32)
    sign = np.where(np.arange(HH) < HH // 2, -1.0, 1.0).astype(np.float32)
    c = np.ones((SEQ, 16), np.float32)
    s = np.zeros((SEQ, 16), np.float32)
    c[:, HH:] = np.cos(f)
    s[:, HH:] = np.sin(f) * sign
    c, s = (np.tile(a.T, (8, 1)) for a in (c, s))
    return np.stack([c, s, c * np.float32(0.25), s * np.float32(0.25)]).astype(np.float32)


def ffn_layouts(inputs):
    g = {k: np.asarray(v) for k, v in inputs.items()}
    a = {n: g['L0_ffn_' + n] for n in ('w_ln1', 'w_ln2', 'W_kvd', 'W_qd', 'W_vu', 'W_o', 'W_router', 'routing_bias')}

    def heads(first, second, swap):
        w = np.zeros(((first if first is not None else second).shape[0], 16, 16), np.float32)
        if first is not None:
            w[:, :, 0:8] = first.reshape(-1, 16, 8)
        if second is not None:
            s = second.reshape(-1, 16, 2, 4)
            w[:, :, 8:16] = (s[:, :, ::-1, :] if swap else s).reshape(-1, 16, 8)
        return w.reshape(-1, 256)
    a['W_ka'] = heads(g['L0_ffn_W_ku'], None, False)
    a['W_kra'] = heads(None, g['L0_ffn_W_ropek'], False)
    a['W_krb'] = heads(None, g['L0_ffn_W_ropek'], True)
    a['W_qa'] = heads(g['L0_ffn_W_qu'], g['L0_ffn_W_ropeq'], False)
    a['W_qb'] = heads(None, g['L0_ffn_W_ropeq'], True)
    for n in ('Wg', 'Wu', 'Wd'):
        a[n] = np.concatenate([g[f'L0_ffn_{n}_s'][None], g[f'L0_ffn_{n}_r']])
    a['rope_tab'] = rope_tables()
    return {n: np.ascontiguousarray(a[n]) for n in _FFN_INS}


def build(nc, t, out):
    part = nc.dram_tensor("x_plus_ffn", (SEQ * BATCH, DM), mybir.dt.float32).ap()
    with ExitStack() as ctx:
        build_ffn(nc, ctx, t["x_tm"], part, *[t[n] for n in _FFN_INS])
    with ExitStack() as ctx:
        build_mamba(nc, ctx, t["x_tm"], part, out, *[t[n] for n in _MAMBA_INS])


def kernel(**inputs):
    import concourse.bacc as _bacc
    from concourse.bass_utils import run_bass_kernel_spmd as _run

    nc = _bacc.Bacc("TRN2", target_bir_lowering=False, num_devices=1)
    arrays = {}
    x = np.asarray(inputs['L0_attn_x'])
    arrays["x_tm"] = np.ascontiguousarray(x.transpose(1, 0, 2)).reshape(SEQ * BATCH, DM)
    for n in _MAMBA_INS:
        arrays[n] = np.ascontiguousarray(np.asarray(inputs[n]))
    arrays.update(ffn_layouts(inputs))
    t = {k: nc.dram_tensor(k, v.shape, mybir.dt.from_np(v.dtype), kind="ExternalInput").ap() for k, v in arrays.items()}
    out = nc.dram_tensor("out_tm", (SEQ * BATCH, DM), mybir.dt.float32, kind="ExternalOutput").ap()
    build(nc, t, out)
    r = _run(nc, [arrays], core_ids=[0])
    got = r.results[0]["out_tm"].reshape(SEQ, BATCH, DM)
    return np.ascontiguousarray(got.transpose(1, 0, 2))
```

```python
import concourse.bass as bass
from concourse import mybir
from contextlib import ExitStack
import math
import numpy as np

BATCH, SEQ, DM = 16, 512, 256
DI, NST, RANK, TAPS = 512, 16, 64, 4
P = 128


def build_ffn(nc, ctx, x_tm, out_tm, w_ln1, w_ln2, W_kvd, W_qd, W_ka, W_kra, W_krb, W_qa, W_qb, W_vu, W_o,
              Wg, Wu, Wd, W_router, routing_bias, rope_tab):
    f32, bf16 = mybir.dt.float32, mybir.dt.bfloat16
    ALU, ACT, AX = mybir.AluOpType, mybir.ActivationFunctionType, mybir.AxisListType

    NH, HD, LAT = 16, 16, 64
    NX = 8
    ER = NX - 1
    KM = DM // P
    TT = SEQ // P
    PARTS = 3
    K_PART = (0, 0, 1, 0, 2, 1)
    Q_PART = (0, 1, 0, 2, 0, 1)
    KS = HD * len(K_PART)
    MASKED = -1e30
    VA = HD + 1
    HH = NH // 2

    def sb(name, shape, dt=f32):
        return ctx.enter_context(nc.sbuf_tensor(name, shape, dt))

    def pb(name, shape, dt=f32):
        return ctx.enter_context(nc.psum_tensor(name, shape, dt))

    def sem(name):
        return ctx.enter_context(nc.semaphore(name))

    ln1 = sb("f_ln1", [P, KM])
    ln2 = sb("f_ln2", [P, KM])
    w_lat = sb("f_w_lat", [P, KM, 2 * LAT])
    w_ka = sb("f_w_ka", [LAT, 2, P])
    w_kra = sb("f_w_kra", [P, KM, 2, P])
    w_krb = sb("f_w_krb", [P, KM, 2, P])
    w_q = sb("f_w_q", [P, 2, 2, P])
    w_vu = sb("f_w_vu", [LAT, DM])
    w_o = sb("f_w_o", [P, KM, DM])
    wg = sb("f_wg", [P, NX, KM, DM])
    wu = sb("f_wu", [P, NX, KM, DM])
    wd = sb("f_wd", [P, NX, KM, DM])
    w_r = sb("f_w_r", [P, KM, ER])
    b_r = sb("f_b_r", [1, ER])
    rope = sb("f_rope", [P, 4, SEQ])
    ident = sb("f_ident", [P, P])
    identb = sb("f_identb", [P, P], bf16)
    mask_q = sb("f_mask_q", [P, P], bf16)
    mask_k = sb("f_mask_k", [P, P], bf16)
    ones = sb("f_ones", [1, P])
    before = sb("f_before", [P, ER, ER])
    consts = sb("f_consts", [P, 3, TT])

    xm = sb("f_xm", [P, TT, DM])
    st6 = sb("f_st6", [P, TT, 6])
    mv = sb("f_mv", [P, TT, 2])
    sc1 = sb("f_sc1", [P, 8, TT])
    xn = sb("f_xn", [P, TT, DM])
    h1 = sb("f_h1", [P, TT, DM])
    h1T = sb("f_h1T", [P, KM, SEQ])
    lat = sb("f_lat", [P, SEQ])
    kq = sb("f_kq", [P, 4, SEQ])
    parts = sb("f_parts", [P, PARTS, 4, SEQ], bf16)
    kst = sb("f_kst", [KS + PARTS, NH, SEQ], bf16)
    qst = sb("f_qst", [KS + PARTS, NH, SEQ], bf16)
    va = sb("f_va", [P, TT, NH, VA])
    nm = sb("f_nm", [P, TT, NH])
    nm_rest = sb("f_nm_rest", [P, TT, NH])
    nm_part = sb("f_nm_part", [P, TT, PARTS, NH], bf16)
    nmT = sb("f_nmT", [PARTS * NH, SEQ], bf16)
    NPT = 3
    pt = sb("f_pt", [P, NPT, 1280])
    kq_rest = pt[:, :, :].rearrange("p a n -> p (a n)")[:, 0:4 * SEQ].rearrange("p (g n) -> p g n", g=4)
    ra = pt[:, :, :].rearrange("p a n -> p (a n)")[:, 4 * SEQ:5 * SEQ]
    rb = pt[:, :, :].rearrange("p a n -> p (a n)")[:, 5 * SEQ:6 * SEQ]
    rec = sb("f_rec", [P, TT, HH])
    y = h1
    yT = h1T
    x2 = xn
    xs_next = sb("f_xs_next", [P, TT, DM])
    xs = sb("f_xs", [P, TT, DM])
    h2 = sb("f_h2", [P, TT, DM])
    h2T = sb("f_h2T", [P, KM, SEQ])
    st2 = sb("f_st2", [P, TT, 6])
    mv2 = sb("f_mv2", [P, TT, 2])
    sc2 = sb("f_sc2", [P, 6, TT])
    pe_ = sb("f_pe", [P, TT, ER])
    prob = sb("f_prob", [P, TT, ER])
    cmp1 = sb("f_cmp1", [P, TT, ER, ER])
    cmp2 = sb("f_cmp2", [P, TT, ER, ER])
    rank = sb("f_rank", [P, TT, ER])
    wsel = sb("f_wsel", [P, TT, ER])
    wsum = sb("f_wsum", [P, TT])
    wrec = sb("f_wrec", [P, TT])
    wt = sb("f_wt", [P, TT, NX])
    wtT = sb("f_wtT", [TT * NX, P])
    wbc = sb("f_wbc", [P, ER, SEQ])
    th = sb("f_th", [P, 2, SEQ])
    sg = sb("f_sg", [P, 2, SEQ])
    NHM = 3
    hm = sb("f_hm", [P, NHM, SEQ])
    parts_dram = nc.dram_tensor("f_parts_dram", [2, 8, HD, PARTS, 2, SEQ], bf16).ap()
    w_dram = nc.dram_tensor("f_w_dram", [ER, TT, P], f32).ap()

    A = [pb(f"f_A{i}", [P, SEQ]) for i in range(2)]
    O = [pb(f"f_O{i}", [P, 2, HH, VA]) for i in range(2)]
    ACC = [pb(f"f_ACC{i}", [P, 2, DM]) for i in range(2)]
    G = pb("f_G", [P, SEQ])
    U = pb("f_U", [P, SEQ])

    F_S1 = 0
    F_NM = F_S1 + 5 * (NH // 2)
    F_S2 = F_NM + 1
    F_YT = F_S2 + 3 * NH
    F_WO, F_T = F_YT + 2, F_YT + 4
    F_LAT, F_KQ, F_V, F_HT = F_T + 2, F_T + 3, F_T + 11, F_T + 13
    F_RT, F_WT = F_HT + 2, F_HT + 3
    NF = F_WT + 1
    N_EARLY = F_HT - F_T
    assert NF % 2 == 0

    def place(k, r):
        if isinstance(r, int) and r < 0:
            return (k - F_T) % 2, (k - F_T) // 2
        if isinstance(r, int) and r == BATCH - 1 and k >= F_HT:
            k -= N_EARLY
        k += N_EARLY
        return k % 2, r * (NF // 2) + k // 2

    w_loaded = sem("f_w_loaded")
    moe_w_loaded = sem("f_moe_w_loaded")
    const_ready = sem("f_const_ready")
    a_full = [sem(f"f_a_full{i}") for i in range(2)]
    a_free = [sem(f"f_a_free{i}") for i in range(2)]
    x_loaded = sem("f_x_loaded")
    stat1 = sem("f_stat1")
    stats_done = sem("f_stats_done")
    sc_step = sem("f_sc_step")
    rms_rec = sem("f_rms_rec")
    xn_done = sem("f_xn_done")
    h1_done = sem("f_h1_done")
    kq_ready = sem("f_kq_ready")
    hi_ready = [sem(f"f_hi_ready{g}") for g in range(2)]
    rest_ready = [sem(f"f_rest_ready{g}") for g in range(2)]
    mid_ready = [sem(f"f_mid_ready{g}") for g in range(2)]
    lo_ready = [sem(f"f_lo_ready{g}") for g in range(2)]
    parts_stored = [sem(f"f_parts_stored{g}") for g in range(2)]
    stacked = [sem(f"f_stacked{g}") for g in range(2)]
    NSTACK = 2 * len(K_PART)
    nm_step = sem("f_nm_step")
    nm_stacked = sem("f_nm_stacked")
    pv_done = sem("f_pv_done")
    rec_done = sem("f_rec_done")
    y_done = sem("f_y_done")
    xs_ready = sem("f_xs_ready")
    stat2 = sem("f_stat2")
    stats2_done = sem("f_stats2_done")
    sc2_step = sem("f_sc2_step")
    rms2_rec = sem("f_rms2_rec")
    h2_done = sem("f_h2_done")
    rt_step = sem("f_rt_step")
    wt_ready = sem("f_wt_ready")
    w_stored = sem("f_w_stored")
    wbc_loaded = sem("f_wbc_loaded")
    g_full = sem("f_g_full")
    u_full = sem("f_u_full")
    th_ready = sem("f_th_ready")
    sg_ready = sem("f_sg_ready")
    hm_raw = sem("f_hm_raw")
    hm_ready = sem("f_hm_ready")
    down_done = sem("f_down_done")
    ot_done = sem("f_ot_done")
    xs_moved = sem("f_xs_moved")
    ot_stored = sem("f_ot_stored")
    taken = sem("f_taken")
    RT = 10

    def filled(k, r):
        i, n = place(k, r)
        return a_full[i], n + 1

    def freed(k, r):
        i, n = place(k, r)
        return a_free[i], n

    def used(k, r):
        i, n = place(k, r)
        return a_free[i], n + 1

    def bank_of(k, r):
        return A[place(k, r)[0]]

    def free_sem(k, r):
        return a_free[place(k, r)[0]]

    NS = 2 * NX
    MOE = []
    for s in range(NS):
        MOE += [("g", s, 0), ("g", s, 1), ("u", s, 0), ("u", s, 1)]
        if s >= 1:
            MOE += [("d", s - 1, 0), ("d", s - 1, 1)]
    MOE += [("ht", 0, 0), ("d", NS - 1, 0), ("d", NS - 1, 1), ("final", 0, 0)]
    BETWEEN = {}

    def put(at, *names):
        BETWEEN.setdefault(at, []).extend(names)
    for i in range(NH // 2):
        for n in range(3):
            put(3 * i + n, ("s1", i, n))
    put(24, ("nm", 0, 0))
    for h in range(NH):
        put(33 + h * 5 // 4, ("s2", h, 0))
    put(53, ("pv", 0, 0))
    put(57, ("yt", 0, 0))
    put(61, ("wo", 0, 0))
    put(64, ("xload", 0, 0), ("stats", 0, 0))
    put(70, ("T", 0, 0))
    put(73, ("lat", 0, 0))
    put(75, ("kq", 0, 0), ("split", 0, 0))
    put(78, ("kq", 1, 0), ("split", 1, 0))
    put(81, ("v", 0, 0))
    EARLY = ("xload", "stats", "T", "lat", "kq", "split", "v")
    ORDER = []
    for i, m in enumerate(MOE):
        ORDER.append(m)
        ORDER += BETWEEN.get(i, [])
    ORDER.append(("route", 0, 0))

    def run(eng, late, early, moe):
        def rnd(r):
            for kind, i, j in ORDER:
                if kind in EARLY:
                    if not (isinstance(r, int) and r >= BATCH - 1):
                        early(kind, i, j, r + 1, r)
                elif kind in ("g", "u", "d", "final"):
                    if not (isinstance(r, int) and r == 0):
                        moe(kind, i, j, r - 1)
                elif not (isinstance(r, int) and r == BATCH):
                    late(kind, i, j, r)
        for kind, i, j in ORDER:
            if kind in EARLY:
                early(kind, i, j, 0, -1)
        rnd(0)
        rnd(1)
        with eng.Fori(2, BATCH - 1) as r:
            rnd(r)
        rnd(BATCH - 1)
        rnd(BATCH)

    block = ctx.enter_context(nc.Block())
    act_loads = []

    @block.sync
    def _(sp):
        kp = "(k p) n -> p k n"
        loads = [
            (w_lat[:, :, 0:LAT], W_kvd.rearrange(kp, p=P)), (w_lat[:, :, LAT:2 * LAT], W_qd.rearrange(kp, p=P)),
            (w_ka[:, :, :], W_ka.rearrange("p (g n) -> p g n", g=2)),
            (w_kra[:, :, :, :], W_kra.rearrange("(k p) (g n) -> p k g n", p=P, g=2)),
            (w_krb[:, :, :, :], W_krb.rearrange("(k p) (g n) -> p k g n", p=P, g=2)),
            (w_q[LAT:P, 0, :, :], W_qa.rearrange("p (g n) -> p g n", g=2)),
            (w_q[LAT:P, 1, :, :], W_qb.rearrange("p (g n) -> p g n", g=2)),
            (w_vu[:, :], W_vu), (w_o[:, :, :], W_o.rearrange(kp, p=P)),
            (w_r[:, :, :], W_router.rearrange(kp, p=P)),
            (b_r[:, :], routing_bias.rearrange("(a n) -> a n", a=1)),
            (rope[:, :, :], rope_tab.rearrange("i p t -> p i t")),
        ]
        for dst, src in loads:
            sp.dma_start(dst, src).then_inc(w_loaded, 16)
        with nc.allow_non_contiguous_dma(reason="per-feature columns, once"):
            sp.dma_start(ln1[:, :], w_ln1.rearrange("(k p) -> p k", p=P)).then_inc(w_loaded, 16)
            sp.dma_start(ln2[:, :], w_ln2.rearrange("(k p) -> p k", p=P)).then_inc(w_loaded, 16)

        rows = x_tm.rearrange("(t b) d -> b t d", b=BATCH)
        rows_out = out_tm.rearrange("(t b) d -> b t d", b=BATCH)

        def at(view, b):
            b = b if isinstance(b, int) else sp.snap(b)
            return view[bass.ds(b, 1), :, :].rearrange("a (j p) d -> p (a j) d", p=P)

        def held(s, v):
            sp.wait_ge(s, v)
            sp.sem_inc(taken)

        def late(kind, i, j, b):
            if kind == "nm":
                held(*used(F_NM, b))
                for c in range(PARTS):
                    sp.dma_start(qst[KS + c:KS + c + 1, :, :], nmT[c * NH:(c + 1) * NH, :]).then_inc(nm_stacked, 16)
            if kind == "route":
                held(wbc_loaded, 16 * b)
                held(*used(F_WT, b))
                for q in range(TT):
                    sp.dma_start(w_dram[:, q, :], wtT[q * NX:q * NX + ER, :]).then_inc(w_stored, 16)
                held(w_stored, 64 * (b + 1))
                held(hm_ready, 14 * b)
                sp.dma_start(wbc[:, :, :], w_dram.rearrange("e j t -> (e j t)").rearrange("(a n) -> a n", a=1)
                             .to_broadcast([P, ER * SEQ]).rearrange("p (e t) -> p e t", e=ER)).then_inc(wbc_loaded, 16)

        def early(kind, i, j, b, r):
            if kind == "xload":
                src = at(rows, b)
                held(xs_ready, b)
                sp.dma_start(xm[:, :, :], src).then_inc(x_loaded, 16)
            if kind == "split":
                g = i
                held(stacked[g], 16 * NSTACK * b)
                held(hi_ready[g], b + 1)
                held(mid_ready[g], b + 1)
                held(lo_ready[g], b + 1)
                sp.dma_start(parts_dram[g, :, :, :, :, :].rearrange("h d c n t -> (h d) c n t"),
                             parts[:, :, 2 * g:2 * g + 2, :]).then_inc(parts_stored[g], 16)
                held(parts_stored[g], 16 * (b + 1))
                held(pv_done, NH * b)
                for q in range(len(K_PART)):
                    for n, (dst, part) in enumerate(((kst, K_PART[q]), (qst, Q_PART[q]))):
                        sp.dma_start(dst[q * HD:(q + 1) * HD, g * 8:(g + 1) * 8, :],
                                     parts_dram[g, :, :, part, n, :].rearrange("h d t -> d h t")).then_inc(stacked[g], 16)

        def moe(kind, i, j, b):
            if kind == "final":
                dst = at(rows_out, b)
                held(ot_done, 2 * (b + 1))
                sp.dma_start(dst, xs[:, :, :]).then_inc(ot_stored, 16)

        for e in range(NX):
            for dst, src in ((wg, Wg), (wu, Wu), (wd, Wd)):
                act_loads.append((dst[:, e, :, :], src[e, :, :].rearrange("(k p) n -> p k n", p=P)))
        run(sp, late, early, moe)
        sp.wait_ge(ot_stored, 16 * BATCH)

    W_SMALL = 16 * 14

    @block.gpsimd
    def _(pool):
        def fixed(ins, n=[0]):
            ins.then_inc(const_ready, 1)
            n[0] += 1
            pool.wait_ge(const_ready, n[0])
        fixed(pool.memset(ident[:, :], 0.0))
        fixed(pool.affine_select(out=ident[:, :], in_=ident[:, :], compare_op=ALU.not_equal, fill=1.0,
                                 base=0, pattern=[[-1, P]], channel_multiplier=1))
        fixed(pool.memset(identb[:, :], 0.0))
        fixed(pool.affine_select(out=identb[:, :], in_=identb[:, :], compare_op=ALU.not_equal, fill=1.0,
                                 base=0, pattern=[[-1, P]], channel_multiplier=1))
        fixed(pool.memset(mask_q[:, :], 0.0))
        fixed(pool.affine_select(out=mask_q[:, :], in_=mask_q[:, :], compare_op=ALU.is_ge, fill=MASKED,
                                 base=0, pattern=[[-1, P]], channel_multiplier=1))
        fixed(pool.memset(mask_k[:, :], 0.0))
        fixed(pool.affine_select(out=mask_k[:, :], in_=mask_k[:, :], compare_op=ALU.is_ge, fill=MASKED,
                                 base=0, pattern=[[1, P]], channel_multiplier=-1))
        fixed(pool.memset(before[:, :, :], 0.0))
        fixed(pool.affine_select(out=before[:, :, :], in_=before[:, :, :], compare_op=ALU.is_ge, fill=1.0,
                                 base=0, pattern=[[-1, ER], [1, ER]], channel_multiplier=0))
        fixed(pool.memset(ones[:, :], 1.0))
        fixed(pool.memset(consts[:, 0, :], -0.5))
        fixed(pool.memset(consts[:, 1, :], 0.5))
        fixed(pool.memset(consts[:, 2, :], 1e-5))
        fixed(pool.memset(va[:, :, :, HD:VA], 1.0))
        fixed(pool.memset(kst[KS:KS + PARTS, :, :], 1.0))
        fixed(pool.memset(wt[:, :, :], 0.0))

        def chain(s, K, b, n, ins):
            ins.then_inc(s, 1)
            pool.wait_ge(s, K * b + n)

        def early(kind, i, j, b, r):
            if kind == "stats":
                pool.wait_ge(stats_done, TT * (b + 1))
                tt = pool.tensor_tensor
                chain(sc_step, 7, b, 1, tt(sc1[:, 0, :], mv[:, :, 1], consts[:, 2, :], ALU.add))
                chain(sc_step, 7, b, 2, tt(sc1[:, 1, :], sc1[:, 0, :], consts[:, 0, :], ALU.pow))
                chain(sc_step, 7, b, 3, tt(sc1[:, 2, :], mv[:, :, 1], sc1[:, 1, :], ALU.mult))
                chain(sc_step, 7, b, 4, tt(sc1[:, 3, :], sc1[:, 2, :], sc1[:, 1, :], ALU.mult))
                chain(sc_step, 7, b, 5, tt(sc1[:, 4, :], sc1[:, 3, :], consts[:, 1, :], ALU.pow))
                chain(sc_step, 7, b, 6, tt(sc1[:, 5, :], sc1[:, 4, :], consts[:, 2, :], ALU.add))
                pool.wait_ge(rms_rec, b + 1)
                tt(sc1[:, 7, :], sc1[:, 1, :], sc1[:, 6, :], ALU.mult).then_inc(sc_step, 1)

        def late(kind, i, j, b):
            if kind == "wo":
                pool.wait_ge(stats2_done, TT * (b + 1))
                tt = pool.tensor_tensor
                chain(sc2_step, 4, b, 1, tt(sc2[:, 0, :], mv2[:, :, 0], mv2[:, :, 0], ALU.mult))
                chain(sc2_step, 4, b, 2, tt(sc2[:, 1, :], sc2[:, 0, :], mv2[:, :, 1], ALU.add))
                chain(sc2_step, 4, b, 3, tt(sc2[:, 2, :], sc2[:, 1, :], consts[:, 1, :], ALU.pow))
                tt(sc2[:, 3, :], sc2[:, 2, :], consts[:, 2, :], ALU.add).then_inc(sc2_step, 1)
                pool.wait_ge(xs_moved, b)
                pool.tensor_tensor(xs_next[:, :, :], x2[:, :, :], xm[:, :, :], ALU.add).then_inc(xs_ready, 1)

        def moe(kind, s, j, b):
            if kind == "u" and j == 1 and s >= 2:
                pool.wait_ge(wbc_loaded, 16 * (b + 1))
                pool.wait_ge(hm_raw, NS * b + s + 1)
                pool.tensor_tensor(hm[:, s % NHM, :], hm[:, s % NHM, :], wbc[:, s // 2 - 1, :], ALU.mult).then_inc(hm_ready, 1)
        run(nc.gpsimd, late, early, moe)

    @block.scalar
    def _(act):
        for dst, src in act_loads:
            act.dma_start(dst, src).then_inc(moe_w_loaded, 16)
        act.wait_ge(w_loaded, W_SMALL)

        def reader(r):
            def read(k, out, cols, func, **kw):
                act.wait_ge(*filled(k, r))
                act.activation(out, cols(bank_of(k, r)), func, **kw).then_inc(free_sem(k, r), 1)
            return read

        def early(kind, i, j, b, r):
            read = reader(r)
            if kind == "T":
                for k in range(KM):
                    read(F_T + k, h1T[:, k, :], lambda bank: bank[:, :], ACT.Copy, scale=ln1[:, k:k + 1])
            if kind == "lat":
                read(F_LAT, lat[:, :], lambda bank: bank[:, :], ACT.Copy)
            if kind == "split":
                g = i
                act.wait_ge(kq_ready, 4 * b + 2 * (g + 1))
                act.wait_ge(parts_stored[g], 16 * b)
                act.activation(parts[:, 0, 2 * g:2 * g + 2, :], kq[:, 2 * g:2 * g + 2, :], ACT.Copy).then_inc(hi_ready[g], 1)
                act.wait_ge(rest_ready[g], b + 1)
                act.activation(parts[:, 1, 2 * g:2 * g + 2, :], kq_rest[:, 2 * g:2 * g + 2, :], ACT.Copy).then_inc(mid_ready[g], 1)
            if kind == "v":
                for n in range(2):
                    read(F_V + n, va[:, 2 * n:2 * n + 2, :, 0:HD],
                         lambda bank: bank[:, :].rearrange("p (j h d) -> p j h d", j=2, h=NH), ACT.Copy)

        def late(kind, i, j, b):
            read = reader(b)
            if kind == "nm":
                act.wait_ge(nm_stacked, 48 * b)
                read(F_NM, nmT[:, :], lambda bank: bank[0:PARTS * NH, 0:SEQ // 2].bitcast(bf16), ACT.Copy)
            if kind == "s2":
                h = i
                for n, (c0, w) in enumerate(((0, 512), (512, 384), (896, 384))):
                    read(F_S2 + 3 * h + n, pt[:, h % NPT, c0:c0 + w], lambda bank: bank[:, 0:w], ACT.Exp)
            if kind == "yt":
                for k in range(KM):
                    read(F_YT + k, yT[:, k, :], lambda bank: bank[:, :], ACT.Copy)
            if kind == "ht":
                for k in range(KM):
                    read(F_HT + k, h2T[:, k, :], lambda bank: bank[:, :], ACT.Copy, scale=ln2[:, k:k + 1])
            if kind == "route":
                act.wait_ge(xs_ready, b + 1)
                act.wait_ge(ot_stored, 16 * b)
                act.activation(xs[:, :, :], xs_next[:, :, :], ACT.Copy).then_inc(xs_moved, 1)
                read(F_RT, pe_[:, :, :], lambda bank: bank[:, 0:TT * ER].rearrange("p (j e) -> p j e", j=TT), ACT.Exp, scale=-1.0)
                act.wait_ge(w_stored, 64 * b)
                read(F_WT, wtT[:, :], lambda bank: bank[0:TT * NX, 0:P], ACT.Copy)

        def moe(kind, s, j, b):
            if kind == "g" and j == 1:
                act.wait_ge(g_full, NS * b + s + 1)
                act.wait_ge(sg_ready, NS * b + max(s - 1, 0))
                act.activation(th[:, s % 2, :], G[:, :], ACT.Tanh, scale=0.5).then_inc(th_ready, 1)
        run(nc.scalar, late, early, moe)

    @block.vector
    def _(dve):
        dve.wait_ge(w_loaded, W_SMALL)
        dve.wait_ge(const_ready, 17)

        def full(k, r):
            dve.wait_ge(*filled(k, r))
            return bank_of(k, r)

        def early(kind, i, j, b, r):
            if kind == "stats":
                dve.wait_ge(x_loaded, 16 * (b + 1))
                for j in range(TT):
                    dve.bn_stats(st6[:, j, :], xm[:, j, :]).then_inc(stat1, 1)
                dve.wait_ge(sc_step, 7 * b)
                dve.sem_inc(taken)
                for j in range(TT):
                    dve.wait_ge(stat1, TT * b + j + 1)
                    dve.sem_inc(taken)
                    dve.bn_aggr(mv[:, j, :], st6[:, j, :]).then_inc(stats_done, 1)
                dve.wait_ge(sc_step, 7 * b + 6)
                dve.reciprocal(sc1[:, 6, :], sc1[:, 5, :]).then_inc(rms_rec, 1)
                dve.wait_ge(sc_step, 7 * b + 2)
                for j in range(TT):
                    last = dve.tensor_scalar(xn[:, j, :], xm[:, j, :], mv[:, j, 0:1], sc1[:, 1, j:j + 1], ALU.subtract, ALU.mult)
                last.then_inc(xn_done, 1)
                dve.wait_ge(sc_step, 7 * b + 7)
                for j in range(TT):
                    last = dve.tensor_scalar(h1[:, j, :], xm[:, j, :], mv[:, j, 0:1], sc1[:, 7, j:j + 1], ALU.subtract, ALU.mult)
                last.then_inc(h1_done, 1)
            if kind == "kq":
                g = i
                for n in range(2):
                    k = F_KQ + 4 * g + 2 * n
                    dve.wait_ge(kq_ready, 4 * b + 2 * g + n)
                    dve.tensor_tensor(ra, full(k, r)[:, :], rope[:, 2 * n, :], ALU.mult).then_inc(free_sem(k, r), 1)
                    dve.tensor_tensor(rb, full(k + 1, r)[:, :], rope[:, 2 * n + 1, :], ALU.mult).then_inc(free_sem(k + 1, r), 1)
                    if n == 0:
                        dve.wait_ge(hi_ready[g], b)
                        dve.wait_ge(rest_ready[g], b)
                    dve.wait_ge(*used(k, r))
                    dve.wait_ge(*used(k + 1, r))
                    dve.tensor_tensor(kq[:, 2 * g + n, :], ra, rb, ALU.add).then_inc(kq_ready, 1)
            if kind == "split":
                g = i
                pair = slice(2 * g, 2 * g + 2)
                dve.wait_ge(hi_ready[g], b + 1)
                dve.tensor_tensor(kq_rest[:, pair, :], kq[:, pair, :], parts[:, 0, pair, :], ALU.subtract).then_inc(rest_ready[g], 1)
                dve.wait_ge(mid_ready[g], b + 1)
                dve.wait_ge(parts_stored[g], 16 * b)
                dve.tensor_tensor(parts[:, 2, pair, :], kq_rest[:, pair, :], parts[:, 1, pair, :], ALU.subtract).then_inc(lo_ready[g], 1)

        def norm_y(half, b):
            dve.wait_ge(pv_done, NH * b + HH * (half + 1))
            dve.wait_ge(y_done, 4 * b + 2 * half)
            for n in range(2):
                dve.reciprocal(rec[:, 2 * n:2 * n + 2, :], O[n][:, :, :, HD]).then_inc(rec_done, 1)
            for n in range(2):
                dve.wait_ge(rec_done, 4 * b + 2 * half + n + 1)
                for q in range(2):
                    t = 2 * n + q
                    last = dve.tensor_tensor(
                        y[:, t, half * P:(half + 1) * P].rearrange("p (h d) -> p h d", d=HD), O[n][:, q, :, 0:HD],
                        rec[:, t, :, None].to_broadcast([P, HH, HD]), ALU.mult)
                last.then_inc(y_done, 1)

        def late(kind, i, j, b):
            def row_max(k, out, cols, last=True):
                ins = dve.tensor_reduce(out, cols(full(k, b)), AX.X, ALU.max, negate=True)
                if last:
                    ins.then_inc(free_sem(k, b), 1)
            if kind == "s1":
                h = 2 * i
                k = F_S1 + 5 * i + 2 * j
                if i == 0 and j == 0:
                    dve.wait_ge(nm_step, 5 * b)
                if j < 2:
                    row_max(k, nm[:, 3, h + j:h + j + 1], lambda bank: bank[:, :])
                    row_max(k + 1, nm[:, 2, h + j:h + j + 1], lambda bank: bank[:, 0:384], last=False)
                    row_max(k + 1, nm[:, 0, h + j:h + j + 1], lambda bank: bank[:, 384:512])
                else:
                    row_max(k, nm[:, 1, h:h + 2], lambda bank: bank[:, :].rearrange("p (h n) -> p h n", h=2))
            if kind == "nm":
                dve.wait_ge(*used(F_NM - 2, b))
                dve.wait_ge(*used(F_NM - 1, b))
                dve.tensor_copy(nm_part[:, :, 0, :], nm[:, :, :]).then_inc(nm_step, 1)
                dve.wait_ge(nm_step, 5 * b + 1)
                dve.tensor_tensor(nm_rest[:, :, :], nm[:, :, :], nm_part[:, :, 0, :], ALU.subtract).then_inc(nm_step, 1)
                dve.wait_ge(nm_step, 5 * b + 2)
                dve.tensor_copy(nm_part[:, :, 1, :], nm_rest[:, :, :]).then_inc(nm_step, 1)
                dve.wait_ge(nm_step, 5 * b + 3)
                dve.tensor_tensor(nm_rest[:, :, :], nm_rest[:, :, :], nm_part[:, :, 1, :], ALU.subtract).then_inc(nm_step, 1)
                dve.wait_ge(nm_step, 5 * b + 4)
                dve.tensor_copy(nm_part[:, :, 2, :], nm_rest[:, :, :]).then_inc(nm_step, 1)
            if kind == "s2" and i == HH + 1:
                norm_y(0, b)
            if kind == "pv":
                norm_y(1, b)
            if kind == "wo":
                for n in range(2):
                    dve.tensor_tensor(x2[:, 2 * n:2 * n + 2, :], full(F_WO + n, b)[:, :].rearrange("p (j d) -> p j d", j=2),
                                      xn[:, 2 * n:2 * n + 2, :], ALU.add).then_inc(free_sem(F_WO + n, b), 1)
                for t in range(TT):
                    dve.wait_ge(*used(F_WO + t // 2, b))
                    dve.bn_stats(st2[:, t, :], x2[:, t, :]).then_inc(stat2, 1)
                for t in range(TT):
                    dve.wait_ge(stat2, TT * b + t + 1)
                    dve.sem_inc(taken)
                    dve.bn_aggr(mv2[:, t, :], st2[:, t, :]).then_inc(stats2_done, 1)
                dve.wait_ge(sc2_step, 4 * (b + 1))
                dve.reciprocal(sc2[:, 4, :], sc2[:, 3, :]).then_inc(rms2_rec, 1)
                dve.wait_ge(rms2_rec, b + 1)
                for t in range(TT):
                    last = dve.tensor_scalar(h2[:, t, :], x2[:, t, :], sc2[:, 4, t:t + 1], None, ALU.mult)
                last.then_inc(h2_done, 1)
            if kind == "route":
                steps = [0]

                def step(ins):
                    ins.then_inc(rt_step, 1)
                    steps[0] += 1
                    dve.wait_ge(rt_step, RT * b + steps[0])
                dve.wait_ge(*used(F_RT, b))
                step(dve.tensor_scalar(pe_[:, :, :], pe_[:, :, :], 1.0, None, ALU.add))
                step(dve.reciprocal(prob[:, :, :], pe_[:, :, :]))
                over = prob[:, :, None, :].to_broadcast([P, TT, ER, ER])
                own = prob[:, :, :, None].to_broadcast([P, TT, ER, ER])
                step(dve.tensor_tensor(cmp1[:, :, :, :], over, own, ALU.is_gt))
                step(dve.tensor_tensor(cmp2[:, :, :, :], over, own, ALU.is_equal))
                step(dve.tensor_tensor(cmp2[:, :, :, :], cmp2[:, :, :, :], before[:, None, :, :].to_broadcast([P, TT, ER, ER]), ALU.mult))
                step(dve.tensor_tensor(cmp1[:, :, :, :], cmp1[:, :, :, :], cmp2[:, :, :, :], ALU.add))
                step(dve.tensor_reduce(rank[:, :, :], cmp1[:, :, :, :], AX.X, ALU.add))
                step(dve.scalar_tensor_tensor(wsel[:, :, :], rank[:, :, :], 2.0, prob[:, :, :], ALU.is_lt, ALU.mult))
                step(dve.tensor_reduce(wsum[:, :], wsel[:, :, :], AX.X, ALU.add))
                step(dve.reciprocal(wrec[:, :], wsum[:, :]))
                dve.tensor_tensor(wt[:, :, 0:ER], wsel[:, :, :], wrec[:, :, None].to_broadcast([P, TT, ER]), ALU.mult).then_inc(wt_ready, 1)

        def moe(kind, s, j, b):
            if kind == "g" and j == 1:
                dve.wait_ge(th_ready, NS * b + s + 1)
                dve.wait_ge(hm_raw, NS * b + max(s - 1, 0))
                dve.scalar_tensor_tensor(sg[:, s % 2, :], th[:, s % 2, :], 1.0, G[:, :], ALU.add, ALU.mult).then_inc(sg_ready, 1)
            if kind == "u" and j == 1:
                dve.wait_ge(sg_ready, NS * b + s + 1)
                dve.wait_ge(u_full, NS * b + s + 1)
                dve.wait_ge(down_done, NS * b + max(s - NHM + 1, 0))
                dve.tensor_tensor(hm[:, s % NHM, :], sg[:, s % 2, :], U[:, :], ALU.mult).then_inc(hm_raw, 1)
            if kind == "final":
                dve.wait_ge(down_done, NS * (b + 1))
                dve.wait_ge(xs_moved, b + 1)
                for n in range(2):
                    dve.scalar_tensor_tensor(xs[:, 2 * n:2 * n + 2, :], ACC[n][:, :, :], 0.5, xs[:, 2 * n:2 * n + 2, :],
                                             ALU.mult, ALU.add).then_inc(ot_done, 1)
        run(nc.vector, late, early, moe)

    @block.tensor
    def _(pe):
        pe.wait_ge(w_loaded, W_SMALL)
        pe.wait_ge(const_ready, 17)

        def free(k, r):
            pe.wait_ge(*freed(k, r))
            return bank_of(k, r)

        def full(k, r, ins):
            ins.then_inc(a_full[place(k, r)[0]], 1)

        def transposed(first, r, src):
            for k in range(KM):
                bank = free(first + k, r)
                for t in range(TT):
                    last = pe.transpose(bank[:, t * P:(t + 1) * P], src[:, t, k * P:(k + 1) * P], ident[:, :])
                full(first + k, r, last)

        def early(kind, i, j, b, r):
            if kind == "T":
                pe.wait_ge(h1_done, b + 1)
                transposed(F_T, r, h1)
            if kind == "lat":
                bank = free(F_LAT, r)
                pe.wait_ge(*used(F_T, r))
                pe.wait_ge(*used(F_T + 1, r))
                for k in range(KM):
                    last = pe.matmul(bank[:, :], w_lat[:, k, :], h1T[:, k, :], start=(k == 0), stop=(k == KM - 1))
                full(F_LAT, r, last)
            if kind == "kq":
                g = i
                k0 = F_KQ + 4 * g
                pe.wait_ge(*used(F_LAT, r))
                bank = free(k0, r)
                pe.matmul(bank[:, :], w_ka[:, g, :], lat[0:LAT, :], start=True, stop=False)
                for k in range(KM):
                    last = pe.matmul(bank[:, :], w_kra[:, k, g, :], h1T[:, k, :], start=False, stop=(k == KM - 1))
                full(k0, r, last)
                bank = free(k0 + 1, r)
                for k in range(KM):
                    last = pe.matmul(bank[:, :], w_krb[:, k, g, :], h1T[:, k, :], start=(k == 0), stop=(k == KM - 1))
                full(k0 + 1, r, last)
                for n in range(2):
                    bank = free(k0 + 2 + n, r)
                    full(k0 + 2 + n, r, pe.matmul(bank[:, :], w_q[LAT:P, n, g, :], lat[LAT:P, :], start=True, stop=True))
            if kind == "v":
                for n in range(2):
                    bank = free(F_V + n, r)
                    for q in range(2):
                        t = 2 * n + q
                        last = pe.matmul(bank[:, q * DM:(q + 1) * DM], lat[0:LAT, t * P:(t + 1) * P], w_vu[:, :], start=True, stop=True)
                    full(F_V + n, r, last)

        def scores(bank, c0, h, qb):
            n = P * (qb + 1)
            pe.matmul(bank[:, c0:c0 + n], qst[0:KS, h, qb * P:(qb + 1) * P], kst[0:KS, h, 0:n], start=True, stop=False)
            return pe.matmul(bank[:, c0 + qb * P:c0 + n], identb[:, :], mask_q[:, :], start=False, stop=True)

        def scores_t(bank, c0, h, kb):
            n = SEQ - P * kb
            pe.matmul(bank[:, c0:c0 + n], kst[:, h, kb * P:(kb + 1) * P], qst[:, h, kb * P:SEQ], start=True, stop=False)
            return pe.matmul(bank[:, c0:c0 + P], identb[:, :], mask_k[:, :], start=False, stop=True)

        def values(h, b):
            k = F_S2 + 3 * h + 2
            pe.wait_ge(*used(k, b))
            pe.wait_ge(*used(k - 1, b))
            if h == 0:
                pe.wait_ge(y_done, 4 * b)
            if h == HH:
                pe.wait_ge(y_done, 4 * b + 2)
            at = [0, 512, 896, 1152]
            for qb in range(TT):
                for kb in range(qb + 1):
                    c = at[kb] + (qb - kb) * P
                    last = pe.matmul(O[qb // 2][:, qb % 2, h % HH, :], pt[:, h % NPT, c:c + P], va[:, kb, h, :],
                                     start=(kb == 0), stop=(kb == qb))
            last.then_inc(pv_done, 1)

        def late(kind, i, j, b):
            if kind == "s1":
                h = 2 * i
                k = F_S1 + 5 * i + 2 * j
                if j == 0 and i % 4 == 0:
                    pe.wait_ge(stacked[i // 4], 16 * NSTACK * (b + 1))
                if j < 2:
                    full(k, b, scores(free(k, b), 0, h + j, 3))
                    bank = free(k + 1, b)
                    scores(bank, 0, h + j, 2)
                    full(k + 1, b, scores(bank, 384, h + j, 0))
                else:
                    bank = free(k, b)
                    scores(bank, 0, h, 1)
                    full(k, b, scores(bank, 256, h + 1, 1))
            if kind == "nm":
                bank = free(F_NM, b)
                pe.wait_ge(nm_step, 5 * (b + 1))
                pe.sem_inc(taken)
                for t in range(TT):
                    last = pe.transpose(bank[0:PARTS * NH, t * 64:(t + 1) * 64].bitcast(bf16),
                                        nm_part[:, t, :, :].rearrange("p c h -> p (c h)"), identb[:, :])
                full(F_NM, b, last)
            if kind == "s2":
                h = i
                if h == 0:
                    pe.wait_ge(nm_stacked, 48 * (b + 1))
                    pe.wait_ge(*used(F_V, b - 1 if not isinstance(b, int) or b > 0 else -1))
                    pe.wait_ge(*used(F_V + 1, b - 1 if not isinstance(b, int) or b > 0 else -1))
                k = F_S2 + 3 * h
                full(k, b, scores_t(free(k, b), 0, h, 0))
                full(k + 1, b, scores_t(free(k + 1, b), 0, h, 1))
                if h >= 1:
                    values(h - 1, b)
                bank = free(k + 2, b)
                scores_t(bank, 0, h, 2)
                full(k + 2, b, scores_t(bank, 256, h, 3))
            if kind == "pv":
                values(NH - 1, b)
            if kind == "yt":
                pe.wait_ge(y_done, 4 * (b + 1))
                transposed(F_YT, b, y)
            if kind == "wo":
                pe.wait_ge(*used(F_YT, b))
                pe.wait_ge(*used(F_YT + 1, b))
                for n in range(2):
                    bank = free(F_WO + n, b)
                    for q in range(2):
                        t = 2 * n + q
                        for k in range(KM):
                            last = pe.matmul(bank[:, q * DM:(q + 1) * DM], yT[:, k, t * P:(t + 1) * P], w_o[:, k, :],
                                             start=(k == 0), stop=(k == KM - 1))
                    full(F_WO + n, b, last)
            if kind == "ht":
                pe.wait_ge(h2_done, b + 1)
                transposed(F_HT, b, h2)
            if kind == "route":
                bank = free(F_RT, b)
                pe.wait_ge(*used(F_HT, b))
                pe.wait_ge(*used(F_HT + 1, b))
                for t in range(TT):
                    cols = bank[:, t * ER:(t + 1) * ER]
                    for k in range(KM):
                        pe.matmul(cols, h2T[:, k, t * P:(t + 1) * P], w_r[:, k, :], start=(k == 0), stop=False)
                    last = pe.matmul(cols, ones[:, :], b_r[:, :], start=False, stop=True)
                full(F_RT, b, last)
                bank = free(F_WT, b)
                pe.wait_ge(wt_ready, b + 1)
                full(F_WT, b, pe.transpose(bank[0:TT * NX, 0:P], wt[:, :, :].rearrange("p j e -> p (j e)"), ident[:, :]))

        def moe(kind, s, j, b):
            e, i = s // 2, s % 2
            if kind in ("g", "u"):
                w, bank, done, free_ = (wg, G, g_full, sg_ready) if kind == "g" else (wu, U, u_full, hm_raw)
                if j == 0:
                    if s == 0 and kind == "g":
                        pe.wait_ge(moe_w_loaded, 16 * 3 * NX)
                    pe.wait_ge(free_, NS * b + s)
                last = pe.matmul(bank[:, :], w[:, e, j, i * P:(i + 1) * P], h2T[:, j, :], start=(j == 0), stop=(j == KM - 1))
                if j == KM - 1:
                    last.then_inc(done, 1)
            if kind == "d":
                if j == 0:
                    if s == 0:
                        pe.wait_ge(ot_done, 2 * b)
                    if s < 2:
                        pe.wait_ge(hm_raw, NS * b + s + 1)
                    else:
                        pe.wait_ge(hm_ready, 14 * b + s - 1)
                for q in range(2):
                    t = 2 * j + q
                    last = pe.matmul(ACC[j][:, q, :], hm[:, s % NHM, t * P:(t + 1) * P], wd[:, e, i, :],
                                     start=(s == 0 and q == 0), stop=(s == NS - 1 and q == 1), skip_group_check=True)
                if j == 1:
                    last.then_inc(down_done, 1)
        run(nc.tensor, late, early, moe)


def build_mamba(nc, ctx, x_tm, res_tm, out_tm, W_in, W_conv, b_conv, W_xproj, W_dt, b_dt, A_log, D, W_out):
    f32 = mybir.dt.float32
    ALU = mybir.AluOpType
    ACT = mybir.ActivationFunctionType

    CT = 16
    CN = CT * BATCH
    NCH = SEQ // CT
    ST = 8
    SN = ST * BATCH
    NSUB = CT // ST
    NU = 2 * NSUB
    KM = DM // P
    MI = DI // P
    TT = CN // P
    HALO = (TAPS - 1) * BATCH
    UW = 2 * NST * BATCH
    CLIP = 10.0
    DA_MIN = math.exp(-CLIP)

    def sb(name, shape, dt=f32):
        return ctx.enter_context(nc.sbuf_tensor(name, shape, dt))

    def pb(name, shape, dt=f32):
        return ctx.enter_context(nc.psum_tensor(name, shape, dt))

    def sem(name):
        return ctx.enter_context(nc.semaphore(name))

    w_in = sb("m_w_in", [P, KM, 2 * DI])
    w_xp = sb("m_w_xp", [P, MI, RANK + 2 * NST])
    w_dt = sb("m_w_dt", [RANK + 1, DI])
    w_out = sb("m_w_out", [P, MI, DM])
    w_cv = sb("m_w_cv", [P, TAPS, MI])
    b_cv = sb("m_b_cv", [1, DI])
    a_neg = sb("m_a_neg", [P, MI, NST])
    d_col = sb("m_d_col", [P, MI])
    ident = sb("m_ident", [P, P])
    cv_diag = sb("m_cv_diag", [P, TAPS * MI, P])
    d_diag = sb("m_d_diag", [P, MI, P])
    ones = sb("m_ones", [1, CN])
    mhalf = sb("m_mhalf", [P, TT])
    eps = sb("m_eps", [P, TT])

    xm = sb("m_xm", [P, TT, DM])
    st6 = sb("m_st6", [P, TT, 6])
    mv = sb("m_mv", [P, TT, 2])
    veps = sb("m_veps", [P, TT])
    rstd = sb("m_rstd", [P, TT])
    xn = sb("m_xn", [P, TT, DM])
    xnT = sb("m_xnT", [P, KM, CN])
    xpad = sb("m_xpad", [P, MI, HALO + CN])
    th_z = sb("m_th_z", [P, MI, CN])
    th_x = sb("m_th_x", [P, MI, CN])
    dt_in = sb("m_dt_in", [RANK + 1, CN])
    bc_row = sb("m_bc_row", [RANK + 2 * NST, CN])
    sp_e = sb("m_sp_e", [P, MI, CN])
    sp_u = sb("m_sp_u", [P, MI, CN])
    sp_v = sb("m_sp_v", [P, MI, CN])
    sp_r = sb("m_sp_r", [P, MI, CN])
    x2 = sb("m_x2", [P, 2, MI, CN])
    zs = sb("m_zs", [P, 2, MI, CN])
    dtt = sb("m_dt", [P, 2, MI, CN])
    dtx = sb("m_dtx", [P, 2, MI, CN])
    dA = sb("m_dA", [P, 2, 2, NST, SN])
    ub = sb("m_ub", [P, 2, 2, NST, SN])
    Bb = sb("m_Bb", [P, NSUB, NST, SN])
    Cb = sb("m_Cb", [P, NSUB, NST, SN])
    yz = sb("m_yz", [P, MI, CN])
    res = sb("m_res", [P, TT, DM])
    ot = sb("m_ot", [P, TT, DM])
    bc_dram = nc.dram_tensor("m_bc_dram", [NSUB, 2, NST, SN], f32).ap()

    S = [pb(f"m_S{h}", [P, UW]) for h in range(2)]
    PR = pb("m_PR", [P, UW])
    Y = pb("m_Y", [P, 512])
    F = [pb(f"m_F{i}", [P, 2, CN]) for i in range(4)]

    w_loaded = sem("m_w_loaded")
    ident_ready = sem("m_ident_ready")
    setup_done = sem("m_setup_done")
    setup_neg = sem("m_setup_neg")
    sp_taken = sem("m_sp_taken")
    taken = sem("m_taken")
    x_loaded = sem("m_x_loaded")
    stat = sem("m_stat")
    stats_done = sem("m_stats_done")
    veps_done = sem("m_veps_done")
    rstd_done = sem("m_rstd_done")
    xn_done = sem("m_xn_done")
    xT_done = sem("m_xT_done")
    xnT_ready = sem("m_xnT_ready")
    xz_done = sem("m_xz_done")
    xpad_ready = sem("m_xpad_ready")
    halo_done = sem("m_halo_done")
    thz_ready = sem("m_thz_ready")
    zs_ready = sem("m_zs_ready")
    conv_done = sem("m_conv_done")
    thx_ready = sem("m_thx_ready")
    x2_ready = sem("m_x2_ready")
    dbc_done = sem("m_dbc_done")
    dtin_ready = sem("m_dtin_ready")
    bcrow_ready = sem("m_bcrow_ready")
    dtp_done = sem("m_dtp_done")
    sp_abs = sem("m_sp_abs")
    sp_relu = sem("m_sp_relu")
    sp_exp = sem("m_sp_exp")
    sp_one = sem("m_sp_one")
    sp_low = sem("m_sp_low")
    sp_ln = sem("m_sp_ln")
    sp_sub = sem("m_sp_sub")
    dt_ready = sem("m_dt_ready")
    dtx_ready = sem("m_dtx_ready")
    bc_stored = sem("m_bc_stored")
    b_loaded = [sem(f"m_b_loaded{s}") for s in range(NSUB)]
    c_loaded = [sem(f"m_c_loaded{s}") for s in range(NSUB)]
    dA_ready = [sem(f"m_dA_ready{u}") for u in range(NU)]
    u_ready = [sem(f"m_u_ready{u}") for u in range(NU)]
    p_step = sem("m_p_step")
    s_step = sem("m_s_step")
    sc_unit = [sem(f"m_sc_unit{u}") for u in range(NU)]
    nsum_done = [sem(f"m_nsum_done{u}") for u in range(NU)]
    yz_done = sem("m_yz_done")
    outp_done = sem("m_outp_done")
    res_loaded = sem("m_res_loaded")
    ot_done = sem("m_ot_done")
    ot_stored = sem("m_ot_stored")

    def same_half_before(u, c):
        return (u - 2, c + 1) if u >= 2 else (u + 2, c)

    def chunk_order(body, tail):
        def run(eng):
            body(0, 0, True, False)
            with eng.Fori(0, NCH // 2 - 1) as g:
                body(g * 2 + 1, 1, False, False)
                body(g * 2 + 2, 0, False, False)
            body(NCH - 1, 1, False, True)
            tail(NCH - 1, 1)
        return run

    block = ctx.enter_context(nc.Block())

    @block.sync
    def _(sp):
        loads = [
            (w_in[:, :, :], W_in.rearrange("(k p) n -> p k n", p=P)),
            (w_xp[:, :, :], W_xproj.rearrange("(k p) n -> p k n", p=P)),
            (w_dt[0:RANK, :], W_dt),
            (w_dt[RANK:RANK + 1, :], b_dt.rearrange("(a n) -> a n", a=1)),
            (w_out[:, :, :], W_out.rearrange("(k p) n -> p k n", p=P)),
            (a_neg[:, :, :], A_log.rearrange("(m p) n -> p m n", p=P)),
            (b_cv[:, :], b_conv.rearrange("(a n) -> a n", a=1)),
        ]
        for dst, src in loads:
            sp.dma_start(dst, src).then_inc(w_loaded, 16)
        with nc.allow_non_contiguous_dma(reason="per-channel columns, once"):
            for k in range(TAPS):
                sp.dma_start(w_cv[:, k, :], W_conv[k, :].rearrange("(m p) -> p m", p=P)).then_inc(w_loaded, 16)
            sp.dma_start(d_col[:, :], D.rearrange("(m p) -> p m", p=P)).then_inc(w_loaded, 16)

        def held(s, v):
            sp.wait_ge(s, v)
            sp.sem_inc(sp_taken)

        def row_of(c):
            return c * CN if isinstance(c, int) else sp.snap(c * CN)

        def load_x(c):
            rows = row_of(c)
            held(xn_done, TT * c)
            sp.dma_start(xm[:, :, :], x_tm[bass.ds(rows, CN), :].rearrange("(j p) d -> p j d", p=P)).then_inc(x_loaded, 16)

        def spread_bc(c):
            for s in range(NSUB):
                held(b_loaded[s], 16 * c)
                held(c_loaded[s], 16 * c)
            held(bcrow_ready, c + 1)
            for s in range(NSUB):
                for i in range(2):
                    sp.dma_start(bc_dram[s, i, :, :], bc_row[RANK + i * NST:RANK + (i + 1) * NST, s * SN:(s + 1) * SN]).then_inc(bc_stored, 16)
            held(bc_stored, 64 * (c + 1))
            for s in range(NSUB):
                held(u_ready[2 * s + 1], 2 * c)
                sp.dma_start(Bb[:, s, :, :], bc_dram[s:s + 1, 0, :, :].to_broadcast([P, NST, SN])).then_inc(b_loaded[s], 16)
                held(sc_unit[2 * s + 1], c)
                sp.dma_start(Cb[:, s, :, :], bc_dram[s:s + 1, 1, :, :].to_broadcast([P, NST, SN])).then_inc(c_loaded[s], 16)

        def load_res(c):
            rows = row_of(c)
            held(ot_done, c)
            sp.dma_start(res[:, :, :], res_tm[bass.ds(rows, CN), :].rearrange("(j p) d -> p j d", p=P)).then_inc(res_loaded, 16)

        def store(c):
            rows = row_of(c)
            held(ot_done, c + 1)
            sp.dma_start(out_tm[bass.ds(rows, CN), :].rearrange("(j p) d -> p j d", p=P), ot[:, :, :]).then_inc(ot_stored, 16)

        load_x(0)
        spread_bc(0)
        load_x(1)

        def chunk(c, rows_ahead=True):
            store(c - 1)
            load_res(c)
            spread_bc(c + 1)
            if rows_ahead:
                load_x(c + 2)

        load_res(0)
        spread_bc(1)
        load_x(2)
        with sp.Fori(1, NCH - 2) as c:
            chunk(c)
        chunk(NCH - 2, rows_ahead=False)
        store(NCH - 2)
        load_res(NCH - 1)
        store(NCH - 1)
        sp.wait_ge(ot_stored, 16 * NCH)

    @block.gpsimd
    def _(pool):
        pool.memset(ident[:, :], 0.0).then_inc(ident_ready, 1)
        pool.wait_ge(ident_ready, 1)
        pool.affine_select(out=ident[:, :], in_=ident[:, :], compare_op=ALU.not_equal, fill=1.0,
                           base=0, pattern=[[-1, P]], channel_multiplier=1).then_inc(ident_ready, 1)
        pool.wait_ge(ident_ready, 2)
        pool.memset(mhalf[:, :], -0.5).then_inc(ident_ready, 1)
        pool.wait_ge(ident_ready, 3)
        pool.memset(dt_in[RANK:RANK + 1, :], 1.0).then_inc(ident_ready, 1)
        pool.wait_ge(ident_ready, 4)
        pool.memset(ones[:, :], 1.0).then_inc(ident_ready, 1)
        pool.wait_ge(ident_ready, 5)
        pool.memset(xpad[:, :, 0:HALO], 0.0).then_inc(ident_ready, 1)
        pool.wait_ge(ident_ready, 6)
        pool.memset(eps[:, :], 1e-5).then_inc(ident_ready, 1)
        pool.wait_ge(ident_ready, 7)

        def rstd_of(c):
            pool.wait_ge(stats_done, TT * (c + 1))
            pool.tensor_tensor(veps[:, :], mv[:, :, 1], eps[:, :], ALU.add).then_inc(veps_done, 1)
            pool.wait_ge(veps_done, c + 1)
            pool.wait_ge(xn_done, TT * c)
            pool.tensor_tensor(rstd[:, :], veps[:, :], mhalf[:, :], ALU.pow).then_inc(rstd_done, 1)

        def dt_sum(c, par):
            pool.wait_ge(sp_ln, c + 1)
            pool.wait_ge(sp_relu, 2 * (c + 1))
            pool.tensor_tensor(sp_u[:, :, :], sp_u[:, :, :], sp_r[:, :, :], ALU.add).then_inc(sp_sub, 1)
            pool.wait_ge(sp_sub, c + 1)
            pool.wait_ge(sp_low, c + 1)
            if not isinstance(c, int) or c >= 2:
                pool.wait_ge(dtx_ready, c - 1)
                pool.wait_ge(dA_ready[NU - 1], c - 1)
            pool.tensor_tensor(dtt[:, par, :, :], sp_u[:, :, :], sp_v[:, :, :], ALU.subtract).then_inc(dt_ready, 1)

        def inputs_of(c, par, u):
            s, h = u // 2, u % 2
            pool.wait_ge(dtx_ready, c + 1)
            pool.wait_ge(b_loaded[s], 16 * (c + 1))
            pu, pc = same_half_before(u, c)
            for i in range(2):
                m = 2 * h + i
                pool.wait_ge(nsum_done[pu], 2 * (pc - 1) + i + 1 if isinstance(pc, int) and pc >= 1 or not isinstance(pc, int) else 0)
                pool.tensor_tensor(ub[:, h, i, :, :], Bb[:, s, :, :],
                                   dtx[:, par, m, None, s * SN:(s + 1) * SN].to_broadcast([P, NST, SN]),
                                   ALU.mult).then_inc(u_ready[u], 1)

        def front(c, par):
            rstd_of(c)
            dt_sum(c, par)

        front(0, 0)
        inputs_of(0, 0, 0)
        inputs_of(0, 0, 1)

        def body(c, par, first, last):
            if not last:
                rstd_of(c + 1)
            inputs_of(c, par, 2)
            inputs_of(c, par, 3)
            if not last:
                dt_sum(c + 1, 1 - par)
                inputs_of(c + 1, 1 - par, 0)
                inputs_of(c + 1, 1 - par, 1)
        chunk_order(body, lambda c, par: None)(nc.gpsimd)

    @block.scalar
    def _(act):
        act.wait_ge(w_loaded, 16 * 12)
        act.activation(a_neg[:, :, :], a_neg[:, :, :], ACT.Exp).then_inc(setup_neg, 1)

        def evac_T(c):
            act.wait_ge(xT_done, c + 1)
            act.wait_ge(xz_done, 4 * c)
            act.activation(xnT[:, :, :], F[0][:, :, :], ACT.Copy).then_inc(xnT_ready, 1)

        def evac_x(c):
            act.wait_ge(conv_done, 2 * c)
            act.wait_ge(xpad_ready, 2 * c)
            act.wait_ge(ident_ready, 6)
            if not isinstance(c, int) or c > 0:
                act.activation(xpad[:, :, 0:HALO], xpad[:, :, CN:CN + HALO], ACT.Copy).then_inc(halo_done, 1)
                act.wait_ge(halo_done, c)
            for i in range(2):
                act.wait_ge(xz_done, 4 * c + i + 1)
                act.activation(xpad[:, 2 * i:2 * i + 2, HALO:HALO + CN], F[1 + i][:, :, :], ACT.Copy).then_inc(xpad_ready, 1)

        def tanh_z(c):
            for i in range(2):
                act.wait_ge(xz_done, 4 * c + 3 + i)
                act.wait_ge(zs_ready, 2 * c)
                act.activation(th_z[:, 2 * i:2 * i + 2, :], F[(3 + i) % 4][:, :, :], ACT.Tanh, scale=0.5).then_inc(thz_ready, 1)

        def tanh_x(c):
            for i in range(2):
                act.wait_ge(conv_done, 2 * c + i + 1)
                act.wait_ge(x2_ready, 2 * c)
                act.activation(th_x[:, 2 * i:2 * i + 2, :], F[1 + i][:, :, :], ACT.Tanh, scale=0.5).then_inc(thx_ready, 1)

        def evac_dbc(c):
            act.wait_ge(dbc_done, c + 1)
            act.wait_ge(dtp_done, 2 * c)
            act.activation(dt_in[0:RANK, :], F[3][0:RANK, 0, :], ACT.Copy).then_inc(dtin_ready, 1)
            act.wait_ge(bc_stored, 64 * c)
            act.activation(bc_row[RANK:RANK + 2 * NST, :], F[3][RANK:RANK + 2 * NST, 0, :], ACT.Copy).then_inc(bcrow_ready, 1)

        def softplus(c):
            act.wait_ge(dt_ready, c)
            for i in range(2):
                act.wait_ge(dtp_done, 2 * c + i + 1)
                act.activation(sp_e[:, 2 * i:2 * i + 2, :], F[i][:, :, :], ACT.Abs).then_inc(sp_abs, 1)
                act.activation(sp_r[:, 2 * i:2 * i + 2, :], F[i][:, :, :], ACT.Relu).then_inc(sp_relu, 1)
            act.wait_ge(sp_abs, 2 * (c + 1))
            act.activation(sp_e[:, :, :], sp_e[:, :, :], ACT.Exp, scale=-1.0).then_inc(sp_exp, 1)

        def ln(c):
            act.wait_ge(sp_exp, c + 1)
            act.activation(sp_u[:, :, :], sp_e[:, :, :], ACT.Ln, bias=1.0).then_inc(sp_ln, 1)

        def decays(c, par, u):
            s, h = u // 2, u % 2
            act.wait_ge(dt_ready, c + 1)
            pu, pc = same_half_before(u, c)
            if pu < u:
                act.wait_ge(s_step, NU * ST * c + ST * (pu + 1) + 2)
            elif not isinstance(c, int) or c > 0:
                act.wait_ge(s_step, NU * ST * (c - 1) + ST * (pu + 1) + 2)
            for i in range(2):
                m = 2 * h + i
                for n in range(NST):
                    last = act.activation(dA[:, h, i, n, :], dtt[:, par, m, s * SN:(s + 1) * SN], ACT.Exp,
                                          scale=a_neg[:, m, n:n + 1])
            last.then_inc(dA_ready[u], 1)

        act.wait_ge(setup_neg, 2)
        evac_T(0)
        evac_x(0)
        tanh_z(0)
        tanh_x(0)
        evac_dbc(0)
        softplus(0)
        ln(0)
        decays(0, 0, 0)
        decays(0, 0, 1)

        def body(c, par, first, last):
            if not last:
                evac_T(c + 1)
                evac_x(c + 1)
                tanh_z(c + 1)
            decays(c, par, 2)
            if not last:
                tanh_x(c + 1)
                evac_dbc(c + 1)
                softplus(c + 1)
            decays(c, par, 3)
            if not last:
                ln(c + 1)
                decays(c + 1, 1 - par, 0)
                decays(c + 1, 1 - par, 1)
        chunk_order(body, lambda c, par: None)(nc.scalar)

    @block.vector
    def _(dve):
        dve.memset(S[0][:, :], 0.0).then_inc(s_step, 1)
        dve.memset(S[1][:, :], 0.0).then_inc(s_step, 1)
        dve.wait_ge(w_loaded, 16 * 12)
        dve.wait_ge(ident_ready, 6)
        dve.wait_ge(setup_neg, 1)
        dve.tensor_scalar(a_neg[:, :, :], a_neg[:, :, :], -1.0, None, ALU.mult).then_inc(setup_neg, 1)
        dve.tensor_scalar(w_xp[:, :, :], w_xp[:, :, :], 0.5, None, ALU.mult).then_inc(setup_done, 1)
        for k in range(TAPS):
            for m in range(MI):
                dve.tensor_scalar(cv_diag[:, k * MI + m, :], ident[:, :], w_cv[:, k, m:m + 1], None, ALU.mult).then_inc(setup_done, 1)
        for m in range(MI):
            dve.tensor_scalar(d_diag[:, m, :], ident[:, :], d_col[:, m:m + 1], 0.5, ALU.mult, ALU.mult).then_inc(setup_done, 1)

        def stats(c):
            dve.wait_ge(x_loaded, 16 * (c + 1))
            for j in range(TT):
                dve.bn_stats(st6[:, j, :], xm[:, j, :]).then_inc(stat, 1)
            for j in range(TT):
                dve.wait_ge(stat, TT * c + j + 1)
                dve.wait_ge(xn_done, TT * c)
                dve.wait_ge(veps_done, c)
                dve.sem_inc(taken)
                dve.bn_aggr(mv[:, j, :], st6[:, j, :]).then_inc(stats_done, 1)

        def normalise(c):
            dve.wait_ge(rstd_done, c + 1)
            dve.wait_ge(xT_done, c)
            for j in range(TT):
                dve.tensor_scalar(xn[:, j, :], xm[:, j, :], mv[:, j, 0:1], rstd[:, j:j + 1],
                                  ALU.subtract, ALU.mult).then_inc(xn_done, 1)

        def gate_z(c, par):
            if not isinstance(c, int) or c >= 2:
                dve.wait_ge(yz_done, NU * (c - 1))
            for i in range(2):
                dve.wait_ge(thz_ready, 2 * c + i + 1)
                dve.scalar_tensor_tensor(zs[:, par, 2 * i:2 * i + 2, :], th_z[:, 2 * i:2 * i + 2, :], 1.0,
                                         F[(3 + i) % 4][:, :, :], ALU.add, ALU.mult).then_inc(zs_ready, 1)

        def silu_x(c, par):
            if not isinstance(c, int) or c >= 2:
                dve.wait_ge(nsum_done[NU - 1], 2 * (c - 1))
            for i in range(2):
                dve.wait_ge(thx_ready, 2 * c + i + 1)
                dve.scalar_tensor_tensor(x2[:, par, 2 * i:2 * i + 2, :], th_x[:, 2 * i:2 * i + 2, :], 1.0,
                                         F[1 + i][:, :, :], ALU.add, ALU.mult).then_inc(x2_ready, 1)

        def log_rest(c):
            dve.wait_ge(sp_exp, c + 1)
            dve.wait_ge(dt_ready, c)
            dve.tensor_scalar(sp_v[:, :, :], sp_e[:, :, :], 1.0, 1.0, ALU.add, ALU.subtract).then_inc(sp_one, 1)
            dve.wait_ge(sp_one, c + 1)
            dve.tensor_tensor(sp_v[:, :, :], sp_v[:, :, :], sp_e[:, :, :], ALU.subtract).then_inc(sp_low, 1)

        def dt_times_x(c, par):
            dve.wait_ge(dt_ready, c + 1)
            dve.wait_ge(x2_ready, 2 * (c + 1))
            if not isinstance(c, int) or c >= 2:
                dve.wait_ge(u_ready[NU - 1], 2 * (c - 1))
            dve.scalar_tensor_tensor(dtx[:, par, :, :], x2[:, par, :, :], 0.5, dtt[:, par, :, :],
                                     ALU.mult, ALU.mult).then_inc(dtx_ready, 1)

        def scan(c, u, between):
            s, h = u // 2, u % 2
            base = NU * ST * c + ST * u
            dve.wait_ge(dA_ready[u], c + 1)
            dve.wait_ge(u_ready[u], 2 * (c + 1))
            dve.wait_ge(c_loaded[s], 16 * (c + 1))
            banks = (S[h], PR)

            def times_c(t):
                cols = slice(t * BATCH, (t + 1) * BATCH)
                return dve.tensor_tensor(ub[:, h, :, :, cols],
                                         banks[(t + 1) % 2][:, :].rearrange("p (i n b) -> p i n b", i=2, n=NST),
                                         Cb[:, s, None, :, cols].to_broadcast([P, 2, NST, BATCH]), ALU.mult)
            for t in range(ST):
                cols = slice(t * BATCH, (t + 1) * BATCH)
                old = banks[t % 2][:, :].rearrange("p (a b) -> p a b", b=BATCH)
                new = banks[(t + 1) % 2][:, :].rearrange("p (a b) -> p a b", b=BATCH)
                dve.wait_ge(s_step, base + t + 2)
                step = dve.scalar_tensor_tensor(new, dA[:, h, :, :, cols].rearrange("p i n b -> p (i n) b"), DA_MIN,
                                                old, ALU.max, ALU.mult)
                step.then_inc(p_step, 1)
                if t > 0:
                    times_c(t - 1)
                if t in between:
                    between[t]()
                dve.wait_ge(p_step, base + t + 1)
                dve.sem_inc(taken)
                dve._custom_dve(bass.dve_ops.TENSOR_ADD_SAT, out=new, in0=new,
                                in1=ub[:, h, :, :, cols].rearrange("p i n b -> p (i n) b"),
                                s0=CLIP, s1=-CLIP).then_inc(s_step, 1)
            dve.wait_ge(s_step, base + ST + 2)
            times_c(ST - 1).then_inc(sc_unit[u], 1)

        def gate_y(c, par, u):
            s, h = u // 2, u % 2
            dve.wait_ge(nsum_done[u], 2 * (c + 1))
            dve.wait_ge(outp_done, c)
            dve.tensor_tensor(yz[:, 2 * h:2 * h + 2, s * SN:(s + 1) * SN],
                              Y[:, 0:2 * SN].rearrange("p (i q) -> p i q", i=2),
                              zs[:, par, 2 * h:2 * h + 2, s * SN:(s + 1) * SN], ALU.mult).then_inc(yz_done, 1)

        def add_res(c):
            dve.wait_ge(outp_done, c + 1)
            dve.wait_ge(res_loaded, 16 * (c + 1))
            dve.wait_ge(ot_stored, 16 * c)
            dve.scalar_tensor_tensor(ot[:, :, :], Y[:, :].rearrange("p (j d) -> p j d", j=TT), 0.5, res[:, :, :],
                                     ALU.mult, ALU.add).then_inc(ot_done, 1)

        stats(0)
        normalise(0)
        gate_z(0, 0)
        silu_x(0, 0)
        log_rest(0)
        dt_times_x(0, 0)

        def body(c, par, first, last):
            slots = [dict() for _ in range(NU)]
            if not first:
                slots[0][3] = lambda: gate_y(c - 1, 1 - par, NU - 1)
                slots[0][6] = lambda: add_res(c - 1)
            for u in range(1, NU):
                slots[u][4] = lambda u=u: gate_y(c, par, u - 1)
            if not last:
                slots[0][1] = lambda: stats(c + 1)
                slots[0][4] = lambda: normalise(c + 1)
                slots[1][2] = lambda: gate_z(c + 1, 1 - par)
                slots[1][6] = lambda: silu_x(c + 1, 1 - par)
                slots[2][6] = lambda: log_rest(c + 1)
                slots[3][3] = lambda: dt_times_x(c + 1, 1 - par)
            for u in range(NU):
                scan(c, u, slots[u])

        def tail(c, par):
            gate_y(c, par, NU - 1)
            add_res(c)
        chunk_order(body, tail)(nc.vector)

    @block.tensor
    def _(pe):
        pe.wait_ge(w_loaded, 16 * 12)
        pe.wait_ge(setup_done, 1 + TAPS * MI + MI)
        pe.wait_ge(ident_ready, 6)

        def transposes(c):
            pe.wait_ge(xn_done, TT * (c + 1))
            pe.wait_ge(sp_abs, 2 * c)
            pe.wait_ge(sp_relu, 2 * c)
            for k in range(KM):
                for j in range(TT):
                    last = pe.transpose(F[0][:, k, j * P:(j + 1) * P], xn[:, j, k * P:(k + 1) * P], ident[:, :])
            last.then_inc(xT_done, 1)

        def project(c):
            pe.wait_ge(xnT_ready, c + 1)
            for i in range(4):
                if i == 0:
                    pe.wait_ge(sp_abs, 2 * c)
                    pe.wait_ge(sp_relu, 2 * c)
                if i == 1:
                    pe.wait_ge(x2_ready, 2 * c)
                if i == 2:
                    pe.wait_ge(bcrow_ready, c)
                    pe.wait_ge(dtin_ready, c)
                for m in range(2):
                    blk = 2 * i + m
                    for k in range(KM):
                        last = pe.matmul(F[(1 + i) % 4][:, m, :], w_in[:, k, blk * P:(blk + 1) * P], xnT[:, k, :],
                                         start=(k == 0), stop=(k == KM - 1))
                last.then_inc(xz_done, 1)

        def conv(c):
            for i in range(2):
                pe.wait_ge(xpad_ready, 2 * (c + 1))
                for j in range(2):
                    m = 2 * i + j
                    pe.matmul(F[1 + i][:, j, :], b_cv[:, m * P:(m + 1) * P], ones[:, :], start=True, stop=False)
                    for k in range(TAPS):
                        last = pe.matmul(F[1 + i][:, j, :], cv_diag[:, k * MI + m, :],
                                         xpad[:, m, k * BATCH:k * BATCH + CN], start=False, stop=(k == TAPS - 1))
                last.then_inc(conv_done, 1)

        def dbc(c):
            pe.wait_ge(zs_ready, 2 * c + 1)
            for m in range(MI):
                pe.wait_ge(x2_ready, 2 * c + m // 2 + 1)
                last = pe.matmul(F[3][0:RANK + 2 * NST, 0, :], w_xp[:, m, :], x2[:, ipar[0], m, :],
                                 start=(m == 0), stop=(m == MI - 1))
            last.then_inc(dbc_done, 1)

        ipar = [0]

        def dt_proj(c):
            pe.wait_ge(dtin_ready, c + 1)
            pe.wait_ge(zs_ready, 2 * (c + 1))
            for m in range(MI):
                last = pe.matmul(F[m // 2][:, m % 2, :], w_dt[:, m * P:(m + 1) * P], dt_in[:, :], start=True, stop=True)
                if m % 2:
                    last.then_inc(dtp_done, 1)

        def nsum(c, par, u):
            s, h = u // 2, u % 2
            if u > 0:
                pe.wait_ge(yz_done, NU * c + u)
            else:
                pe.wait_ge(ot_done, c)
            pe.wait_ge(sc_unit[u], c + 1)
            for i in range(2):
                m = 2 * h + i
                pe.matmul(Y[:, i * SN:(i + 1) * SN], d_diag[:, m, :], x2[:, par, m, s * SN:(s + 1) * SN], start=True, stop=False)
                for n in range(NST):
                    last = pe.matmul(Y[:, i * SN:(i + 1) * SN], ident[:, :], ub[:, h, i, n, :], start=False, stop=(n == NST - 1))
                last.then_inc(nsum_done[u], 1)

        def project_out(c):
            pe.wait_ge(yz_done, NU * (c + 1))
            for j in range(TT):
                for m in range(MI):
                    last = pe.matmul(Y[:, j * DM:(j + 1) * DM], yz[:, m, j * P:(j + 1) * P], w_out[:, m, :],
                                     start=(m == 0), stop=(m == MI - 1))
            last.then_inc(outp_done, 1)

        transposes(0)
        project(0)
        conv(0)
        dbc(0)
        dt_proj(0)

        def body(c, par, first, last):
            if not first:
                nsum(c - 1, 1 - par, NU - 1)
                project_out(c - 1)
            ipar[0] = 1 - par
            if not last:
                transposes(c + 1)
                project(c + 1)
            nsum(c, par, 0)
            if not last:
                conv(c + 1)
                dbc(c + 1)
            nsum(c, par, 1)
            if not last:
                dt_proj(c + 1)
            nsum(c, par, 2)

        def tail(c, par):
            nsum(c, par, NU - 1)
            project_out(c)
        chunk_order(body, tail)(nc.tensor)


_MAMBA_INS = ['L0_attn_W_in', 'L0_attn_W_conv', 'L0_attn_b_conv', 'L0_attn_W_xproj', 'L0_attn_W_dt', 'L0_attn_b_dt',
        'L0_attn_A_log', 'L0_attn_D', 'L0_attn_W_out']


_FFN_INS = ['w_ln1', 'w_ln2', 'W_kvd', 'W_qd', 'W_ka', 'W_kra', 'W_krb', 'W_qa', 'W_qb', 'W_vu', 'W_o', 'Wg', 'Wu', 'Wd',
        'W_router', 'routing_bias', 'rope_tab']


def rope_tables():
    HH = 8
    inv = (np.float32(1.0) / np.float32(10000.0) ** (np.arange(0, HH, 2, dtype=np.float32) / np.float32(HH))).astype(np.float32)
    f = np.arange(SEQ, dtype=np.float32)[:, None] * inv[None, :]
    f = np.concatenate([f, f], axis=1).astype(np.float32)
    sign = np.where(np.arange(HH) < HH // 2, -1.0, 1.0).astype(np.float32)
    c = np.ones((SEQ, 16), np.float32)
    s = np.zeros((SEQ, 16), np.float32)
    c[:, HH:] = np.cos(f)
    s[:, HH:] = np.sin(f) * sign
    c, s = (np.tile(a.T, (8, 1)) for a in (c, s))
    return np.stack([c, s, c * np.float32(0.25), s * np.float32(0.25)]).astype(np.float32)


def ffn_layouts(inputs):
    g = {k: np.asarray(v) for k, v in inputs.items()}
    a = {n: g['L0_ffn_' + n] for n in ('w_ln1', 'w_ln2', 'W_kvd', 'W_qd', 'W_vu', 'W_o', 'W_router', 'routing_bias')}

    def heads(first, second, swap):
        w = np.zeros(((first if first is not None else second).shape[0], 16, 16), np.float32)
        if first is not None:
            w[:, :, 0:8] = first.reshape(-1, 16, 8)
        if second is not None:
            s = second.reshape(-1, 16, 2, 4)
            w[:, :, 8:16] = (s[:, :, ::-1, :] if swap else s).reshape(-1, 16, 8)
        return w.reshape(-1, 256)
    a['W_ka'] = heads(g['L0_ffn_W_ku'], None, False)
    a['W_kra'] = heads(None, g['L0_ffn_W_ropek'], False)
    a['W_krb'] = heads(None, g['L0_ffn_W_ropek'], True)
    a['W_qa'] = heads(g['L0_ffn_W_qu'], g['L0_ffn_W_ropeq'], False)
    a['W_qb'] = heads(None, g['L0_ffn_W_ropeq'], True)
    for n in ('Wg', 'Wu', 'Wd'):
        a[n] = np.concatenate([g[f'L0_ffn_{n}_s'][None], g[f'L0_ffn_{n}_r']])
    a['rope_tab'] = rope_tables()
    return {n: np.ascontiguousarray(a[n]) for n in _FFN_INS}


def build(nc, t, out):
    part = nc.dram_tensor("x_plus_ffn", (SEQ * BATCH, DM), mybir.dt.float32).ap()
    with ExitStack() as ctx:
        build_ffn(nc, ctx, t["x_tm"], part, *[t[n] for n in _FFN_INS])
    with ExitStack() as ctx:
        build_mamba(nc, ctx, t["x_tm"], part, out, *[t[n] for n in _MAMBA_INS])


def kernel(**inputs):
    import concourse.bacc as _bacc
    from concourse.bass_utils import run_bass_kernel_spmd as _run

    nc = _bacc.Bacc("TRN2", target_bir_lowering=False, num_devices=1)
    arrays = {}
    x = np.asarray(inputs['L0_attn_x'])
    arrays["x_tm"] = np.ascontiguousarray(x.transpose(1, 0, 2)).reshape(SEQ * BATCH, DM)
    for n in _MAMBA_INS:
        arrays[n] = np.ascontiguousarray(np.asarray(inputs[n]))
    arrays.update(ffn_layouts(inputs))
    t = {k: nc.dram_tensor(k, v.shape, mybir.dt.from_np(v.dtype), kind="ExternalInput").ap() for k, v in arrays.items()}
    out = nc.dram_tensor("out_tm", (SEQ * BATCH, DM), mybir.dt.float32, kind="ExternalOutput").ap()
    build(nc, t, out)
    r = _run(nc, [arrays], core_ids=[0])
    got = r.results[0]["out_tm"].reshape(SEQ, BATCH, DM)
    return np.ascontiguousarray(got.transpose(1, 0, 2))
```

```python
import concourse.bass as bass
from concourse import mybir
from contextlib import ExitStack
import math
import numpy as np

BATCH, SEQ, DM = 16, 512, 256
DI, NST, RANK, TAPS = 512, 16, 64, 4
P = 128


def build_ffn(nc, ctx, x_tm, out_tm, w_ln1, w_ln2, W_kvd, W_qd, W_ka, W_kra, W_krb, W_qa, W_qb, W_vu, W_o,
              Wg, Wu, Wd, W_router, routing_bias, rope_tab):
    f32, bf16 = mybir.dt.float32, mybir.dt.bfloat16
    ALU, ACT, AX = mybir.AluOpType, mybir.ActivationFunctionType, mybir.AxisListType

    NH, HD, LAT = 16, 16, 64
    NX = 8
    ER = NX - 1
    KM = DM // P
    TT = SEQ // P
    PARTS = 3
    K_PART = (0, 0, 1, 0, 2, 1)
    Q_PART = (0, 1, 0, 2, 0, 1)
    KS = HD * len(K_PART)
    MASKED = -1e30
    VA = 32
    HG = P // VA
    NG = NH // HG

    def sb(name, shape, dt=f32):
        return ctx.enter_context(nc.sbuf_tensor(name, shape, dt))

    def pb(name, shape, dt=f32):
        return ctx.enter_context(nc.psum_tensor(name, shape, dt))

    def sem(name):
        return ctx.enter_context(nc.semaphore(name))

    ln1 = sb("f_ln1", [P, KM])
    ln2 = sb("f_ln2", [P, KM])
    w_lat = sb("f_w_lat", [P, KM, 2 * LAT])
    w_kra = sb("f_w_kra", [P, KM, 2, P])
    w_krb = sb("f_w_krb", [P, KM, 2, P])
    w_q = sb("f_w_q", [P, 2, 2, P])
    w_ka = w_q[0:LAT, 0, :, :]
    w_vu = w_q[0:LAT, 1, :, :].rearrange("p g n -> p (g n)")
    w_o = sb("f_w_o", [P, NG, DM])
    wg = sb("f_wg", [P, NX, KM, DM])
    wu = sb("f_wu", [P, NX, KM, DM])
    wd = sb("f_wd", [P, NX, KM, DM])
    w_r = sb("f_w_r", [P, KM, ER])
    b_r = sb("f_b_r", [1, ER])
    rope = sb("f_rope", [P, 2, SEQ])
    sel = sb("f_sel", [P, P])
    ident = sb("f_ident", [P, P])
    identb = sb("f_identb", [P, P], bf16)
    mask_q = sb("f_mask_q", [P, P], bf16)
    mask_k = sb("f_mask_k", [P, P], bf16)
    ones = sb("f_ones", [1, P])
    before = sb("f_before", [P, ER, ER])
    consts = sb("f_consts", [P, 3, TT])

    xm = sb("f_xm", [P, TT, DM])
    st6 = sb("f_st6", [P, TT, 6])
    mv = sb("f_mv", [P, TT, 2])
    sc1 = sb("f_sc1", [P, 8, TT])
    xn = sb("f_xn", [P, TT, DM])
    h1 = sb("f_h1", [P, TT, DM])
    h1T = sb("f_h1T", [P, KM, SEQ])
    lat = sb("f_lat", [P, SEQ])
    kq = sb("f_kq", [P, 4, SEQ])
    parts = sb("f_parts", [P, PARTS, 4, SEQ], bf16)
    kst = sb("f_kst", [KS + PARTS, NH, SEQ], bf16)
    qst = sb("f_qst", [KS + PARTS, NH, SEQ], bf16)
    va = sb("f_va", [P, TT, NH, VA])
    nm = sb("f_nm", [P, TT, NH])
    nm_rest = sb("f_nm_rest", [P, TT, NH])
    nm_part = sb("f_nm_part", [P, TT, PARTS, NH], bf16)
    nmT = sb("f_nmT", [PARTS * NH, SEQ], bf16)
    PT_W = SEQ * HG
    pt = sb("f_pt", [P, PT_W + PT_W * 3 // 4])
    kq_rest = pt[:, 0:4 * SEQ].rearrange("p (g n) -> p g n", g=4)
    ra = pt[:, 4 * SEQ:5 * SEQ]
    rb = pt[:, 5 * SEQ:6 * SEQ]
    yT = kq
    x2 = xn
    xs_next = sb("f_xs_next", [P, TT, DM])
    xs = sb("f_xs", [P, TT, DM])
    h2 = sb("f_h2", [P, TT, DM])
    h2T = sb("f_h2T", [P, KM, SEQ])
    st2 = sb("f_st2", [P, TT, 6])
    mv2 = sb("f_mv2", [P, TT, 2])
    sc2 = sb("f_sc2", [P, 6, TT])
    pe_ = sb("f_pe", [P, TT, ER])
    prob = sb("f_prob", [P, TT, ER])
    cmp1 = sb("f_cmp1", [P, TT, ER, ER])
    cmp2 = sb("f_cmp2", [P, TT, ER, ER])
    rank = sb("f_rank", [P, TT, ER])
    wsel = sb("f_wsel", [P, TT, ER])
    wsum = sb("f_wsum", [P, TT])
    wrec = sb("f_wrec", [P, TT])
    wt = sb("f_wt", [P, TT, NX])
    wtT = sb("f_wtT", [TT * NX, P])
    wbc = sb("f_wbc", [P, ER, SEQ])
    th = sb("f_th", [P, 2, SEQ])
    sg = sb("f_sg", [P, 2, SEQ])
    NHM = 3
    hm = sb("f_hm", [P, NHM, SEQ])
    parts_dram = nc.dram_tensor("f_parts_dram", [2, 8, HD, PARTS, 2, SEQ], bf16).ap()
    w_dram = nc.dram_tensor("f_w_dram", [ER, TT, P], f32).ap()

    A = [pb(f"f_A{i}", [P, SEQ]) for i in range(2)]
    O = [pb(f"f_O{i}", [P, SEQ]) for i in range(2)]
    ACC = [pb(f"f_ACC{i}", [P, 2, DM]) for i in range(2)]
    G = pb("f_G", [P, SEQ])
    U = pb("f_U", [P, SEQ])

    F_S1, F_WT = 0, 10
    F_NM = 5 * (NH // 2) + 1
    F_S2 = F_NM + 1
    S2_FILL = {}
    S2_ITEMS = []
    n_fills = F_S2
    N_S2 = [HG, HG, HG // 2, HG // 4]
    for q in range(NG * TT):
        g, kb = divmod(q, TT)
        for n in range(N_S2[kb]):
            if g > 0:
                if kb == 1 and n == 0:
                    S2_ITEMS.append(("bc", g - 1, 0))
                if kb == 1 and n == 2:
                    S2_ITEMS.append(("rc", g - 1, 0))
                if kb == 2 and n == 0:
                    S2_ITEMS.append(("rc", g - 1, 1))
                if kb == 2 and n == 1:
                    S2_ITEMS.append(("ym", g - 1, 0))
            S2_FILL[q, n] = n_fills
            n_fills += 1
            S2_ITEMS.append(("s2", q, n))
            if n == min(2, N_S2[kb]) - 1 and q > 0:
                S2_ITEMS.append(("pv", q - 1, 0))
                if kb == 0:
                    S2_ITEMS.append(("oc", g - 1, 0))
    F_T = n_fills
    F_LAT, F_WO, F_KQ, F_V, F_HT = F_T + 2, F_T + 3, F_T + 5, F_T + 13, F_T + 15
    F_RT = F_HT + 2
    NF = F_RT + 1
    N_EARLY = F_HT - F_T - 2
    assert NF % 2 == 0

    def place(k, r):
        if isinstance(r, int) and r < 0:
            k -= F_T if k < F_WO else F_T + 2
            return k % 2, k // 2
        if isinstance(r, int) and r == BATCH - 1 and F_WO <= k < F_KQ:
            k -= F_WO - F_T
        if isinstance(r, int) and r == BATCH - 1 and k >= F_HT:
            k -= N_EARLY
        if isinstance(r, int) and r == BATCH:
            k -= N_EARLY + F_WT
        if isinstance(r, int) and r == 0 and k < F_WT:
            k += 1
        k += N_EARLY - 1
        return k % 2, r * (NF // 2) + k // 2

    def probs_width(q):
        return 384 if q % TT == 1 else SEQ

    def probs(q, n):
        w = probs_width(q)
        c = (PT_W if q % 2 else 0) + n * w
        return pt[:, c:c + w]

    def s1_fill(i, j):
        return F_S1 + 5 * i + 2 * j + (1 if i > 1 else 0)

    w_loaded = sem("f_w_loaded")
    moe_w_loaded = sem("f_moe_w_loaded")
    const_ready = sem("f_const_ready")
    a_full = [sem(f"f_a_full{i}") for i in range(2)]
    a_free = [sem(f"f_a_free{i}") for i in range(2)]
    x_loaded = sem("f_x_loaded")
    stat1 = sem("f_stat1")
    stats_done = sem("f_stats_done")
    sc_step = sem("f_sc_step")
    rms_rec = sem("f_rms_rec")
    xn_done = sem("f_xn_done")
    xs_copied = sem("f_xs_copied")
    h1_done = sem("f_h1_done")
    kq_ready = sem("f_kq_ready")
    hi_ready = [sem(f"f_hi_ready{g}") for g in range(2)]
    rest_ready = [sem(f"f_rest_ready{g}") for g in range(2)]
    mid_ready = [sem(f"f_mid_ready{g}") for g in range(2)]
    lo_ready = [sem(f"f_lo_ready{g}") for g in range(2)]
    parts_stored = [sem(f"f_parts_stored{g}") for g in range(2)]
    stacked = [sem(f"f_stacked{g}") for g in range(2)]
    NSTACK = 2 * len(K_PART)
    nm_step = sem("f_nm_step")
    nm_stacked = sem("f_nm_stacked")
    pv_done = sem("f_pv_done")
    o_copied = sem("f_o_copied")
    sums_spread = sem("f_sums_spread")
    rec_done = sem("f_rec_done")
    y_done = sem("f_y_done")
    q_scaled = sem("f_q_scaled")
    xs_ready = sem("f_xs_ready")
    stat2 = sem("f_stat2")
    stats2_done = sem("f_stats2_done")
    sc2_step = sem("f_sc2_step")
    rms2_rec = sem("f_rms2_rec")
    h2_done = sem("f_h2_done")
    rt_step = sem("f_rt_step")
    wt_ready = sem("f_wt_ready")
    w_stored = sem("f_w_stored")
    wbc_loaded = sem("f_wbc_loaded")
    g_full = sem("f_g_full")
    u_full = sem("f_u_full")
    th_ready = sem("f_th_ready")
    sg_ready = sem("f_sg_ready")
    hm_raw = sem("f_hm_raw")
    hm_ready = sem("f_hm_ready")
    down_done = sem("f_down_done")
    ot_done = sem("f_ot_done")
    xs_moved = sem("f_xs_moved")
    ot_stored = sem("f_ot_stored")
    taken = sem("f_taken")
    RT = 10

    def filled(k, r):
        i, n = place(k, r)
        return a_full[i], n + 1

    def freed(k, r):
        i, n = place(k, r)
        return a_free[i], n

    def used(k, r):
        i, n = place(k, r)
        return a_free[i], n + 1

    def bank_of(k, r):
        return A[place(k, r)[0]]

    def free_sem(k, r):
        return a_free[place(k, r)[0]]

    NS = 2 * NX
    MOE = []
    for s in range(NS):
        MOE += [("g", s, 0), ("g", s, 1), ("u", s, 0), ("u", s, 1)]
        if s == NS - 1:
            MOE += [("ht", 0, 0)]
        if s >= 1:
            MOE += [("d", s - 1, 0), ("d", s - 1, 1)]
    MOE += [("d", NS - 1, 0), ("d", NS - 1, 1), ("final", 0, 0)]
    BETWEEN = {}

    def put(at, *names):
        BETWEEN.setdefault(at, []).extend(names)
    put(0, ("xload", 0, 0), ("rank", 0, 0))
    for i in range(NH // 2):
        for n in range(3):
            put(2 + 3 * i + n + (i > 0) + (i > 1), ("s1", i, n))
    put(6, ("xc", 0, 0))
    put(9, ("wt", 0, 0))
    put(28, ("nm", 0, 0))
    put(30, ("nmt", 0, 0))
    for n, item in enumerate(S2_ITEMS):
        put(36 + n * 24 // len(S2_ITEMS), item)
    put(40, ("bn", 0, 0))
    put(45, ("h1", 0, 0))
    put(60, ("pv", NG * TT - 1, 0), ("oc", NG - 1, 0))
    put(61, ("bc", NG - 1, 0), ("rc", NG - 1, 0))
    put(62, ("rc", NG - 1, 1), ("ym", NG - 1, 0), ("T", 0, 0))
    put(64, ("lat", 0, 0))
    put(66, ("wo", 0, 0))
    put(68, ("h2", 0, 0), ("xn", 0, 0))
    put(70, ("kq", 0, 0))
    put(73, ("kq", 0, 1), ("split", 0, 0))
    put(76, ("kq", 1, 0))
    put(79, ("kq", 1, 1), ("split", 1, 0))
    put(82, ("v", 0, 0))
    EARLY = ("xload", "bn", "h1", "xn", "T", "lat", "kq", "split", "v")
    ORDER = []
    for i, m in enumerate(MOE):
        ORDER.append(m)
        ORDER += BETWEEN.get(i, [])
    ORDER.append(("route", 0, 0))

    def run(eng, late, early, moe):
        def rnd(r):
            for kind, i, j in ORDER:
                if kind in EARLY:
                    if not (isinstance(r, int) and r >= BATCH - 1):
                        early(kind, i, j, r + 1, r)
                elif kind in ("g", "u", "d", "final", "rank", "wt", "xc"):
                    if not (isinstance(r, int) and r == 0):
                        moe(kind, i, j, r - 1)
                elif not (isinstance(r, int) and r == BATCH):
                    late(kind, i, j, r)
        for kind, i, j in ORDER:
            if kind in EARLY:
                early(kind, i, j, 0, -1)
        rnd(0)
        rnd(1)
        with eng.Fori(2, BATCH - 1) as r:
            rnd(r)
        rnd(BATCH - 1)
        rnd(BATCH)

    block = ctx.enter_context(nc.Block())
    act_loads = []

    @block.sync
    def _(sp):
        kp = "(k p) n -> p k n"
        loads = [
            (w_lat[:, :, 0:LAT], W_kvd.rearrange(kp, p=P)), (w_lat[:, :, LAT:2 * LAT], W_qd.rearrange(kp, p=P)),
            (w_ka, W_ka.rearrange("p (g n) -> p g n", g=2)),
            (w_kra[:, :, :, :], W_kra.rearrange("(k p) (g n) -> p k g n", p=P, g=2)),
            (w_krb[:, :, :, :], W_krb.rearrange("(k p) (g n) -> p k g n", p=P, g=2)),
            (w_q[LAT:P, 0, :, :], W_qa.rearrange("p (g n) -> p g n", g=2)),
            (w_q[LAT:P, 1, :, :], W_qb.rearrange("p (g n) -> p g n", g=2)),
            (w_vu, W_vu), (w_o[:, :, :], W_o.rearrange(kp, p=P)),
            (w_r[:, :, :], W_router.rearrange(kp, p=P)),
            (b_r[:, :], routing_bias.rearrange("(a n) -> a n", a=1)),
            (rope[:, :, :], rope_tab.rearrange("i p t -> p i t")),
        ]
        def load_weights():
            for dst, src in loads:
                sp.dma_start(dst, src).then_inc(w_loaded, 16)
            with nc.allow_non_contiguous_dma(reason="per-feature columns, once"):
                sp.dma_start(ln1[:, :], w_ln1.rearrange("(k p) -> p k", p=P)).then_inc(w_loaded, 16)
                sp.dma_start(ln2[:, :], w_ln2.rearrange("(k p) -> p k", p=P)).then_inc(w_loaded, 16)

        rows = x_tm.rearrange("(t b) d -> b t d", b=BATCH)
        rows_out = out_tm.rearrange("(t b) d -> b t d", b=BATCH)

        def at(view, b):
            b = b if isinstance(b, int) else sp.snap(b)
            return view[bass.ds(b, 1), :, :].rearrange("a (j p) d -> p (a j) d", p=P)

        def held(s, v):
            sp.wait_ge(s, v)
            sp.sem_inc(taken)

        def late(kind, i, j, b):
            if kind == "nmt":
                held(*used(F_NM, b))
                for c in range(PARTS):
                    sp.dma_start(qst[KS + c:KS + c + 1, :, :], nmT[c * NH:(c + 1) * NH, :]).then_inc(nm_stacked, 16)
        def early(kind, i, j, b, r):
            if kind == "xload":
                src = at(rows, b)
                held(xn_done, b)
                held(xs_copied, b)
                sp.dma_start(xm[:, :, :], src).then_inc(x_loaded, 16)
                if isinstance(r, int) and r < 0:
                    load_weights()
            if kind == "split":
                g = i
                held(stacked[g], 16 * NSTACK * b)
                held(hi_ready[g], b + 1)
                held(mid_ready[g], b + 1)
                held(lo_ready[g], b + 1)
                sp.dma_start(parts_dram[g, :, :, :, :, :].rearrange("h d c n t -> (h d) c n t"),
                             parts[:, :, 2 * g:2 * g + 2, :]).then_inc(parts_stored[g], 16)
                held(parts_stored[g], 16 * (b + 1))
                held(pv_done, NG * TT * b)
                for q in range(len(K_PART)):
                    for n, (dst, part) in enumerate(((kst, K_PART[q]), (qst, Q_PART[q]))):
                        sp.dma_start(dst[q * HD:(q + 1) * HD, g * 8:(g + 1) * 8, :],
                                     parts_dram[g, :, :, part, n, :].rearrange("h d t -> d h t")).then_inc(stacked[g], 16)

        def moe(kind, i, j, b):
            if kind == "wt":
                held(wbc_loaded, 16 * b)
                held(*used(F_WT, b + 1))
                for q in range(TT):
                    sp.dma_start(w_dram[:, q, :], wtT[q * NX:q * NX + ER, :]).then_inc(w_stored, 16)
                held(w_stored, 64 * (b + 1))
                held(hm_ready, 14 * b)
                sp.dma_start(wbc[:, :, :], w_dram.rearrange("e j t -> (e j t)").rearrange("(a n) -> a n", a=1)
                             .to_broadcast([P, ER * SEQ]).rearrange("p (e t) -> p e t", e=ER)).then_inc(wbc_loaded, 16)
            if kind == "final":
                dst = at(rows_out, b)
                held(ot_done, 2 * (b + 1))
                sp.dma_start(dst, xs[:, :, :]).then_inc(ot_stored, 16)

        for e in range(NX):
            for dst, src in ((wg, Wg), (wu, Wu), (wd, Wd)):
                act_loads.append((dst[:, e, :, :], src[e, :, :].rearrange("(k p) n -> p k n", p=P)))
        run(sp, late, early, moe)
        sp.wait_ge(ot_stored, 16 * BATCH)

    W_SMALL = 16 * 14

    @block.gpsimd
    def _(pool):
        def fixed(ins, n=[0]):
            ins.then_inc(const_ready, 1)
            n[0] += 1
            pool.wait_ge(const_ready, n[0])
        fixed(pool.memset(ident[:, :], 0.0))
        fixed(pool.affine_select(out=ident[:, :], in_=ident[:, :], compare_op=ALU.not_equal, fill=1.0,
                                 base=0, pattern=[[-1, P]], channel_multiplier=1))
        fixed(pool.memset(identb[:, :], 0.0))
        fixed(pool.affine_select(out=identb[:, :], in_=identb[:, :], compare_op=ALU.not_equal, fill=1.0,
                                 base=0, pattern=[[-1, P]], channel_multiplier=1))
        fixed(pool.memset(mask_q[:, :], 0.0))
        fixed(pool.affine_select(out=mask_q[:, :], in_=mask_q[:, :], compare_op=ALU.is_ge, fill=MASKED,
                                 base=0, pattern=[[-1, P]], channel_multiplier=1))
        fixed(pool.memset(mask_k[:, :], 0.0))
        fixed(pool.affine_select(out=mask_k[:, :], in_=mask_k[:, :], compare_op=ALU.is_ge, fill=MASKED,
                                 base=0, pattern=[[1, P]], channel_multiplier=-1))
        fixed(pool.memset(before[:, :, :], 0.0))
        fixed(pool.affine_select(out=before[:, :, :], in_=before[:, :, :], compare_op=ALU.is_ge, fill=1.0,
                                 base=0, pattern=[[-1, ER], [1, ER]], channel_multiplier=0))
        fixed(pool.memset(ones[:, :], 1.0))
        fixed(pool.memset(consts[:, 0, :], -0.5))
        fixed(pool.memset(consts[:, 1, :], 0.5))
        fixed(pool.memset(consts[:, 2, :], 1e-5))
        fixed(pool.memset(va[:, :, :, HD:HD + 1], 1.0))
        fixed(pool.memset(va[:, :, :, HD + 1:VA], 0.0))
        fixed(pool.memset(sel[:, :], 0.0))
        fixed(pool.affine_select(out=sel[:, :].rearrange("p (h d) -> p h d", d=VA), in_=sel[:, :].rearrange("p (h d) -> p h d", d=VA),
                                 compare_op=ALU.not_equal, fill=1.0, base=-HD, pattern=[[-VA, HG], [0, VA]], channel_multiplier=1))
        fixed(pool.memset(kst[KS:KS + PARTS, :, :], 1.0))
        fixed(pool.memset(wt[:, :, :], 0.0))

        def chain(s, K, b, n, ins):
            ins.then_inc(s, 1)
            pool.wait_ge(s, K * b + n)

        def early(kind, i, j, b, r):
            if kind == "bn":
                pool.wait_ge(stats_done, TT * (b + 1))
                tt = pool.tensor_tensor
                chain(sc_step, 7, b, 1, tt(sc1[:, 0, :], mv[:, :, 1], consts[:, 2, :], ALU.add))
                chain(sc_step, 7, b, 2, tt(sc1[:, 1, :], sc1[:, 0, :], consts[:, 0, :], ALU.pow))
                chain(sc_step, 7, b, 3, tt(sc1[:, 2, :], mv[:, :, 1], sc1[:, 1, :], ALU.mult))
                chain(sc_step, 7, b, 4, tt(sc1[:, 3, :], sc1[:, 2, :], sc1[:, 1, :], ALU.mult))
                chain(sc_step, 7, b, 5, tt(sc1[:, 4, :], sc1[:, 3, :], consts[:, 1, :], ALU.pow))
                chain(sc_step, 7, b, 6, tt(sc1[:, 5, :], sc1[:, 4, :], consts[:, 2, :], ALU.add))
            if kind == "h1":
                pool.wait_ge(rms_rec, b + 1)
                tt = pool.tensor_tensor
                tt(sc1[:, 7, :], sc1[:, 1, :], sc1[:, 6, :], ALU.mult).then_inc(sc_step, 1)

        def late(kind, i, j, b):
            if kind == "wo":
                pool.wait_ge(stats2_done, TT * (b + 1))
                tt = pool.tensor_tensor
                chain(sc2_step, 4, b, 1, tt(sc2[:, 0, :], mv2[:, :, 0], mv2[:, :, 0], ALU.mult))
                chain(sc2_step, 4, b, 2, tt(sc2[:, 1, :], sc2[:, 0, :], mv2[:, :, 1], ALU.add))
                chain(sc2_step, 4, b, 3, tt(sc2[:, 2, :], sc2[:, 1, :], consts[:, 1, :], ALU.pow))
                tt(sc2[:, 3, :], sc2[:, 2, :], consts[:, 2, :], ALU.add).then_inc(sc2_step, 1)
                pool.wait_ge(xs_copied, b + 1)
                pool.tensor_tensor(xs_next[:, :, :], x2[:, :, :], xs_next[:, :, :], ALU.add).then_inc(xs_ready, 1)

        def moe(kind, s, j, b):
            if kind == "u" and j == 1 and s >= 2:
                pool.wait_ge(wbc_loaded, 16 * (b + 1))
                pool.wait_ge(hm_raw, NS * b + s + 1)
                pool.tensor_tensor(hm[:, s % NHM, :], hm[:, s % NHM, :], wbc[:, s // 2 - 1, :], ALU.mult).then_inc(hm_ready, 1)
        run(nc.gpsimd, late, early, moe)

    @block.scalar
    def _(act):
        for dst, src in act_loads:
            act.dma_start(dst, src).then_inc(moe_w_loaded, 16)
        act.wait_ge(w_loaded, W_SMALL)

        def reader(r):
            def read(k, out, cols, func, **kw):
                act.wait_ge(*filled(k, r))
                act.activation(out, cols(bank_of(k, r)), func, **kw).then_inc(free_sem(k, r), 1)
            return read

        def early(kind, i, j, b, r):
            read = reader(r)
            if kind == "bn" and isinstance(r, int) and r < 0:
                copy_x(b)
            if kind == "T":
                for k in range(KM):
                    read(F_T + k, h1T[:, k, :], lambda bank: bank[:, :], ACT.Copy, scale=ln1[:, k:k + 1])
            if kind == "lat":
                read(F_LAT, lat[:, :], lambda bank: bank[:, :], ACT.Copy)
            if kind == "split":
                g = i
                act.wait_ge(kq_ready, 4 * b + 2 * (g + 1))
                act.wait_ge(parts_stored[g], 16 * b)
                act.activation(parts[:, 0, 2 * g:2 * g + 2, :], kq[:, 2 * g:2 * g + 2, :], ACT.Copy).then_inc(hi_ready[g], 1)
                act.wait_ge(rest_ready[g], b + 1)
                act.activation(parts[:, 1, 2 * g:2 * g + 2, :], kq_rest[:, 2 * g:2 * g + 2, :], ACT.Copy).then_inc(mid_ready[g], 1)
            if kind == "v":
                for n in range(2):
                    read(F_V + n, va[:, 2 * n:2 * n + 2, :, 0:HD],
                         lambda bank: bank[:, :].rearrange("p (j h d) -> p j h d", j=2, h=NH), ACT.Copy)

        def copy_x(b):
            act.wait_ge(x_loaded, 16 * (b + 1))
            act.activation(xs_next[:, :, :], xm[:, :, :], ACT.Copy).then_inc(xs_copied, 1)

        def late(kind, i, j, b):
            read = reader(b)
            if kind == "nmt":
                act.wait_ge(nm_stacked, 48 * b)
                read(F_NM, nmT[:, :], lambda bank: bank[0:PARTS * NH, 0:SEQ // 2].bitcast(bf16), ACT.Copy)
            if kind == "s2":
                act.wait_ge(pv_done, NG * TT * b + max(i - 1, 0))
                read(S2_FILL[i, j], probs(i, j), lambda bank: bank[:, 0:probs_width(i)], ACT.Exp)
            if kind == "oc":
                act.wait_ge(pv_done, NG * TT * b + TT * (i + 1))
                act.wait_ge(rest_ready[1], b + 1)
                act.activation(yT[:, i, :], O[i % 2][:, :], ACT.Copy).then_inc(o_copied, 1)
            if kind == "ht":
                for k in range(KM):
                    read(F_HT + k, h2T[:, k, :], lambda bank: bank[:, :], ACT.Copy, scale=ln2[:, k:k + 1])
            if kind == "route":
                read(F_RT, pe_[:, :, :], lambda bank: bank[:, 0:TT * ER].rearrange("p (j e) -> p j e", j=TT), ACT.Exp, scale=-1.0)
        def moe(kind, s, j, b):
            if kind == "xc":
                act.wait_ge(xs_ready, b + 1)
                act.wait_ge(ot_stored, 16 * b)
                act.activation(xs[:, :, :], xs_next[:, :, :], ACT.Copy).then_inc(xs_moved, 1)
                if not isinstance(b, int) or b < BATCH - 1:
                    act.wait_ge(xs_moved, b + 1)
                    copy_x(b + 1)
            if kind == "wt":
                if not isinstance(b, int) or b > 0:
                    act.wait_ge(w_stored, 64 * b)
                reader(b + 1)(F_WT, wtT[:, :], lambda bank: bank[0:TT * NX, 0:P], ACT.Copy)
            if kind == "g" and j == 1:
                act.wait_ge(g_full, NS * b + s + 1)
                act.wait_ge(sg_ready, NS * b + max(s - 1, 0))
                act.activation(th[:, s % 2, :], G[:, :], ACT.Tanh, scale=0.5).then_inc(th_ready, 1)
        run(nc.scalar, late, early, moe)

    @block.vector
    def _(dve):
        dve.wait_ge(const_ready, 20)

        def full(k, r):
            dve.wait_ge(*filled(k, r))
            return bank_of(k, r)

        def early(kind, i, j, b, r):
            if kind == "bn":
                dve.wait_ge(x_loaded, 16 * (b + 1))
                for t in range(TT):
                    dve.bn_stats(st6[:, t, :], xm[:, t, :]).then_inc(stat1, 1)
                dve.wait_ge(sc_step, 7 * b)
                dve.wait_ge(xn_done, b)
                dve.sem_inc(taken)
                for t in range(TT):
                    dve.wait_ge(stat1, TT * b + t + 1)
                    dve.sem_inc(taken)
                    dve.bn_aggr(mv[:, t, :], st6[:, t, :]).then_inc(stats_done, 1)
            if kind == "h1":
                dve.wait_ge(sc_step, 7 * b + 6)
                dve.reciprocal(sc1[:, 6, :], sc1[:, 5, :]).then_inc(rms_rec, 1)
                if not isinstance(b, int) or b > 0:
                    dve.wait_ge(*used(F_T, r - 1))
                    dve.wait_ge(*used(F_T + 1, r - 1))
                dve.wait_ge(sc_step, 7 * b + 7)
                for t in range(TT):
                    last = dve.tensor_scalar(h1[:, t, :], xm[:, t, :], mv[:, t, 0:1], sc1[:, 7, t:t + 1], ALU.subtract, ALU.mult)
                last.then_inc(h1_done, 1)
            if kind == "xn" and isinstance(r, int) and r < 0:
                dve.wait_ge(w_loaded, W_SMALL)
                dve.tensor_scalar(w_q[LAT:P, :, :, :], w_q[LAT:P, :, :, :], 1.0 / math.sqrt(HD), None, ALU.mult).then_inc(q_scaled, 1)
            if kind == "xn":
                dve.wait_ge(sc_step, 7 * b + 2)
                dve.wait_ge(h2_done, b)
                dve.wait_ge(xs_ready, b)
                for t in range(TT):
                    last = dve.tensor_scalar(xn[:, t, :], xm[:, t, :], mv[:, t, 0:1], sc1[:, 1, t:t + 1], ALU.subtract, ALU.mult)
                last.then_inc(xn_done, 1)
            if kind == "kq":
                g, n = i, j
                k = F_KQ + 4 * g + 2 * n
                dve.wait_ge(kq_ready, 4 * b + 2 * g + n)
                dve.tensor_tensor(ra, full(k, r)[:, :], rope[:, 0, :], ALU.mult).then_inc(free_sem(k, r), 1)
                dve.tensor_tensor(rb, full(k + 1, r)[:, :], rope[:, 1, :], ALU.mult).then_inc(free_sem(k + 1, r), 1)
                if n == 0:
                    dve.wait_ge(hi_ready[g], b)
                    dve.wait_ge(rest_ready[g], b)
                dve.wait_ge(*used(k, r))
                dve.wait_ge(*used(k + 1, r))
                dve.tensor_tensor(kq[:, 2 * g + n, :], ra, rb, ALU.add).then_inc(kq_ready, 1)
            if kind == "split":
                g = i
                pair = slice(2 * g, 2 * g + 2)
                dve.wait_ge(hi_ready[g], b + 1)
                dve.tensor_tensor(kq_rest[:, pair, :], kq[:, pair, :], parts[:, 0, pair, :], ALU.subtract).then_inc(rest_ready[g], 1)
                dve.wait_ge(mid_ready[g], b + 1)
                dve.wait_ge(parts_stored[g], 16 * b)
                dve.tensor_tensor(parts[:, 2, pair, :], kq_rest[:, pair, :], parts[:, 1, pair, :], ALU.subtract).then_inc(lo_ready[g], 1)

        def late(kind, i, j, b):
            def row_max(k, out, cols, last=True):
                ins = dve.tensor_reduce(out, cols(full(k, b)), AX.X, ALU.max, negate=True)
                if last:
                    ins.then_inc(free_sem(k, b), 1)
            if kind == "s1":
                h = 2 * i
                k = s1_fill(i, j)
                if i == 0 and j == 0:
                    dve.wait_ge(nm_step, 5 * b)
                if j < 2:
                    row_max(k, nm[:, 3, h + j:h + j + 1], lambda bank: bank[:, :])
                    row_max(k + 1, nm[:, 2, h + j:h + j + 1], lambda bank: bank[:, 0:384], last=False)
                    row_max(k + 1, nm[:, 0, h + j:h + j + 1], lambda bank: bank[:, 384:512])
                else:
                    row_max(k, nm[:, 1, h:h + 2], lambda bank: bank[:, :].rearrange("p (h n) -> p h n", h=2))
            if kind == "rc":
                half = slice(j * SEQ // 2, (j + 1) * SEQ // 2)
                dve.wait_ge(sums_spread, NG * b + i + 1)
                dve.reciprocal(O[i % 2][:, half], O[i % 2][:, half]).then_inc(rec_done, 1)
            if kind == "ym":
                dve.wait_ge(rec_done, 2 * (NG * b + i + 1))
                dve.tensor_tensor(yT[:, i, :], yT[:, i, :], O[i % 2][:, :], ALU.mult).then_inc(y_done, 1)
            if kind == "nm":
                dve.wait_ge(*used(F_NM - 2, b))
                dve.wait_ge(*used(F_NM - 1, b))
                dve.tensor_copy(nm_part[:, :, 0, :], nm[:, :, :]).then_inc(nm_step, 1)
                dve.wait_ge(nm_step, 5 * b + 1)
                dve.tensor_tensor(nm_rest[:, :, :], nm[:, :, :], nm_part[:, :, 0, :], ALU.subtract).then_inc(nm_step, 1)
                dve.wait_ge(nm_step, 5 * b + 2)
                dve.tensor_copy(nm_part[:, :, 1, :], nm_rest[:, :, :]).then_inc(nm_step, 1)
                dve.wait_ge(nm_step, 5 * b + 3)
                dve.tensor_tensor(nm_rest[:, :, :], nm_rest[:, :, :], nm_part[:, :, 1, :], ALU.subtract).then_inc(nm_step, 1)
                dve.wait_ge(nm_step, 5 * b + 4)
                dve.tensor_copy(nm_part[:, :, 2, :], nm_rest[:, :, :]).then_inc(nm_step, 1)
            if kind == "wo":
                for n in range(2):
                    dve.tensor_tensor(x2[:, 2 * n:2 * n + 2, :], full(F_WO + n, b)[:, :].rearrange("p (j d) -> p j d", j=2),
                                      xn[:, 2 * n:2 * n + 2, :], ALU.add).then_inc(free_sem(F_WO + n, b), 1)
                for t in range(TT):
                    dve.wait_ge(*used(F_WO + t // 2, b))
                    dve.bn_stats(st2[:, t, :], x2[:, t, :]).then_inc(stat2, 1)
                for t in range(TT):
                    dve.wait_ge(stat2, TT * b + t + 1)
                    dve.sem_inc(taken)
                    dve.bn_aggr(mv2[:, t, :], st2[:, t, :]).then_inc(stats2_done, 1)
            if kind == "h2":
                dve.wait_ge(sc2_step, 4 * (b + 1))
                dve.reciprocal(sc2[:, 4, :], sc2[:, 3, :]).then_inc(rms2_rec, 1)
                dve.wait_ge(rms2_rec, b + 1)
                for t in range(TT):
                    last = dve.tensor_scalar(h2[:, t, :], x2[:, t, :], sc2[:, 4, t:t + 1], None, ALU.mult)
                last.then_inc(h2_done, 1)

        def moe(kind, s, j, b):
            if kind == "rank":
                steps = [0]

                def step(ins):
                    ins.then_inc(rt_step, 1)
                    steps[0] += 1
                    dve.wait_ge(rt_step, RT * b + steps[0])
                dve.wait_ge(*used(F_RT, b))
                step(dve.tensor_scalar(pe_[:, :, :], pe_[:, :, :], 1.0, None, ALU.add))
                step(dve.reciprocal(prob[:, :, :], pe_[:, :, :]))
                over = prob[:, :, None, :].to_broadcast([P, TT, ER, ER])
                own = prob[:, :, :, None].to_broadcast([P, TT, ER, ER])
                step(dve.tensor_tensor(cmp1[:, :, :, :], over, own, ALU.is_gt))
                step(dve.tensor_tensor(cmp2[:, :, :, :], over, own, ALU.is_equal))
                step(dve.tensor_tensor(cmp2[:, :, :, :], cmp2[:, :, :, :], before[:, None, :, :].to_broadcast([P, TT, ER, ER]), ALU.mult))
                step(dve.tensor_tensor(cmp1[:, :, :, :], cmp1[:, :, :, :], cmp2[:, :, :, :], ALU.add))
                step(dve.tensor_reduce(rank[:, :, :], cmp1[:, :, :, :], AX.X, ALU.add))
                step(dve.scalar_tensor_tensor(wsel[:, :, :], rank[:, :, :], 2.0, prob[:, :, :], ALU.is_lt, ALU.mult))
                step(dve.tensor_reduce(wsum[:, :], wsel[:, :, :], AX.X, ALU.add))
                step(dve.reciprocal(wrec[:, :], wsum[:, :]))
                dve.tensor_tensor(wt[:, :, 0:ER], wsel[:, :, :], wrec[:, :, None].to_broadcast([P, TT, ER]), ALU.mult).then_inc(wt_ready, 1)
            if kind == "g" and j == 1:
                dve.wait_ge(th_ready, NS * b + s + 1)
                dve.wait_ge(hm_raw, NS * b + max(s - 1, 0))
                dve.scalar_tensor_tensor(sg[:, s % 2, :], th[:, s % 2, :], 1.0, G[:, :], ALU.add, ALU.mult).then_inc(sg_ready, 1)
            if kind == "u" and j == 1:
                dve.wait_ge(sg_ready, NS * b + s + 1)
                dve.wait_ge(u_full, NS * b + s + 1)
                dve.wait_ge(down_done, NS * b + max(s - NHM + 1, 0))
                dve.tensor_tensor(hm[:, s % NHM, :], sg[:, s % 2, :], U[:, :], ALU.mult).then_inc(hm_raw, 1)
            if kind == "final":
                dve.wait_ge(down_done, NS * (b + 1))
                dve.wait_ge(xs_moved, b + 1)
                for n in range(2):
                    dve.scalar_tensor_tensor(xs[:, 2 * n:2 * n + 2, :], ACC[n][:, :, :], 0.5, xs[:, 2 * n:2 * n + 2, :],
                                             ALU.mult, ALU.add).then_inc(ot_done, 1)
        run(nc.vector, late, early, moe)

    @block.tensor
    def _(pe):
        pe.wait_ge(w_loaded, W_SMALL)
        pe.wait_ge(const_ready, 20)


        def free(k, r):
            pe.wait_ge(*freed(k, r))
            return bank_of(k, r)

        def full(k, r, ins):
            ins.then_inc(a_full[place(k, r)[0]], 1)

        def transposed(first, r, src):
            for k in range(KM):
                bank = free(first + k, r)
                for t in range(TT):
                    last = pe.transpose(bank[:, t * P:(t + 1) * P], src[:, t, k * P:(k + 1) * P], ident[:, :])
                full(first + k, r, last)

        def early(kind, i, j, b, r):
            if kind == "T":
                pe.wait_ge(h1_done, b + 1)
                transposed(F_T, r, h1)
            if kind == "lat":
                bank = free(F_LAT, r)
                pe.wait_ge(*used(F_T, r))
                pe.wait_ge(*used(F_T + 1, r))
                for k in range(KM):
                    last = pe.matmul(bank[:, :], w_lat[:, k, :], h1T[:, k, :], start=(k == 0), stop=(k == KM - 1))
                full(F_LAT, r, last)
            if kind == "kq":
                if isinstance(r, int) and r < 0:
                    pe.wait_ge(q_scaled, 1)
                g, k0 = i, F_KQ + 4 * i + 2 * j
                bank = free(k0, r)
                if j == 0:
                    pe.wait_ge(*used(F_LAT, r))
                    pe.matmul(bank[:, :], w_ka[:, g, :], lat[0:LAT, :], start=True, stop=False)
                    for k in range(KM):
                        last = pe.matmul(bank[:, :], w_kra[:, k, g, :], h1T[:, k, :], start=False, stop=(k == KM - 1))
                    full(k0, r, last)
                    bank = free(k0 + 1, r)
                    for k in range(KM):
                        last = pe.matmul(bank[:, :], w_krb[:, k, g, :], h1T[:, k, :], start=(k == 0), stop=(k == KM - 1))
                    full(k0 + 1, r, last)
                else:
                    full(k0, r, pe.matmul(bank[:, :], w_q[LAT:P, 0, g, :], lat[LAT:P, :], start=True, stop=True))
                    bank = free(k0 + 1, r)
                    full(k0 + 1, r, pe.matmul(bank[:, :], w_q[LAT:P, 1, g, :], lat[LAT:P, :], start=True, stop=True))
            if kind == "v":
                for n in range(2):
                    bank = free(F_V + n, r)
                    for q in range(2):
                        t = 2 * n + q
                        last = pe.matmul(bank[:, q * DM:(q + 1) * DM], lat[0:LAT, t * P:(t + 1) * P], w_vu, start=True, stop=True)
                    full(F_V + n, r, last)

        def scores(bank, c0, h, qb):
            n = P * (qb + 1)
            pe.matmul(bank[:, c0:c0 + n], qst[0:KS, h, qb * P:(qb + 1) * P], kst[0:KS, h, 0:n], start=True, stop=False)
            return pe.matmul(bank[:, c0 + qb * P:c0 + n], identb[:, :], mask_q[:, :], start=False, stop=True)

        def scores_t(bank, c0, h, kb):
            n = SEQ - P * kb
            pe.matmul(bank[:, c0:c0 + n], kst[:, h, kb * P:(kb + 1) * P], qst[:, h, kb * P:SEQ], start=True, stop=False)
            return pe.matmul(bank[:, c0:c0 + P], identb[:, :], mask_k[:, :], start=False, stop=True)

        def values(q, b):
            g, kb = divmod(q, TT)
            n = SEQ - P * kb
            pe.wait_ge(*used(S2_FILL[q, N_S2[kb] - 1], b))
            if kb == 0:
                if g >= 2 or not isinstance(b, int) or b > 0:
                    pe.wait_ge(y_done, NG * b + g - 1)
            src = pt[:, PT_W:] if q % 2 else pt[:, 0:PT_W]
            for j in range(HG):
                last = pe.matmul(O[g % 2][j * VA:(j + 1) * VA, kb * P:SEQ], va[:, kb, g * HG + j, :], src[:, j * n:(j + 1) * n],
                                 start=(kb == 0), stop=(kb == TT - 1), tile_position=(0, j * VA))
            last.then_inc(pv_done, 1)

        def late(kind, i, j, b):
            if kind == "s1":
                h = 2 * i
                k = s1_fill(i, j)
                if j == 0 and i % 4 == 0:
                    pe.wait_ge(stacked[i // 4], 16 * NSTACK * (b + 1))
                if j < 2:
                    full(k, b, scores(free(k, b), 0, h + j, 3))
                    bank = free(k + 1, b)
                    scores(bank, 0, h + j, 2)
                    full(k + 1, b, scores(bank, 384, h + j, 0))
                else:
                    bank = free(k, b)
                    scores(bank, 0, h, 1)
                    full(k, b, scores(bank, 256, h + 1, 1))
            if kind == "nmt":
                bank = free(F_NM, b)
                pe.wait_ge(nm_step, 5 * (b + 1))
                pe.sem_inc(taken)
                for t in range(TT):
                    last = pe.transpose(bank[0:PARTS * NH, t * 64:(t + 1) * 64].bitcast(bf16),
                                        nm_part[:, t, :, :].rearrange("p c h -> p (c h)"), identb[:, :])
                full(F_NM, b, last)
            if kind == "s2":
                g, kb = divmod(i, TT)
                if i == 0 and j == 0:
                    pe.wait_ge(nm_stacked, 48 * (b + 1))
                    pe.wait_ge(*used(F_V, b - 1 if not isinstance(b, int) or b > 0 else -1))
                    pe.wait_ge(*used(F_V + 1, b - 1 if not isinstance(b, int) or b > 0 else -1))
                k = S2_FILL[i, j]
                bank = free(k, b)
                heads = HG // N_S2[kb]
                for n in range(heads):
                    last = scores_t(bank, n * (SEQ - P * kb), g * HG + j * heads + n, kb)
                full(k, b, last)
            if kind == "pv":
                values(i, b)
            if kind == "bc":
                pe.wait_ge(o_copied, NG * b + i + 1)
                pe.matmul(O[i % 2][:, :], sel[:, :], yT[:, i, :], start=True, stop=True).then_inc(sums_spread, 1)
            if kind == "wo":
                pe.wait_ge(y_done, NG * (b + 1))
                for n in range(2):
                    bank = free(F_WO + n, b)
                    for q in range(2):
                        t = 2 * n + q
                        for g in range(NG):
                            last = pe.matmul(bank[:, q * DM:(q + 1) * DM], yT[:, g, t * P:(t + 1) * P], w_o[:, g, :],
                                             start=(g == 0), stop=(g == NG - 1))
                    full(F_WO + n, b, last)
            if kind == "ht":
                pe.wait_ge(h2_done, b + 1)
                transposed(F_HT, b, h2)
            if kind == "route":
                bank = free(F_RT, b)
                pe.wait_ge(*used(F_HT, b))
                pe.wait_ge(*used(F_HT + 1, b))
                for t in range(TT):
                    cols = bank[:, t * ER:(t + 1) * ER]
                    for k in range(KM):
                        pe.matmul(cols, h2T[:, k, t * P:(t + 1) * P], w_r[:, k, :], start=(k == 0), stop=False)
                    last = pe.matmul(cols, ones[:, :], b_r[:, :], start=False, stop=True)
                full(F_RT, b, last)

        def moe(kind, s, j, b):
            if kind == "wt":
                bank = free(F_WT, b + 1)
                pe.wait_ge(wt_ready, b + 1)
                full(F_WT, b + 1, pe.transpose(bank[0:TT * NX, 0:P], wt[:, :, :].rearrange("p j e -> p (j e)"), ident[:, :]))
            e, i = s // 2, s % 2
            if kind in ("g", "u"):
                w, bank, done, free_ = (wg, G, g_full, sg_ready) if kind == "g" else (wu, U, u_full, hm_raw)
                if j == 0:
                    if s == 0 and kind == "g":
                        pe.wait_ge(moe_w_loaded, 16 * 3 * NX)
                    pe.wait_ge(free_, NS * b + s)
                last = pe.matmul(bank[:, :], w[:, e, j, i * P:(i + 1) * P], h2T[:, j, :], start=(j == 0), stop=(j == KM - 1))
                if j == KM - 1:
                    last.then_inc(done, 1)
            if kind == "d":
                if j == 0:
                    if s == 0:
                        pe.wait_ge(ot_done, 2 * b)
                    if s < 2:
                        pe.wait_ge(hm_raw, NS * b + s + 1)
                    else:
                        pe.wait_ge(hm_ready, 14 * b + s - 1)
                for q in range(2):
                    t = 2 * j + q
                    last = pe.matmul(ACC[j][:, q, :], hm[:, s % NHM, t * P:(t + 1) * P], wd[:, e, i, :],
                                     start=(s == 0 and q == 0), stop=(s == NS - 1 and q == 1), skip_group_check=True)
                if j == 1:
                    last.then_inc(down_done, 1)
        run(nc.tensor, late, early, moe)


def build_mamba(nc, ctx, x_tm, res_tm, out_tm, W_in, W_conv, b_conv, W_xproj, W_dt, b_dt, A_log, D, W_out):
    f32 = mybir.dt.float32
    ALU = mybir.AluOpType
    ACT = mybir.ActivationFunctionType

    CT = 16
    CN = CT * BATCH
    NCH = SEQ // CT
    ST = 8
    SN = ST * BATCH
    NSUB = CT // ST
    NU = 2 * NSUB
    KM = DM // P
    MI = DI // P
    TT = CN // P
    HALO = (TAPS - 1) * BATCH
    UW = 2 * NST * BATCH
    CLIP = 10.0
    DA_MIN = math.exp(-CLIP)

    def sb(name, shape, dt=f32):
        return ctx.enter_context(nc.sbuf_tensor(name, shape, dt))

    def pb(name, shape, dt=f32):
        return ctx.enter_context(nc.psum_tensor(name, shape, dt))

    def sem(name):
        return ctx.enter_context(nc.semaphore(name))

    w_in = sb("m_w_in", [P, KM, 2 * DI])
    w_xp = sb("m_w_xp", [P, MI, RANK + 2 * NST])
    w_dt = sb("m_w_dt", [RANK + 1, DI])
    w_out = sb("m_w_out", [P, MI, DM])
    w_cv = sb("m_w_cv", [P, TAPS, MI])
    b_cv = sb("m_b_cv", [1, DI])
    a_neg = sb("m_a_neg", [P, MI, NST])
    d_col = sb("m_d_col", [P, MI])
    ident = sb("m_ident", [P, P])
    cv_diag = sb("m_cv_diag", [P, TAPS * MI, P])
    d_diag = sb("m_d_diag", [P, MI, P])
    ones = sb("m_ones", [1, CN])
    mhalf = sb("m_mhalf", [P, TT])
    eps = sb("m_eps", [P, TT])

    xm = sb("m_xm", [P, TT, DM])
    st6 = sb("m_st6", [P, TT, 6])
    mv = sb("m_mv", [P, TT, 2])
    veps = sb("m_veps", [P, TT])
    rstd = sb("m_rstd", [P, TT])
    xn = sb("m_xn", [P, TT, DM])
    xnT = sb("m_xnT", [P, KM, CN])
    xpad = sb("m_xpad", [P, MI, HALO + CN])
    th_z = sb("m_th_z", [P, MI, CN])
    th_x = sb("m_th_x", [P, MI, CN])
    dt_in = sb("m_dt_in", [RANK + 1, CN])
    bc_row = sb("m_bc_row", [RANK + 2 * NST, CN])
    sp_e = sb("m_sp_e", [P, MI, CN])
    sp_u = sb("m_sp_u", [P, MI, CN])
    sp_v = sb("m_sp_v", [P, MI, CN])
    sp_r = sb("m_sp_r", [P, MI, CN])
    z_sb = sp_r
    x2 = sb("m_x2", [P, 2, MI, CN])
    zs = sb("m_zs", [P, 2, MI, CN])
    dtt = sb("m_dt", [P, 2, MI, CN])
    dtx = sb("m_dtx", [P, 2, MI, CN])
    dA = sb("m_dA", [P, 2, 2, NST, SN])
    ub = sb("m_ub", [P, 2, 2, NST, SN])
    Bb = sb("m_Bb", [P, NSUB, NST, SN])
    Cb = sb("m_Cb", [P, NSUB, NST, SN])
    yz = sb("m_yz", [P, MI, CN])
    res = sb("m_res", [P, TT, DM])
    ot = sb("m_ot", [P, TT, DM])
    bc_dram = nc.dram_tensor("m_bc_dram", [NSUB, 2, NST, SN], f32).ap()

    S = [sb(f"m_S{h}", [P, UW]) for h in range(2)]
    PR = pb("m_PR", [P, UW])
    Y = pb("m_Y", [P, 512])
    F = [pb(f"m_F{i}", [P, 2, CN]) for i in range(4)]

    w_loaded = sem("m_w_loaded")
    ident_ready = sem("m_ident_ready")
    setup_done = sem("m_setup_done")
    setup_neg = sem("m_setup_neg")
    sp_taken = sem("m_sp_taken")
    taken = sem("m_taken")
    x_loaded = sem("m_x_loaded")
    stat = sem("m_stat")
    stats_done = sem("m_stats_done")
    veps_done = sem("m_veps_done")
    rstd_done = sem("m_rstd_done")
    xn_done = sem("m_xn_done")
    xT_done = sem("m_xT_done")
    xnT_ready = sem("m_xnT_ready")
    xz_done = sem("m_xz_done")
    xpad_ready = sem("m_xpad_ready")
    halo_done = sem("m_halo_done")
    thz_ready = sem("m_thz_ready")
    z_copied = sem("m_z_copied")
    z_times = sem("m_z_times")
    zs_ready = sem("m_zs_ready")
    conv_done = sem("m_conv_done")
    thx_ready = sem("m_thx_ready")
    x2_ready = sem("m_x2_ready")
    dbc_done = sem("m_dbc_done")
    dtin_ready = sem("m_dtin_ready")
    bcrow_ready = sem("m_bcrow_ready")
    dtp_done = sem("m_dtp_done")
    sp_abs = sem("m_sp_abs")
    sp_relu = sem("m_sp_relu")
    sp_exp = sem("m_sp_exp")
    sp_one = sem("m_sp_one")
    sp_low = sem("m_sp_low")
    sp_ln = sem("m_sp_ln")
    sp_sub = sem("m_sp_sub")
    dt_ready = sem("m_dt_ready")
    dtx_ready = sem("m_dtx_ready")
    bc_stored = sem("m_bc_stored")
    b_loaded = [sem(f"m_b_loaded{s}") for s in range(NSUB)]
    c_loaded = [sem(f"m_c_loaded{s}") for s in range(NSUB)]
    dA_ready = [sem(f"m_dA_ready{u}") for u in range(NU)]
    u_ready = [sem(f"m_u_ready{u}") for u in range(NU)]
    p_step = sem("m_p_step")
    s_step = sem("m_s_step")
    sc_last = [sem(f"m_sc_last{u}") for u in range(NU)]
    sc_unit = [sem(f"m_sc_unit{u}") for u in range(NU)]
    nsum_done = [sem(f"m_nsum_done{u}") for u in range(NU)]
    yz_done = sem("m_yz_done")
    outp_done = sem("m_outp_done")
    res_loaded = sem("m_res_loaded")
    ot_done = sem("m_ot_done")
    ot_stored = sem("m_ot_stored")

    def same_half_before(u, c):
        return (u - 2, c + 1) if u >= 2 else (u + 2, c)

    def chunk_order(body, tail):
        def run(eng):
            body(0, 0, True, False)
            with eng.Fori(0, NCH // 2 - 2) as g:
                body(g * 2 + 1, 1, False, False)
                body(g * 2 + 2, 0, False, False)
            body(NCH - 3, 1, False, False)
            body(NCH - 2, 0, False, False)
            body(NCH - 1, 1, False, True)
            tail(NCH - 1, 1)
        return run

    def has(c):
        return not isinstance(c, int) or c < NCH

    block = ctx.enter_context(nc.Block())

    @block.sync
    def _(sp):
        loads = [
            (w_in[:, :, :], W_in.rearrange("(k p) n -> p k n", p=P)),
            (w_xp[:, :, :], W_xproj.rearrange("(k p) n -> p k n", p=P)),
            (w_dt[0:RANK, :], W_dt),
            (w_dt[RANK:RANK + 1, :], b_dt.rearrange("(a n) -> a n", a=1)),
            (w_out[:, :, :], W_out.rearrange("(k p) n -> p k n", p=P)),
            (a_neg[:, :, :], A_log.rearrange("(m p) n -> p m n", p=P)),
            (b_cv[:, :], b_conv.rearrange("(a n) -> a n", a=1)),
        ]
        def held(s, v):
            sp.wait_ge(s, v)
            sp.sem_inc(sp_taken)

        def row_of(c):
            return c * CN if isinstance(c, int) else sp.snap(c * CN)

        def load_x(c):
            rows = row_of(c)
            held(xn_done, TT * c)
            sp.dma_start(xm[:, :, :], x_tm[bass.ds(rows, CN), :].rearrange("(j p) d -> p j d", p=P)).then_inc(x_loaded, 16)

        def spread_bc(c):
            for s in range(NSUB):
                held(b_loaded[s], 16 * c)
                held(c_loaded[s], 16 * c)
            held(bcrow_ready, c + 1)
            for s in range(NSUB):
                for i in range(2):
                    sp.dma_start(bc_dram[s, i, :, :], bc_row[RANK + i * NST:RANK + (i + 1) * NST, s * SN:(s + 1) * SN]).then_inc(bc_stored, 16)
            held(bc_stored, 64 * (c + 1))
            for s in range(NSUB):
                held(u_ready[2 * s + 1], 2 * c)
                sp.dma_start(Bb[:, s, :, :], bc_dram[s:s + 1, 0, :, :].to_broadcast([P, NST, SN])).then_inc(b_loaded[s], 16)
                held(sc_unit[2 * s + 1], c)
                held(sc_last[2 * s + 1], 2 * c)
                sp.dma_start(Cb[:, s, :, :], bc_dram[s:s + 1, 1, :, :].to_broadcast([P, NST, SN])).then_inc(c_loaded[s], 16)

        def load_res(c):
            rows = row_of(c)
            held(ot_done, c)
            sp.dma_start(res[:, :, :], res_tm[bass.ds(rows, CN), :].rearrange("(j p) d -> p j d", p=P)).then_inc(res_loaded, 16)

        def store(c):
            rows = row_of(c)
            held(ot_done, c + 1)
            sp.dma_start(out_tm[bass.ds(rows, CN), :].rearrange("(j p) d -> p j d", p=P), ot[:, :, :]).then_inc(ot_stored, 16)

        def chunk(c, rows_ahead=True):
            if rows_ahead:
                load_x(c + 2)
            store(c - 1)
            load_res(c)
            spread_bc(c + 1)

        load_x(0)
        for dst, src in loads:
            sp.dma_start(dst, src).then_inc(w_loaded, 16)
        with nc.allow_non_contiguous_dma(reason="per-channel columns, once"):
            for k in range(TAPS):
                sp.dma_start(w_cv[:, k, :], W_conv[k, :].rearrange("(m p) -> p m", p=P)).then_inc(w_loaded, 16)
            sp.dma_start(d_col[:, :], D.rearrange("(m p) -> p m", p=P)).then_inc(w_loaded, 16)
        load_x(1)
        spread_bc(0)
        load_x(2)
        load_res(0)
        spread_bc(1)
        with sp.Fori(1, NCH - 2) as c:
            chunk(c)
        chunk(NCH - 2, rows_ahead=False)
        store(NCH - 2)
        load_res(NCH - 1)
        store(NCH - 1)
        sp.wait_ge(ot_stored, 16 * NCH)

    @block.gpsimd
    def _(pool):
        pool.memset(ident[:, :], 0.0).then_inc(ident_ready, 1)
        pool.wait_ge(ident_ready, 1)
        pool.affine_select(out=ident[:, :], in_=ident[:, :], compare_op=ALU.not_equal, fill=1.0,
                           base=0, pattern=[[-1, P]], channel_multiplier=1).then_inc(ident_ready, 1)
        pool.wait_ge(ident_ready, 2)
        pool.memset(mhalf[:, :], -0.5).then_inc(ident_ready, 1)
        pool.wait_ge(ident_ready, 3)
        pool.memset(dt_in[RANK:RANK + 1, :], 1.0).then_inc(ident_ready, 1)
        pool.wait_ge(ident_ready, 4)
        pool.memset(ones[:, :], 1.0).then_inc(ident_ready, 1)
        pool.wait_ge(ident_ready, 5)
        pool.memset(xpad[:, :, 0:HALO], 0.0).then_inc(ident_ready, 1)
        pool.wait_ge(ident_ready, 6)
        pool.memset(eps[:, :], 1e-5).then_inc(ident_ready, 1)
        pool.wait_ge(ident_ready, 7)

        def rstd_of(c):
            pool.wait_ge(stats_done, TT * (c + 1))
            pool.tensor_tensor(veps[:, :], mv[:, :, 1], eps[:, :], ALU.add).then_inc(veps_done, 1)
            pool.wait_ge(veps_done, c + 1)
            pool.wait_ge(xn_done, TT * c)
            pool.tensor_tensor(rstd[:, :], veps[:, :], mhalf[:, :], ALU.pow).then_inc(rstd_done, 1)

        def dt_sum(c, par):
            pool.wait_ge(sp_ln, c + 1)
            pool.wait_ge(sp_relu, 2 * (c + 1))
            pool.tensor_tensor(sp_u[:, :, :], sp_u[:, :, :], sp_r[:, :, :], ALU.add).then_inc(sp_sub, 1)
            pool.wait_ge(sp_sub, c + 1)
            pool.wait_ge(sp_low, c + 1)
            if not isinstance(c, int) or c >= 2:
                pool.wait_ge(dtx_ready, c - 1)
                pool.wait_ge(dA_ready[NU - 1], c - 1)
            pool.tensor_tensor(dtt[:, par, :, :], sp_u[:, :, :], sp_v[:, :, :], ALU.subtract).then_inc(dt_ready, 1)

        def dt_times_x(c, par):
            pool.wait_ge(dt_ready, c + 1)
            pool.wait_ge(x2_ready, 2 * (c + 1))
            if not isinstance(c, int) or c >= 2:
                pool.wait_ge(u_ready[NU - 1], 2 * (c - 1))
            pool.tensor_tensor(dtx[:, par, :, :], x2[:, par, :, :], dtt[:, par, :, :], ALU.mult).then_inc(dtx_ready, 1)

        def gate_z(c, par):
            pool.wait_ge(thz_ready, 2 * (c + 1))
            pool.wait_ge(z_copied, 2 * (c + 1))
            pool.tensor_tensor(th_z[:, :, :], th_z[:, :, :], z_sb[:, :, :], ALU.mult).then_inc(z_times, 1)
            pool.wait_ge(z_times, c + 1)
            if not isinstance(c, int) or c >= 2:
                pool.wait_ge(yz_done, NU * (c - 1))
            pool.tensor_tensor(zs[:, par, :, :], th_z[:, :, :], z_sb[:, :, :], ALU.add).then_inc(zs_ready, 1)

        def last_times_c(c, u):
            s, h = u // 2, u % 2
            pool.wait_ge(s_step, NU * ST * c + ST * (u + 1) + 2)
            pool.wait_ge(c_loaded[s], 16 * (c + 1))
            for i in range(2):
                pool.tensor_tensor(ub[:, h, i, :, SN - BATCH:SN],
                                   S[h][:, i * NST * BATCH:(i + 1) * NST * BATCH].rearrange("p (n b) -> p n b", n=NST),
                                   Cb[:, s, :, SN - BATCH:SN], ALU.mult).then_inc(sc_last[u], 1)

        def inputs_of(c, par, u):
            s, h = u // 2, u % 2
            pool.wait_ge(dtx_ready, c + 1)
            pool.wait_ge(b_loaded[s], 16 * (c + 1))
            pu, pc = same_half_before(u, c)
            for i in range(2):
                m = 2 * h + i
                if not isinstance(pc, int) or pc >= 1:
                    pool.wait_ge(nsum_done[pu], 2 * (pc - 1) + i + 1)
                pool.tensor_tensor(ub[:, h, i, :, :], Bb[:, s, :, :],
                                   dtx[:, par, m, None, s * SN:(s + 1) * SN].to_broadcast([P, NST, SN]),
                                   ALU.mult).then_inc(u_ready[u], 1)

        rstd_of(0)
        rstd_of(1)
        gate_z(0, 0)
        dt_sum(0, 0)
        dt_times_x(0, 0)
        inputs_of(0, 0, 0)
        inputs_of(0, 0, 1)

        def body(c, par, first, last):
            if has(c + 2):
                rstd_of(c + 2)
            if not last:
                gate_z(c + 1, 1 - par)
            last_times_c(c, 0)
            inputs_of(c, par, 2)
            last_times_c(c, 1)
            if not last:
                dt_sum(c + 1, 1 - par)
            inputs_of(c, par, 3)
            last_times_c(c, 2)
            if not last:
                dt_times_x(c + 1, 1 - par)
                inputs_of(c + 1, 1 - par, 0)
            last_times_c(c, 3)
            if not last:
                inputs_of(c + 1, 1 - par, 1)

        chunk_order(body, lambda c, par: None)(nc.gpsimd)

    @block.scalar
    def _(act):
        act.wait_ge(w_loaded, 16 * 12)
        act.activation(a_neg[:, :, :], a_neg[:, :, :], ACT.Exp).then_inc(setup_neg, 1)

        def evac_T(c):
            act.wait_ge(xT_done, c + 1)
            act.wait_ge(xz_done, 4 * c)
            act.activation(xnT[:, :, :], F[2][:, :, :], ACT.Copy).then_inc(xnT_ready, 1)

        def evac_x(c):
            act.wait_ge(conv_done, 2 * c)
            act.wait_ge(xpad_ready, 2 * c)
            act.wait_ge(ident_ready, 6)
            if not isinstance(c, int) or c > 0:
                act.activation(xpad[:, :, 0:HALO], xpad[:, :, CN:CN + HALO], ACT.Copy).then_inc(halo_done, 1)
                act.wait_ge(halo_done, c)
            for i in range(2):
                act.wait_ge(xz_done, 4 * c + i + 1)
                act.activation(xpad[:, 2 * i:2 * i + 2, HALO:HALO + CN], F[1 + i][:, :, :], ACT.Copy).then_inc(xpad_ready, 1)

        def tanh_z(c):
            for i in range(2):
                act.wait_ge(xz_done, 4 * c + 3 + i)
                act.wait_ge(zs_ready, c)
                act.activation(th_z[:, 2 * i:2 * i + 2, :], F[(3 + i) % 4][:, :, :], ACT.Tanh, scale=0.5).then_inc(thz_ready, 1)
                act.wait_ge(sp_sub, c)
                act.activation(z_sb[:, 2 * i:2 * i + 2, :], F[(3 + i) % 4][:, :, :], ACT.Copy).then_inc(z_copied, 1)

        def tanh_x(c):
            for i in range(2):
                act.wait_ge(conv_done, 2 * c + i + 1)
                act.wait_ge(x2_ready, 2 * c)
                act.activation(th_x[:, 2 * i:2 * i + 2, :], F[1 + i][:, :, :], ACT.Tanh, scale=0.5).then_inc(thx_ready, 1)

        def evac_dbc(c):
            act.wait_ge(dbc_done, c + 1)
            act.wait_ge(dtp_done, 2 * c)
            act.activation(dt_in[0:RANK, :], F[3][0:RANK, 0, :], ACT.Copy).then_inc(dtin_ready, 1)
            act.wait_ge(bc_stored, 64 * c)
            act.activation(bc_row[RANK:RANK + 2 * NST, :], F[3][RANK:RANK + 2 * NST, 0, :], ACT.Copy).then_inc(bcrow_ready, 1)

        def softplus(c):
            act.wait_ge(dt_ready, c)
            act.wait_ge(zs_ready, c + 1)
            for i in range(2):
                act.wait_ge(dtp_done, 2 * c + i + 1)
                act.activation(sp_e[:, 2 * i:2 * i + 2, :], F[i][:, :, :], ACT.Abs).then_inc(sp_abs, 1)
                act.activation(sp_r[:, 2 * i:2 * i + 2, :], F[i][:, :, :], ACT.Relu).then_inc(sp_relu, 1)
            act.wait_ge(sp_abs, 2 * (c + 1))
            act.activation(sp_e[:, :, :], sp_e[:, :, :], ACT.Exp, scale=-1.0).then_inc(sp_exp, 1)

        def ln(c):
            act.wait_ge(sp_exp, c + 1)
            act.activation(sp_u[:, :, :], sp_e[:, :, :], ACT.Ln, bias=1.0).then_inc(sp_ln, 1)

        def decays(c, par, u):
            s, h = u // 2, u % 2
            act.wait_ge(dt_ready, c + 1)
            pu, pc = same_half_before(u, c)
            if pu < u:
                act.wait_ge(s_step, NU * ST * c + ST * (pu + 1) + 2)
            elif not isinstance(c, int) or c > 0:
                act.wait_ge(s_step, NU * ST * (c - 1) + ST * (pu + 1) + 2)
            for i in range(2):
                m = 2 * h + i
                for n in range(NST):
                    last = act.activation(dA[:, h, i, n, :], dtt[:, par, m, s * SN:(s + 1) * SN], ACT.Exp,
                                          scale=a_neg[:, m, n:n + 1])
            last.then_inc(dA_ready[u], 1)

        act.wait_ge(setup_neg, 2)
        evac_T(0)
        evac_x(0)
        tanh_z(0)
        tanh_x(0)
        evac_dbc(0)
        softplus(0)
        ln(0)
        decays(0, 0, 0)
        evac_T(1)
        evac_x(1)
        tanh_z(1)
        tanh_x(1)
        decays(0, 0, 1)

        def body(c, par, first, last):
            if not last:
                evac_dbc(c + 1)
                softplus(c + 1)
            decays(c, par, 2)
            if not last:
                ln(c + 1)
                if has(c + 2):
                    evac_T(c + 2)
            decays(c, par, 3)
            if not last:
                if has(c + 2):
                    evac_x(c + 2)
                    tanh_z(c + 2)
                decays(c + 1, 1 - par, 0)
                if has(c + 2):
                    tanh_x(c + 2)
                decays(c + 1, 1 - par, 1)
        chunk_order(body, lambda c, par: None)(nc.scalar)

    @block.vector
    def _(dve):
        dve.memset(S[0][:, :], 0.0).then_inc(s_step, 1)
        dve.memset(S[1][:, :], 0.0).then_inc(s_step, 1)

        def stats(c):
            dve.wait_ge(x_loaded, 16 * (c + 1))
            for j in range(TT):
                dve.bn_stats(st6[:, j, :], xm[:, j, :]).then_inc(stat, 1)
            for j in range(TT):
                dve.wait_ge(stat, TT * c + j + 1)
                dve.wait_ge(xn_done, TT * c)
                dve.wait_ge(veps_done, c)
                dve.sem_inc(taken)
                dve.bn_aggr(mv[:, j, :], st6[:, j, :]).then_inc(stats_done, 1)

        def normalise(c):
            dve.wait_ge(rstd_done, c + 1)
            dve.wait_ge(xT_done, c)
            for j in range(TT):
                dve.tensor_scalar(xn[:, j, :], xm[:, j, :], mv[:, j, 0:1], rstd[:, j:j + 1],
                                  ALU.subtract, ALU.mult).then_inc(xn_done, 1)

        def silu_x(c, par, halves=(0, 1)):
            if not isinstance(c, int) or c >= 2:
                dve.wait_ge(nsum_done[NU - 1], 2 * (c - 1))
            for i in halves:
                dve.wait_ge(thx_ready, 2 * c + i + 1)
                dve.scalar_tensor_tensor(x2[:, par, 2 * i:2 * i + 2, :], th_x[:, 2 * i:2 * i + 2, :], 1.0,
                                         F[1 + i][:, :, :], ALU.add, ALU.mult).then_inc(x2_ready, 1)

        def log_rest(c):
            dve.wait_ge(sp_exp, c + 1)
            dve.wait_ge(dt_ready, c)
            dve.tensor_scalar(sp_v[:, :, :], sp_e[:, :, :], 1.0, 1.0, ALU.add, ALU.subtract).then_inc(sp_one, 1)
            dve.wait_ge(sp_one, c + 1)
            dve.tensor_tensor(sp_v[:, :, :], sp_v[:, :, :], sp_e[:, :, :], ALU.subtract).then_inc(sp_low, 1)

        def scan(c, u, between):
            s, h = u // 2, u % 2
            base = NU * ST * c + ST * u
            dve.wait_ge(dA_ready[u], c + 1)
            dve.wait_ge(u_ready[u], 2 * (c + 1))
            dve.wait_ge(c_loaded[s], 16 * (c + 1))
            banks = (S[h], PR)

            def times_c(t):
                cols = slice(t * BATCH, (t + 1) * BATCH)
                return dve.tensor_tensor(ub[:, h, :, :, cols],
                                         banks[(t + 1) % 2][:, :].rearrange("p (i n b) -> p i n b", i=2, n=NST),
                                         Cb[:, s, None, :, cols].to_broadcast([P, 2, NST, BATCH]), ALU.mult)
            for t in range(ST):
                cols = slice(t * BATCH, (t + 1) * BATCH)
                old = banks[t % 2][:, :].rearrange("p (a b) -> p a b", b=BATCH)
                new = banks[(t + 1) % 2][:, :].rearrange("p (a b) -> p a b", b=BATCH)
                dve.wait_ge(s_step, base + t + 2)
                step = dve.scalar_tensor_tensor(new, dA[:, h, :, :, cols].rearrange("p i n b -> p (i n) b"), DA_MIN,
                                                old, ALU.max, ALU.mult)
                step.then_inc(p_step, 1)
                if t > 0:
                    done = times_c(t - 1)
                    if t == ST - 1:
                        done.then_inc(sc_unit[u], 1)
                dve.wait_ge(p_step, base + t + 1)
                dve.sem_inc(taken)
                dve._custom_dve(bass.dve_ops.TENSOR_ADD_SAT, out=new, in0=new,
                                in1=ub[:, h, :, :, cols].rearrange("p i n b -> p (i n) b"),
                                s0=CLIP, s1=-CLIP).then_inc(s_step, 1)
                if t in between:
                    between[t]()

        def gate_y(c, par, u):
            s, h = u // 2, u % 2
            dve.wait_ge(nsum_done[u], 2 * (c + 1))
            dve.wait_ge(outp_done, c)
            dve.wait_ge(zs_ready, c + 1)
            dve.tensor_tensor(yz[:, 2 * h:2 * h + 2, s * SN:(s + 1) * SN],
                              Y[:, 0:2 * SN].rearrange("p (i q) -> p i q", i=2),
                              zs[:, par, 2 * h:2 * h + 2, s * SN:(s + 1) * SN], ALU.mult).then_inc(yz_done, 1)

        def add_res(c):
            dve.wait_ge(outp_done, c + 1)
            dve.wait_ge(res_loaded, 16 * (c + 1))
            dve.wait_ge(ot_stored, 16 * c)
            dve.tensor_tensor(ot[:, :, :], Y[:, :].rearrange("p (j d) -> p j d", j=TT), res[:, :, :], ALU.add).then_inc(ot_done, 1)

        stats(0)
        dve.wait_ge(w_loaded, 16 * 12)
        dve.wait_ge(ident_ready, 6)
        dve.wait_ge(setup_neg, 1)
        dve.tensor_scalar(a_neg[:, :, :], a_neg[:, :, :], -1.0, None, ALU.mult).then_inc(setup_neg, 1)
        dve.tensor_scalar(w_xp[:, :, :], w_xp[:, :, :], 0.5, None, ALU.mult).then_inc(setup_done, 1)
        dve.wait_ge(setup_done, 1)
        b_cols = w_xp[:, :, RANK:RANK + NST]
        dve.tensor_scalar(b_cols, b_cols, 0.5, None, ALU.mult).then_inc(setup_done, 1)
        dve.tensor_scalar(w_out[:, :, :], w_out[:, :, :], 0.5, None, ALU.mult).then_inc(setup_done, 1)
        for k in range(TAPS):
            for m in range(MI):
                dve.tensor_scalar(cv_diag[:, k * MI + m, :], ident[:, :], w_cv[:, k, m:m + 1], None, ALU.mult).then_inc(setup_done, 1)
        for m in range(MI):
            dve.tensor_scalar(d_diag[:, m, :], ident[:, :], d_col[:, m:m + 1], 0.5, ALU.mult, ALU.mult).then_inc(setup_done, 1)
        normalise(0)
        stats(1)
        normalise(1)
        silu_x(0, 0)
        log_rest(0)

        def body(c, par, first, last):
            slots = [dict() for _ in range(NU)]
            if not first:
                slots[0][7] = lambda: add_res(c - 1)
                slots[0][4] = lambda: gate_y(c - 1, 1 - par, NU - 1)
            for u in range(1, NU):
                slots[u][5] = lambda u=u: gate_y(c, par, u - 1)
            if not last:
                slots[0][5] = lambda: silu_x(c + 1, 1 - par, [0])
                slots[0][6] = lambda: silu_x(c + 1, 1 - par, [1])
                slots[1][7] = lambda: log_rest(c + 1)
            if has(c + 2):
                slots[0][3] = lambda: stats(c + 2)
                slots[1][3] = lambda: normalise(c + 2)
            for u in range(NU):
                scan(c, u, slots[u])

        def tail(c, par):
            gate_y(c, par, NU - 1)
            add_res(c)
        chunk_order(body, tail)(nc.vector)

    @block.tensor
    def _(pe):
        pe.wait_ge(w_loaded, 16 * 12)
        pe.wait_ge(setup_done, 3 + TAPS * MI + MI)
        pe.wait_ge(ident_ready, 6)

        def transposes(c):
            pe.wait_ge(xn_done, TT * (c + 1))
            pe.wait_ge(x2_ready, 2 * c)
            for k in range(KM):
                for j in range(TT):
                    last = pe.transpose(F[2][:, k, j * P:(j + 1) * P], xn[:, j, k * P:(k + 1) * P], ident[:, :])
            last.then_inc(xT_done, 1)

        def project(c):
            pe.wait_ge(xnT_ready, c + 1)
            for i in range(4):
                if i == 0:
                    pe.wait_ge(sp_abs, 2 * c)
                    pe.wait_ge(sp_relu, 2 * c)
                if i == 1:
                    pe.wait_ge(x2_ready, 2 * c)
                if i == 2:
                    pe.wait_ge(bcrow_ready, c)
                    pe.wait_ge(dtin_ready, c)
                for m in range(2):
                    blk = 2 * i + m
                    for k in range(KM):
                        last = pe.matmul(F[(1 + i) % 4][:, m, :], w_in[:, k, blk * P:(blk + 1) * P], xnT[:, k, :],
                                         start=(k == 0), stop=(k == KM - 1))
                last.then_inc(xz_done, 1)

        def conv(c):
            for i in range(2):
                pe.wait_ge(xpad_ready, 2 * (c + 1))
                for j in range(2):
                    m = 2 * i + j
                    pe.matmul(F[1 + i][:, j, :], b_cv[:, m * P:(m + 1) * P], ones[:, :], start=True, stop=False)
                    for k in range(TAPS):
                        last = pe.matmul(F[1 + i][:, j, :], cv_diag[:, k * MI + m, :],
                                         xpad[:, m, k * BATCH:k * BATCH + CN], start=False, stop=(k == TAPS - 1))
                last.then_inc(conv_done, 1)

        def dbc(c):
            pe.wait_ge(z_copied, 2 * c + 1)
            for m in range(MI):
                pe.wait_ge(x2_ready, 2 * c + m // 2 + 1)
                last = pe.matmul(F[3][0:RANK + 2 * NST, 0, :], w_xp[:, m, :], x2[:, ipar[0], m, :],
                                 start=(m == 0), stop=(m == MI - 1))
            last.then_inc(dbc_done, 1)

        ipar = [0]

        def dt_proj(c):
            pe.wait_ge(dtin_ready, c + 1)
            pe.wait_ge(z_copied, 2 * (c + 1))
            for m in range(MI):
                last = pe.matmul(F[m // 2][:, m % 2, :], w_dt[:, m * P:(m + 1) * P], dt_in[:, :], start=True, stop=True)
                if m % 2:
                    last.then_inc(dtp_done, 1)

        def nsum(c, par, u):
            s, h = u // 2, u % 2
            if u > 0:
                pe.wait_ge(yz_done, NU * c + u)
            else:
                pe.wait_ge(ot_done, c)
            for i in range(2):
                m = 2 * h + i
                pe.matmul(Y[:, i * SN:(i + 1) * SN], d_diag[:, m, :], x2[:, par, m, s * SN:(s + 1) * SN],
                          start=(i == 0), stop=False, skip_group_check=True)
            pe.wait_ge(sc_unit[u], c + 1)
            for i in range(2):
                pe.wait_ge(sc_last[u], 2 * c + i + 1)
                for n in range(NST):
                    last = pe.matmul(Y[:, i * SN:(i + 1) * SN], ident[:, :], ub[:, h, i, n, :], start=False, stop=(n == NST - 1),
                                     skip_group_check=True)
                last.then_inc(nsum_done[u], 1)

        def project_out(c):
            pe.wait_ge(yz_done, NU * (c + 1))
            for j in range(TT):
                for m in range(MI):
                    last = pe.matmul(Y[:, j * DM:(j + 1) * DM], yz[:, m, j * P:(j + 1) * P], w_out[:, m, :],
                                     start=(m == 0), stop=(m == MI - 1))
            last.then_inc(outp_done, 1)

        transposes(0)
        project(0)
        conv(0)
        dbc(0)
        dt_proj(0)
        transposes(1)
        project(1)
        conv(1)

        def body(c, par, first, last):
            ipar[0] = 1 - par
            if not first:
                nsum(c - 1, 1 - par, NU - 1)
            if not first:
                project_out(c - 1)
            if not last:
                dbc(c + 1)
                dt_proj(c + 1)
            nsum(c, par, 0)
            if has(c + 2):
                transposes(c + 2)
            nsum(c, par, 1)
            if has(c + 2):
                project(c + 2)
            nsum(c, par, 2)
            if has(c + 2):
                conv(c + 2)

        def tail(c, par):
            nsum(c, par, NU - 1)
            project_out(c)
        chunk_order(body, tail)(nc.tensor)


_MAMBA_INS = ['L0_attn_W_in', 'L0_attn_W_conv', 'L0_attn_b_conv', 'L0_attn_W_xproj', 'L0_attn_W_dt', 'L0_attn_b_dt',
        'L0_attn_A_log', 'L0_attn_D', 'L0_attn_W_out']


_FFN_INS = ['w_ln1', 'w_ln2', 'W_kvd', 'W_qd', 'W_ka', 'W_kra', 'W_krb', 'W_qa', 'W_qb', 'W_vu', 'W_o', 'Wg', 'Wu', 'Wd',
        'W_router', 'routing_bias', 'rope_tab']


def rope_tables():
    HH = 8
    inv = (np.float32(1.0) / np.float32(10000.0) ** (np.arange(0, HH, 2, dtype=np.float32) / np.float32(HH))).astype(np.float32)
    f = np.arange(SEQ, dtype=np.float32)[:, None] * inv[None, :]
    f = np.concatenate([f, f], axis=1).astype(np.float32)
    sign = np.where(np.arange(HH) < HH // 2, -1.0, 1.0).astype(np.float32)
    c = np.ones((SEQ, 16), np.float32)
    s = np.zeros((SEQ, 16), np.float32)
    c[:, HH:] = np.cos(f)
    s[:, HH:] = np.sin(f) * sign
    c, s = (np.tile(a.T, (8, 1)) for a in (c, s))
    return np.stack([c, s]).astype(np.float32)


def ffn_layouts(inputs):
    g = {k: np.asarray(v) for k, v in inputs.items()}
    a = {n: g['L0_ffn_' + n] for n in ('w_ln1', 'w_ln2', 'W_kvd', 'W_qd', 'W_vu', 'W_o', 'W_router', 'routing_bias')}

    def heads(first, second, swap):
        w = np.zeros(((first if first is not None else second).shape[0], 16, 16), np.float32)
        if first is not None:
            w[:, :, 0:8] = first.reshape(-1, 16, 8)
        if second is not None:
            s = second.reshape(-1, 16, 2, 4)
            w[:, :, 8:16] = (s[:, :, ::-1, :] if swap else s).reshape(-1, 16, 8)
        return w.reshape(-1, 256)
    a['W_ka'] = heads(g['L0_ffn_W_ku'], None, False)
    a['W_kra'] = heads(None, g['L0_ffn_W_ropek'], False)
    a['W_krb'] = heads(None, g['L0_ffn_W_ropek'], True)
    a['W_qa'] = heads(g['L0_ffn_W_qu'], g['L0_ffn_W_ropeq'], False)
    a['W_qb'] = heads(None, g['L0_ffn_W_ropeq'], True)
    w_o = np.zeros((16, 32, DM), np.float32)
    w_o[:, 0:16] = a['W_o'].reshape(16, 16, DM)
    a['W_o'] = w_o.reshape(512, DM)
    for n in ('Wg', 'Wu', 'Wd'):
        a[n] = np.concatenate([g[f'L0_ffn_{n}_s'][None], g[f'L0_ffn_{n}_r']])
    a['rope_tab'] = rope_tables()
    return {n: np.ascontiguousarray(a[n]) for n in _FFN_INS}


def build(nc, t, out):
    part = nc.dram_tensor("x_plus_ffn", (SEQ * BATCH, DM), mybir.dt.float32).ap()
    with ExitStack() as ctx:
        build_ffn(nc, ctx, t["x_tm"], part, *[t[n] for n in _FFN_INS])
    with ExitStack() as ctx:
        build_mamba(nc, ctx, t["x_tm"], part, out, *[t[n] for n in _MAMBA_INS])


def kernel(**inputs):
    import concourse.bacc as _bacc
    from concourse.bass_utils import run_bass_kernel_spmd as _run

    nc = _bacc.Bacc("TRN2", target_bir_lowering=False, num_devices=1)
    arrays = {}
    x = np.asarray(inputs['L0_attn_x'])
    arrays["x_tm"] = np.ascontiguousarray(x.transpose(1, 0, 2)).reshape(SEQ * BATCH, DM)
    for n in _MAMBA_INS:
        arrays[n] = np.ascontiguousarray(np.asarray(inputs[n]))
    arrays.update(ffn_layouts(inputs))
    t = {k: nc.dram_tensor(k, v.shape, mybir.dt.from_np(v.dtype), kind="ExternalInput").ap() for k, v in arrays.items()}
    out = nc.dram_tensor("out_tm", (SEQ * BATCH, DM), mybir.dt.float32, kind="ExternalOutput").ap()
    build(nc, t, out)
    r = _run(nc, [arrays], core_ids=[0])
    got = r.results[0]["out_tm"].reshape(SEQ, BATCH, DM)
    return np.ascontiguousarray(got.transpose(1, 0, 2))
```
